# Optimizing a Trainium2 kernel written in Bass

```python
import numpy as np
import jax
import jax.numpy as jnp

def _softmax(x, axis=-1):
    return jax.nn.softmax(x, axis=axis)

def _gelu(x):
    return jax.nn.gelu(x, approximate=True)

def _silu(x):
    return jax.nn.silu(x)

def _sigmoid(x):
    return jax.nn.sigmoid(x)

def _layernorm(x, axis=-1, eps=1e-05):
    m = jnp.mean(x, axis=axis, keepdims=True)
    v = jnp.var(x, axis=axis, keepdims=True)
    return (x - m) / jnp.sqrt(v + eps)

def _scatter_add(tgt, idx, src, axis=0):
    return tgt.at[idx].add(src)

def _segment_sum(src, seg, n):
    return jax.ops.segment_sum(src, seg, n)
kernel_name = 'mk_gnn_resnorm_d2_gnn_r32_f4468b'

def setup_inputs(seed: int=0):
    np.random.seed(seed)
    _w = jnp.asarray

    def _rec_inputs():
        import jax
        import jax.numpy as jnp
        _gk = jax.random.key(seed)
        x = -0.000202 + 1 * jax.random.normal(jax.random.fold_in(_gk, 1), (3125, 128), jnp.float32)
        src = jax.random.randint(jax.random.fold_in(_gk, 2), (100000,), 0, 3125, jnp.int32)
        dst = jnp.minimum((3125 * jax.random.uniform(jax.random.fold_in(_gk, 3), (100000,)) ** 2.0).astype(jnp.int32), 99999)
        _o = jnp.argsort(dst, stable=True)
        src = src[_o]
        dst = dst[_o]
        return (x, src, dst)
    x, src, dst = _rec_inputs()

    def _L0_gnn_setup():
        import jax, jax.numpy as jnp
        import numpy as np
        N_NODES = 50000
        N_EDGES = 25000
        IN_FEAT = 128
        UNITS = 128
        EPS = 1e-07
        LEAKY_SLOPE = 0.2
        key = jax.random.key(seed)
        k1, k2, k3, k4 = jax.random.split(key, 4)
        node_states = jax.random.normal(k1, (N_NODES, IN_FEAT), dtype=jnp.float32)
        edges = jax.random.randint(k2, (N_EDGES, 2), 0, N_NODES, dtype=jnp.int64)
        kernel = jax.random.normal(k3, (IN_FEAT, UNITS), dtype=jnp.float32) * 0.05
        kernel_attention = jax.random.normal(k4, (2 * UNITS, 1), dtype=jnp.float32) * 0.05
        return {'node_states': node_states, 'edges': edges, 'kernel': kernel, 'kernel_attention': kernel_attention}
    _L0_gnn_all = _L0_gnn_setup()
    _L0_gnn_in = {k: v for k, v in _L0_gnn_all.items() if k in ('kernel', 'kernel_attention')}
    del _L0_gnn_all

    def _L1_gnn_setup():
        import jax, jax.numpy as jnp
        import numpy as np
        N_NODES = 50000
        N_EDGES = 25000
        NODE_DIM = 128
        HIDDEN = 256

        def _glorot(key, shape):
            fan_in, fan_out = (shape[0], shape[1])
            lim = np.sqrt(6.0 / (fan_in + fan_out)).astype(np.float32)
            return jax.random.uniform(key, shape, jnp.float32, -lim, lim)
        key = jax.random.key(seed)
        ks = jax.random.split(key, 12)
        node_features = jax.random.normal(ks[0], (N_NODES, NODE_DIM), jnp.float32)
        edge_index = jax.random.randint(ks[1], (2, N_EDGES), 0, N_NODES, jnp.int64)
        return {'node_features': node_features, 'edge_index': edge_index, 'Wm1': _glorot(ks[2], (2 * NODE_DIM, HIDDEN)), 'bm1': jnp.zeros((HIDDEN,), jnp.float32), 'Wm2': _glorot(ks[3], (HIDDEN, HIDDEN)), 'bm2': jnp.zeros((HIDDEN,), jnp.float32), 'Wm3': _glorot(ks[4], (HIDDEN, NODE_DIM)), 'bm3': jnp.zeros((NODE_DIM,), jnp.float32), 'Wn1': _glorot(ks[5], (2 * NODE_DIM, HIDDEN)), 'bn1': jnp.zeros((HIDDEN,), jnp.float32), 'Wn2': _glorot(ks[6], (HIDDEN, NODE_DIM)), 'bn2': jnp.zeros((NODE_DIM,), jnp.float32)}
    _L1_gnn_all = _L1_gnn_setup()
    _L1_gnn_in = {k: v for k, v in _L1_gnn_all.items() if k in ('Wm1', 'bm1', 'Wm2', 'bm2', 'Wm3', 'bm3', 'Wn1', 'bn1', 'Wn2', 'bn2')}
    del _L1_gnn_all
    return {'x': x, 'src': src, 'dst': dst, 'L0_gnn_kernel': _L0_gnn_in['kernel'], 'L0_gnn_kernel_attention': _L0_gnn_in['kernel_attention'], 'L1_gnn_Wm1': _L1_gnn_in['Wm1'], 'L1_gnn_bm1': _L1_gnn_in['bm1'], 'L1_gnn_Wm2': _L1_gnn_in['Wm2'], 'L1_gnn_bm2': _L1_gnn_in['bm2'], 'L1_gnn_Wm3': _L1_gnn_in['Wm3'], 'L1_gnn_bm3': _L1_gnn_in['bm3'], 'L1_gnn_Wn1': _L1_gnn_in['Wn1'], 'L1_gnn_bn1': _L1_gnn_in['bn1'], 'L1_gnn_Wn2': _L1_gnn_in['Wn2'], 'L1_gnn_bn2': _L1_gnn_in['bn2']}

def reference(x, src, dst, L0_gnn_kernel, L0_gnn_kernel_attention, L1_gnn_Wm1, L1_gnn_bm1, L1_gnn_Wm2, L1_gnn_bm2, L1_gnn_Wm3, L1_gnn_bm3, L1_gnn_Wn1, L1_gnn_bn1, L1_gnn_Wn2, L1_gnn_bn2):
    import jax
    import jax.numpy as jnp

    def _L0_gnn_ref(node_states, edges, kernel, kernel_attention):
        import jax, jax.numpy as jnp
        import numpy as np
        N_NODES = 50000
        N_EDGES = 25000
        IN_FEAT = 128
        UNITS = 128
        EPS = 1e-07
        LEAKY_SLOPE = 0.2
        n_nodes = node_states.shape[0]
        units = kernel.shape[1]
        h = node_states @ kernel
        edge_states = h[edges].reshape(edges.shape[0], 2 * units)
        scores = jax.nn.leaky_relu(edge_states @ kernel_attention, negative_slope=LEAKY_SLOPE)[:, 0]
        scores_exp = jnp.exp(jnp.clip(scores, -2.0, 2.0))
        tgt = edges[:, 0]
        denom = jax.ops.segment_sum(scores_exp, tgt, num_segments=n_nodes)
        alpha = scores_exp / (denom[tgt] + EPS)
        neigh = h[edges[:, 1]]
        out = jax.ops.segment_sum(neigh * alpha[:, None], tgt, num_segments=n_nodes)
        return out

    def _L1_gnn_ref(node_features, edge_index, Wm1, bm1, Wm2, bm2, Wm3, bm3, Wn1, bn1, Wn2, bn2):
        import jax, jax.numpy as jnp
        import numpy as np
        N_NODES = 50000
        N_EDGES = 25000
        NODE_DIM = 128
        HIDDEN = 256

        def _glorot(key, shape):
            fan_in, fan_out = (shape[0], shape[1])
            lim = np.sqrt(6.0 / (fan_in + fan_out)).astype(np.float32)
            return jax.random.uniform(key, shape, jnp.float32, -lim, lim)
        num_nodes = node_features.shape[0]
        row, col = (edge_index[0], edge_index[1])
        msg_in = jnp.concatenate([node_features[row], node_features[col]], axis=-1)
        h = jax.nn.relu(msg_in @ Wm1 + bm1)
        h = jax.nn.relu(h @ Wm2 + bm2)
        messages = h @ Wm3 + bm3
        agg = jax.ops.segment_sum(messages, col, num_segments=num_nodes)
        count = jax.ops.segment_sum(jnp.ones((messages.shape[0],), messages.dtype), col, num_segments=num_nodes)
        agg = agg / jnp.clip(count, 1.0)[:, None]
        node_in = jnp.concatenate([node_features, agg], axis=-1)
        upd = jax.nn.relu(node_in @ Wn1 + bn1) @ Wn2 + bn2
        return node_features + upd
    edge_index = jnp.stack([src, dst])
    edge_index_t = jnp.stack([src, dst], axis=1)
    x = _layernorm(x + _L0_gnn_ref(x, edge_index_t, L0_gnn_kernel, L0_gnn_kernel_attention), axis=-1)
    x = _layernorm(x + _L1_gnn_ref(x, edge_index, L1_gnn_Wm1, L1_gnn_bm1, L1_gnn_Wm2, L1_gnn_bm2, L1_gnn_Wm3, L1_gnn_bm3, L1_gnn_Wn1, L1_gnn_bn1, L1_gnn_Wn2, L1_gnn_bn2), axis=-1)
    return x

_drawn_inputs = setup_inputs


def setup_inputs(seed=0):
    import zlib

    import numpy as np

    out = dict(_drawn_inputs(seed))
    spreads = {'L1_gnn_bm1': (0.0, 0.788),
     'L1_gnn_bm2': (0.0, 0.356),
     'L1_gnn_bm3': (0.0, 0.312),
     'L1_gnn_bn1': (0.0, 0.1),
     'L1_gnn_bn2': (0.0, 0.1)}
    factors = {}
    for name, (base, spread) in spreads.items():
        noise = np.random.default_rng([zlib.crc32(name.encode()), seed]).standard_normal(out[name].shape)
        drawn = base * np.exp(spread * noise) if base else spread * noise
        out[name] = jnp.asarray(drawn.astype(out[name].dtype))
    for name, factor in factors.items():
        out[name] = (out[name] * factor).astype(out[name].dtype)
    return out
```

```python
import concourse.bass as bass
from concourse import mybir
from contextlib import ExitStack

P = 128
N = 3125
D = 128
H = 256
E = 100000
NBLK, BLK = 25, 125
TILES = 784
QROWS, QTILES = 112, 7
REAL_ROWS = E // (QTILES * P)
REST = E - REAL_ROWS * QTILES * P
PAD_DST = N

WIN = 18
SBLK, SW = 7, 512
WM = WIN * SBLK
NWIN = 174
WQ = NWIN // 2
CROWS, CCOLS = NWIN * WIN, SBLK * SW
WUN = 6

GT = 4
GE = GT * P
GROUPS = TILES // GT
GW = 42
GWM = 3 * GW
GUN = 4
TURNS = GROUPS // GUN
NPAD = N + 1 + GW
STEPS = (N + GW) // GW + 1

EPS_ALPHA = 1e-07
EPS_LN = 1e-05
SLOPE = 0.2
CLIP = 2.0

fp32 = mybir.dt.float32
f32r = mybir.dt.float32r
bf16 = mybir.dt.bfloat16
i32 = mybir.dt.int32
i16 = mybir.dt.int16
ALU = mybir.AluOpType
ACT = mybir.ActivationFunctionType
AX = mybir.AxisListType


def bounded(value, low, high):
    return value.with_bounds(min_val=low, max_val=high)


class Counted:

    def __init__(self, ctx, nc, name):
        self.sem = ctx.enter_context(nc.semaphore(name))
        self.n = 0

    def inc(self, instruction, by=1):
        instruction.then_inc(self.sem, by)
        self.n += by
        return self.n


def index_tables(nc, src, dst, T, scr_tile, scr_dst, scr_win, scr_pass):
    with ExitStack() as ctx:
        def sb(name, shape, dt):
            return ctx.enter_context(nc.sbuf_tensor(name, shape, dt))
        EL = QTILES * P
        e_src = sb("e_src", [QROWS, EL], i32)
        e_dst = sb("e_dst", [QROWS, EL], i32)
        e_blk = sb("e_blk", [QROWS, EL], i32)
        e_rest = sb("e_rest", [QROWS, EL], i32)
        keys = sb("keys", [QROWS, 4, EL], fp32)
        blkf = sb("blkf", [QROWS, EL], fp32)
        dst16 = sb("dst16", [QROWS, EL], i16)
        identf = sb("identf1", [P, P], fp32)
        onesf = sb("onesf1", [P, P], fp32)
        mm = sb("mm", [QROWS, 2, QTILES], fp32)
        mmb = sb("mmb", [P, 2, TILES], fp32)
        up1 = sb("up1", [P, TILES], fp32)
        down = sb("down", [P, TILES], fp32)
        edge = sb("edge", [P, 2, 2], fp32)
        junk = sb("junk", [P, TILES], fp32)
        best = sb("best", [P, 2, 2], fp32)
        wtab = sb("wtab", [P, 2, 2], fp32)
        wtabi = sb("wtabi", [P, 2, 2], i32)
        gmm = sb("gmm", [GROUPS // 2, 2, 2, GT], fp32)
        gbt = sb("gbt", [GROUPS // 2, 2, 2], fp32)
        gspan = sb("gspan", [GROUPS // 2, 2], fp32)
        steps = sb("steps", [P, STEPS], fp32)
        gjunk = sb("gjunk", [P, STEPS], fp32)
        gpass = sb("gpass", [GROUPS // 2, 2], fp32)
        prow = sb("prow", [1, GROUPS], fp32)
        psK = [ctx.enter_context(nc.psum_tensor(f"psK{i}", [P, 512], fp32)) for i in range(QTILES)]
        iota_done = ctx.enter_context(nc.semaphore("iota_done"))
        edges_in = ctx.enter_context(nc.semaphore("edges_in"))
        padded = ctx.enter_context(nc.semaphore("padded"))
        keys_ready = ctx.enter_context(nc.semaphore("keys_ready"))
        keys_turned = ctx.enter_context(nc.semaphore("keys_turned"))
        tile_range = ctx.enter_context(nc.semaphore("tile_range"))
        range_out = ctx.enter_context(nc.semaphore("range_out"))
        range_back = ctx.enter_context(nc.semaphore("range_back"))
        dst16_ready = ctx.enter_context(nc.semaphore("dst16_ready"))
        dst16_out = ctx.enter_context(nc.semaphore("dst16_out"))
        windows_ready = ctx.enter_context(nc.semaphore("windows_ready"))
        groups_ready = ctx.enter_context(nc.semaphore("groups_ready"))
        tables_out = ctx.enter_context(nc.semaphore("tables_out"))
        tables_back = ctx.enter_context(nc.semaphore("tables_back"))
        passes_done = ctx.enter_context(nc.semaphore("passes_done"))
        step_done = Counted(ctx, nc, "step_done")
        block = ctx.enter_context(nc.Block())

        @block.gpsimd
        def _(pool):
            pool.memset(e_src[:, :], 0).then_inc(padded, 1)
            pool.memset(e_dst[:, :], PAD_DST).then_inc(padded, 1)
            pool.memset(onesf[:, :], 1.0).then_inc(iota_done, 1)
            pool.wait_ge(iota_done, 1)
            pool.affine_select(out=identf[:, :], in_=onesf[:, :], compare_op=ALU.is_equal, fill=0.0, base=0,
                               pattern=[[-1, P]], channel_multiplier=1).then_inc(iota_done, 1)
            for out, pattern, base, mult in ((up1[:, :], [[1, TILES]], 1, 0), (down[:, :], [[-1, TILES]], TILES, 0),
                                             (edge[:, :, :], [[WIN * WQ, 2], [WIN, 2]], 0, WIN),
                                             (steps[:, :], [[GW, STEPS]], 0, 0),
                                             (T.iota_m[:, :], [[1, P]], 0, 0),
                                             (T.iota_n[:, :], [[1, SW]], 0, 0),
                                             (T.iota_p[:, :], [[1, 1]], 0, 1),
                                             (T.win_key[:, :], [[WM, NWIN]], 0, 0)):
                pool.iota(out, pattern, base=base, channel_multiplier=mult,
                          allow_small_or_imprecise_dtypes=True).then_inc(iota_done, 1)

        @block.sync
        def _(sp):
            sp.wait_ge(padded, 2)
            for tile, lst in ((e_src, src), (e_dst, dst)):
                sp.dma_start(tile[0:REAL_ROWS, :], lst[0:REAL_ROWS * EL].rearrange("(q n) -> q n", n=EL)).then_inc(edges_in, 16)
                sp.dma_start(tile[REAL_ROWS:REAL_ROWS + 1, 0:REST], lst[REAL_ROWS * EL:E].rearrange("(q n) -> q n", q=1)).then_inc(edges_in, 16)
            sp.wait_ge(tile_range, 1)
            for c in range(2):
                sp.dma_start(scr_tile[c, :].rearrange("(q k) -> q k", k=QTILES), mm[:, c, :]).then_inc(range_out, 16)
            sp.wait_ge(range_out, 32)
            sp.dma_start(mmb[:, :, :], scr_tile.rearrange("c (o t) -> o c t", o=1).broadcast_to([P, 2, TILES])).then_inc(range_back, 16)
            for c in range(2):
                sp.dma_start(gmm[:, c, :, :], scr_tile[c, :].rearrange("(q r k) -> q r k", r=2, k=GT)).then_inc(range_back, 16)
            sp.wait_ge(dst16_ready, 1)
            sp.dma_start(scr_dst.rearrange("(q n) -> q n", n=EL), dst16[:, :]).then_inc(dst16_out, 16)
            sp.wait_ge(windows_ready, 1)
            with nc.allow_non_contiguous_dma(reason="a few hundred words"):
                sp.dma_start(scr_win.rearrange("(r q c) -> q r c", r=2, c=2), wtabi[0:WQ, :, :], allow_slow_non_contiguous=True).then_inc(tables_out, 16)
            sp.wait_ge(groups_ready, 1)
            sp.dma_start(scr_pass[0, :].rearrange("(q r) -> q r", r=2), gpass[:, :]).then_inc(tables_out, 16)
            sp.dma_start(scr_pass[1, :].rearrange("(q r) -> q r", r=2), gbt[:, 0, :]).then_inc(tables_out, 16)
            sp.wait_ge(tables_out, 48)
            sp.dma_start(T.win_tab[0:1, :], scr_win.rearrange("(o n) -> o n", o=1)).then_inc(tables_back, 16)
            sp.dma_start(prow[0:1, :], scr_pass[0:1, :]).then_inc(tables_back, 16)
            sp.dma_start(T.base_row[0:1, :], scr_pass[1:2, :]).then_inc(tables_back, 16)
            sp.dma_start(T.base_all[:, :], scr_pass[1:2, :].broadcast_to([P, GROUPS])).then_inc(tables_back, 16)
            sp.wait_ge(dst16_out, 16)

        @block.vector
        def _(dve):
            def step(ins):
                dve.wait_ge(step_done.sem, step_done.inc(ins))
            dve.wait_ge(edges_in, 64)
            dve.tensor_single_scalar(e_blk[:, :], e_src[:, :], 9, ALU.logical_shift_right).then_inc(keys_ready, 1)
            dve.tensor_single_scalar(e_rest[:, :], e_src[:, :], SW - 1, ALU.bitwise_and).then_inc(keys_ready, 1)
            dve.tensor_copy(keys[:, 3, :], e_dst[:, :]).then_inc(keys_ready, 1)
            dve.tensor_copy(keys[:, 2, :], e_src[:, :]).then_inc(keys_ready, 1)
            dve.wait_ge(keys_ready, 4)
            dve.tensor_copy(keys[:, 1, :], e_rest[:, :]).then_inc(keys_ready, 1)
            step(dve.tensor_copy(blkf[:, :], e_blk[:, :]))
            dve.scalar_tensor_tensor(keys[:, 0, :], keys[:, 3, :], float(SBLK), blkf[:, :], ALU.mult, ALU.add).then_inc(keys_ready, 1)
            by_tile = keys[:, 3, :].rearrange("q (k p) -> q k p", p=P)
            dve.tensor_reduce(mm[:, 0, :], by_tile, AX.X, ALU.min)
            step(dve.tensor_reduce(mm[:, 1, :], by_tile, AX.X, ALU.max))
            dve.tensor_copy(dst16[:, :], keys[:, 3, :]).then_inc(dst16_ready, 1)
            dve.sem_inc(tile_range, 1)
            for k in range(QTILES):
                dve.wait_ge(keys_turned, k + 1)
                dve.tensor_copy(T.edge_keys[:, :, 0:TILES].rearrange("p c (q k) -> p c q k", k=QTILES)[:, :, :, k],
                                psK[k][:, 0:4 * QROWS].rearrange("p (c q) -> p c q", c=4))
            step(dve.memset(T.edge_keys[:, :, TILES:TILES + 2], -1.0))
            step(dve.tensor_copy(T.src_idx[:, :], T.edge_keys[:, 2, 0:TILES]))
            dve.wait_ge(iota_done, 10)
            dve.wait_ge(range_back, 48)
            for r in range(2):
                step(dve.scalar_tensor_tensor(junk[:, :], mmb[:, 0, :], edge[:, r, 1:2], up1[:, :], ALU.is_lt, ALU.mult))
                step(dve.tensor_reduce(best[:, 1, r:r + 1], junk[:, :], AX.X, ALU.max))
                step(dve.scalar_tensor_tensor(junk[:, :], mmb[:, 1, :], edge[:, r, 0:1], down[:, :], ALU.is_ge, ALU.mult))
                step(dve.tensor_reduce(best[:, 0, r:r + 1], junk[:, :], AX.X, ALU.max))
            step(dve.tensor_scalar(wtab[:, :, 0], best[:, 0, :], -1.0, float(TILES), ALU.mult, ALU.add))
            step(dve.tensor_scalar(wtab[:, :, 0], wtab[:, :, 0], float(TILES - 1), None, ALU.min))
            step(dve.tensor_scalar(wtab[:, :, 1], wtab[:, :, 0], 1.0, None, ALU.add))
            step(dve.tensor_tensor(wtab[:, :, 1], best[:, 1, :], wtab[:, :, 1], ALU.max))
            step(dve.tensor_copy(wtabi[:, :, :], wtab[:, :, :]))
            dve.sem_inc(windows_ready, 1)
            step(dve.tensor_reduce(gbt[:, 0, :], gmm[:, 0, :, :], AX.X, ALU.min))
            step(dve.tensor_reduce(gbt[:, 1, :], gmm[:, 1, :, :], AX.X, ALU.max))
            step(dve.tensor_tensor(gspan[:, :], gbt[:, 1, :], gbt[:, 0, :], ALU.subtract))
            for r in range(2):
                step(dve.tensor_scalar(gjunk[0:GROUPS // 2, :], steps[0:GROUPS // 2, :], gspan[:, r:r + 1], 0.0, ALU.is_le, ALU.add,
                                       accum_out=gpass[:, r:r + 1]))
            dve.sem_inc(groups_ready, 1)
            dve.wait_ge(tables_back, 64)
            step(dve.tensor_copy(T.base_i[0:1, :], T.base_row[0:1, :]))
            step(dve.tensor_reduce(T.passes_f[0:1, :], prow[0:1, :], AX.X, ALU.max))
            step(dve.tensor_copy(T.passes_i[0:1, :], T.passes_f[0:1, :]))
            step(dve.tensor_tensor(T.edge_keys[:, 3, 0:TILES].rearrange("p (g k) -> p g k", k=GT),
                                   T.edge_keys[:, 3, 0:TILES].rearrange("p (g k) -> p g k", k=GT),
                                   T.base_all[:, :].rearrange("p (g o) -> p g o", o=1).broadcast_to([P, GROUPS, GT]), ALU.subtract))
            step(dve.tensor_scalar(T.neg_base[:, :], T.base_all[:, :], -1.0, None, ALU.mult))

        @block.tensor
        def _(pe):
            pe.wait_ge(iota_done, 2)
            pe.wait_ge(keys_ready, 6)
            for k in range(QTILES):
                for c in range(4):
                    last = pe.transpose(psK[k][:, c * QROWS:(c + 1) * QROWS], keys[:, c, k * P:(k + 1) * P], identf[0:QROWS, 0:QROWS])
                last.then_inc(keys_turned, 1)


def count_edges(nc, T, counts):
    with ExitStack() as ctx:
        def sb(name, shape, dt):
            return ctx.enter_context(nc.sbuf_tensor(name, shape, dt))

        def sem(name):
            return ctx.enter_context(nc.semaphore(name))
        hot_m = sb("hot_m", [P, 2, P], bf16)
        hot_n = sb("hot_n", [P, 2, SW], bf16)
        zeros = sb("zeros", [P, SW], bf16)
        stage = sb("stage", [P, 2, SW], fp32)
        psC = [ctx.enter_context(nc.psum_tensor(f"psC{i}", [P, SW], fp32)) for i in range(2)]
        zeros_ready = sem("zeros_ready")
        hot_ready = [sem(f"hot_ready{i}") for i in range(2)]
        hot_free = [sem(f"hot_free{i}") for i in range(2)]
        window_summed = sem("window_summed")
        stage_ready = sem("stage_ready")
        stage_out = [sem(f"stage_out{i}") for i in range(2)]
        sp_order = sem("sp_order_c")
        block = ctx.enter_context(nc.Block())

        @block.vector
        def _(dve):
            dve.memset(zeros[:, :], 0.0).then_inc(zeros_ready, 1)
            turn = dve.alloc_register("dve_turn")
            dve.reg_mov(turn, 1)
            regs = [dve.alloc_register(f"dve_win{i}") for i in range(2 * WUN)]
            with dve.Fori(0, NWIN, WUN) as w:
                w = bounded(w, 0, NWIN - WUN)
                dve.reg_load(regs, T.win_tab[0:1, bass.ds(w * 2, 2 * WUN)])
                for u in range(WUN):
                    first = dve.snap(regs[2 * u], min_val=0, max_val=TILES - 1)
                    end = dve.snap(regs[2 * u + 1], min_val=1, max_val=TILES)
                    key0 = T.win_key[:, bass.ds(w + u, 1)]
                    with dve.Fori(first, end, 2) as t:
                        t = bounded(t, 0, TILES)
                        now = dve.snap(turn, min_val=1, max_val=10**6)
                        for s in range(2):
                            dve.wait_ge(hot_free[s], now)
                            dve.tensor_scalar(hot_m[:, s, 0:WM], T.iota_m[:, 0:WM], key0,
                                              T.edge_keys[:, 0, bass.ds(t + s, 1)], ALU.add, ALU.is_equal)
                            dve.tensor_scalar(hot_n[:, s, :], T.iota_n[:, :], T.edge_keys[:, 1, bass.ds(t + s, 1)],
                                              None, ALU.is_equal).then_inc(hot_ready[s], 1)
                        dve.reg_add(turn, turn, 1)

        @block.tensor
        def _(pe):
            for s in range(2):
                pe.sem_inc(hot_free[s], 1)
            pe.wait_ge(zeros_ready, 1)
            turn = pe.alloc_register("pe_turn")
            pe.reg_mov(turn, 1)
            regs = [pe.alloc_register(f"pe_win{i}") for i in range(2 * WUN)]
            with pe.Fori(0, NWIN, WUN) as w:
                w = bounded(w, 0, NWIN - WUN)
                pe.reg_load(regs, T.win_tab[0:1, bass.ds(w * 2, 2 * WUN)])
                for u in range(WUN):
                    first = pe.snap(regs[2 * u], min_val=0, max_val=TILES - 1)
                    end = pe.snap(regs[2 * u + 1], min_val=1, max_val=TILES)
                    bank = psC[u % 2]
                    pe.wait_ge(stage_ready, w + u + 1)
                    pe.matmul(bank[0:WM, :], zeros[:, 0:WM], zeros[:, :], start=True, stop=True, skip_group_check=True)
                    with pe.Fori(first, end, 2):
                        now = pe.snap(turn, min_val=1, max_val=10**6)
                        for s in range(2):
                            pe.wait_ge(hot_ready[s], now)
                            pe.matmul(bank[0:WM, :], hot_m[:, s, 0:WM], hot_n[:, s, :], start=False, stop=True,
                                      skip_group_check=True).then_inc(hot_free[s], 1)
                        pe.reg_add(turn, turn, 1)
                    pe.matmul(bank[0:WM, 0:8], zeros[:, 0:WM], zeros[:, 0:8], start=False, stop=True,
                              skip_group_check=True).then_inc(window_summed, 1)

        @block.scalar
        def _(act):
            act.sem_inc(stage_ready, 2)
            with act.Fori(0, NWIN, 2) as w:
                w = bounded(w, 0, NWIN - 2)
                for s in range(2):
                    act.wait_ge(window_summed, w + s + 1)
                    act.wait_ge(stage_out[s], w * 8 + 16)
                    act.activation(stage[0:WM, s, :], psC[s][0:WM, :], ACT.Copy).then_inc(stage_ready, 1)

        @block.sync
        def _(sp):
            for s in range(2):
                sp.sem_inc(stage_out[s], 16)
            with sp.Fori(0, NWIN, 2) as w:
                w = bounded(w, 0, NWIN - 2)
                for s in range(2):
                    sp.wait_ge(stage_ready, w + s + 3)
                    sp.sem_inc(sp_order, 1)
                    sp.dma_start(counts[bass.ds((w + s) * WM, WM), :], stage[0:WM, s, :]).then_inc(stage_out[s], 16)
            for s in range(2):
                sp.wait_ge(stage_out[s], 16 + 16 * (NWIN // 2))


def layernorm(dve, step, T, rows, moments_ready, std_ready):
    for b in range(NBLK):
        last = dve.bn_stats(T.stats[:, b, :], rows[:, b, :])
    step(last)
    for b in range(NBLK):
        last = dve.bn_aggr(T.mv[:, b, :], T.stats[:, b, :])
    step(last)
    step(dve.tensor_scalar(T.den[:, :], T.mv[:, :, 1], EPS_LN, None, ALU.add))
    dve.sem_inc(moments_ready, 1)
    dve.wait_ge(std_ready, 1)
    step(dve.reciprocal(T.den[:, :], T.std[:, :]))
    for b in range(NBLK):
        last = dve.tensor_scalar(rows[:, b, :], rows[:, b, :], T.mv[:, b, 0:1], T.den[:, b:b + 1], ALU.subtract, ALU.mult)
    step(last)


JG = 5
ROUNDS = NBLK // JG
PR = 6
BANK_BLKS = 3


def attention(nc, T, x, w0, att, counts):
    with ExitStack() as ctx:
        def sb(name, shape, dt):
            return ctx.enter_context(nc.sbuf_tensor(name, shape, dt))

        def sem(name):
            return ctx.enter_context(nc.semaphore(name))
        W2 = D + 1
        xn = T.x1
        w_sb = sb("w_sb", [D, D], fp32)
        wT = sb("wT", [D, D], fp32)
        att_sb = sb("att_sb", [D, 2], fp32)
        ones = sb("ones_a", [P, P], fp32)
        wk = sb("wk", [D, D + 2], fp32)
        a1b = sb("a1b", [D, P], fp32)
        xT = sb("xT", [D, N], fp32)
        hx = sb("hx", [BLK, NBLK, D + 2], fp32)
        s1r = sb("s1r", [P, N], fp32)
        s2s = sb("s2s", [BLK, NBLK], fp32)
        cnt = sb("cnt", [BLK, 2, N], fp32)
        low = xT[0:BLK, :]
        pr = sb("pr", [BLK, PR, N], fp32)
        acc = sb("acc", [BLK, NBLK, W2], fp32)
        psT = [ctx.enter_context(nc.psum_tensor(f"psT{i}", [P, 512], fp32)) for i in range(4)]
        psO = [ctx.enter_context(nc.psum_tensor(f"psO{i}", [P, 512], fp32)) for i in range(2)]
        loaded = sem("loaded")
        set_up = Counted(ctx, nc, "set_up")
        ones_ready = sem("ones_ready")
        k_turned = sem("k_turned")
        k_copied = sem("k_copied")
        ka_done = sem("ka_done")
        wk_ready = sem("wk_ready")
        x_turned = sem("x_turned")
        x_copied = sem("x_copied")
        h_done = sem("h_done")
        h_copied = sem("h_copied")
        s1_done = sem("s1_done")
        s1_copied = sem("s1_copied")
        cnt_in = [sem(f"cnt_in{i}") for i in range(2)]
        low_ready = sem("low_ready")
        leaky_ready = sem("leaky_ready")
        clip_ready = sem("clip_ready")
        exp_ready = sem("exp_ready")
        prob_ready = sem("prob_ready")
        chunk_done = sem("chunk_done")
        chunk_added = sem("chunk_added")
        moments_ready = sem("moments_ready")
        std_ready = sem("std_ready")
        chain = Counted(ctx, nc, "chain_a")
        block = ctx.enter_context(nc.Block())
        CH = -(-NBLK // BANK_BLKS)

        def chunk(c):
            return list(range(c * BANK_BLKS, min(NBLK, (c + 1) * BANK_BLKS)))

        @block.sync
        def _(sp):
            sp.dma_start(w_sb[:, :], w0).then_inc(loaded, 16)
            sp.dma_start(att_sb[:, :], att.rearrange("(c f) o -> f (c o)", c=2), allow_slow_non_contiguous=True).then_inc(loaded, 16)
            sp.dma_start(xn[:, :, :], x.rearrange("(b n) f -> n b f", b=NBLK)).then_inc(loaded, 16)
            for j in range(NBLK):
                if j >= 2:
                    sp.wait_ge(prob_ready, j - 1)
                sp.dma_start(cnt[:, j % 2, :], counts[j * BLK:(j + 1) * BLK, 0:N]).then_inc(cnt_in[j % 2], 16)

        @block.gpsimd
        def _(pool):
            pool.memset(ones[:, :], 1.0).then_inc(ones_ready, 1)
            pool.wait_ge(ones_ready, 1)
            pool.affine_select(out=T.ident[:, :], in_=ones[:, :], compare_op=ALU.is_equal, fill=0.0, base=0,
                               pattern=[[-1, P]], channel_multiplier=1).then_inc(ones_ready, 1)
            for j in range(NBLK):
                pool.wait_ge(cnt_in[j % 2], 16 * (j // 2 + 1))
                pool.wait_ge(exp_ready, j + 1)
                pool.tensor_tensor(pr[:, j % PR, :], pr[:, j % PR, :], cnt[:, j % 2, :], ALU.mult).then_inc(prob_ready, 1)

        @block.tensor
        def _(pe):
            pe.wait_ge(loaded, 48)
            pe.wait_ge(ones_ready, 2)
            pe.transpose(psT[0][:, 0:P], w_sb[:, :], T.ident[:, :]).then_inc(k_turned, 1)
            pe.wait_ge(k_copied, 1)
            pe.matmul(psT[0][:, 256:258], wT[:, :], att_sb[:, :], start=True, stop=True).then_inc(ka_done, 1)
            for b in range(NBLK):
                if b >= 3:
                    pe.wait_ge(x_copied, b - 2)
                pe.transpose(psT[1 + b % 3][:, 0:BLK], xn[:, b, :], T.ident[0:BLK, 0:BLK]).then_inc(x_turned, 1)
            pe.wait_ge(wk_ready, 3)
            pe.wait_ge(x_copied, NBLK)
            for b in range(NBLK):
                if b >= 4:
                    pe.wait_ge(h_copied, b - 3)
                pe.matmul(psT[b % 4][0:BLK, 0:D + 2], xT[:, b * BLK:(b + 1) * BLK], wk[:, :], start=True, stop=True).then_inc(h_done, 1)
            pe.wait_ge(h_copied, NBLK)
            for c in range(7):
                n0, n1 = c * 512, min(N, (c + 1) * 512)
                if c >= 4:
                    pe.wait_ge(s1_copied, c - 3)
                pe.matmul(psT[c % 4][:, 0:n1 - n0], a1b[:, :], xT[:, n0:n1], start=True, stop=True).then_inc(s1_done, 1)
            for r in range(ROUNDS):
                pe.wait_ge(prob_ready, JG * (r + 1))
                for c in range(CH):
                    n = r * CH + c
                    if n >= 2:
                        pe.wait_ge(chunk_added, n - 1)
                    for a, b in enumerate(chunk(c)):
                        for j in range(JG):
                            last = pe.matmul(psO[n % 2][0:BLK, a * W2:(a + 1) * W2], pr[:, (r * JG + j) % PR, b * BLK:(b + 1) * BLK],
                                             hx[:, r * JG + j, 0:W2], start=(j == 0), stop=(j == JG - 1))
                    last.then_inc(chunk_done, 1)

        @block.scalar
        def _(act):
            for b in range(NBLK):
                act.wait_ge(x_turned, b + 1)
                act.activation(xT[:, b * BLK:(b + 1) * BLK], psT[1 + b % 3][:, 0:BLK], ACT.Copy).then_inc(x_copied, 1)
            for c in range(7):
                n0, n1 = c * 512, min(N, (c + 1) * 512)
                act.wait_ge(s1_done, c + 1)
                act.activation(s1r[:, n0:n1], psT[c % 4][:, 0:n1 - n0], ACT.Copy).then_inc(s1_copied, 1)
            act.wait_ge(s1_copied, 7)
            act.wait_ge(set_up.sem, 2)
            for j in range(NBLK):
                if j >= 1:
                    act.wait_ge(leaky_ready, j)
                act.activation(low, s1r[0:BLK, :], ACT.Identity, bias=s2s[:, j:j + 1], scale=SLOPE).then_inc(low_ready, 1)
                act.wait_ge(clip_ready, j + 1)
                act.activation(pr[:, j % PR, :], pr[:, j % PR, :], ACT.Exp).then_inc(exp_ready, 1)
            act.wait_ge(moments_ready, 1)
            act.activation(T.std[:, :], T.den[:, :], ACT.Sqrt).then_inc(std_ready, 1)

        @block.vector
        def _(dve):
            def step(ins):
                dve.wait_ge(chain.sem, chain.inc(ins))
            dve.wait_ge(k_turned, 1)
            dve.tensor_copy(wT[:, :], psT[0][:, 0:P]).then_inc(k_copied, 1)
            dve.tensor_copy(wk[:, 0:D], w_sb[:, :]).then_inc(wk_ready, 1)
            dve.wait_ge(ka_done, 1)
            dve.tensor_copy(wk[:, D:D + 2], psT[0][:, 256:258]).then_inc(wk_ready, 1)
            dve.wait_ge(wk_ready, 2)
            dve.wait_ge(ones_ready, 1)
            dve.tensor_scalar(a1b[:, :], ones[:, :], wk[:, D:D + 1], None, ALU.mult).then_inc(wk_ready, 1)
            for b in range(NBLK):
                dve.wait_ge(h_done, b + 1)
                dve.tensor_copy(hx[:, b, :], psT[b % 4][0:BLK, 0:D + 2]).then_inc(h_copied, 1)
            dve.wait_ge(h_copied, NBLK)
            set_up.inc(dve.tensor_scalar(s2s[:, :], hx[:, :, D + 1], SLOPE, None, ALU.mult))
            set_up.inc(dve.memset(hx[:, :, D:D + 1], 1.0))
            dve.wait_ge(s1_copied, 7)
            step(dve.memset(acc[:, :, :], 0.0))

            def add_round(r):
                for c in range(CH):
                    n = r * CH + c
                    blks = chunk(c)
                    dve.wait_ge(chunk_done, n + 1)
                    part = acc[:, blks[0]:blks[-1] + 1, :]
                    dve.tensor_tensor(part, psO[n % 2][0:BLK, 0:len(blks) * W2].rearrange("p (b w) -> p b w", w=W2),
                                      part, ALU.add).then_inc(chunk_added, 1)

            for j in range(NBLK):
                dve.wait_ge(low_ready, j + 1)
                if j >= PR and (j - PR) % JG == 0:
                    add_round((j - PR) // JG)
                dve.scalar_tensor_tensor(pr[:, j % PR, :], s1r[0:BLK, :], hx[:, j, D + 1:D + 2], low, ALU.add, ALU.max).then_inc(leaky_ready, 1)
                dve.wait_ge(leaky_ready, j + 1)
                dve.tensor_scalar(pr[:, j % PR, :], pr[:, j % PR, :], -CLIP, CLIP, ALU.max, ALU.min).then_inc(clip_ready, 1)
            add_round(ROUNDS - 1)
            dve.wait_ge(chunk_added, ROUNDS * CH)
            step(dve.tensor_scalar(T.den[:, :], acc[:, :, D], EPS_ALPHA, None, ALU.add))
            step(dve.reciprocal(T.den[:, :], T.den[:, :]))
            for b in range(NBLK):
                last = dve.scalar_tensor_tensor(xn[:, b, :], acc[:, b, 0:D], T.den[:, b:b + 1], xn[:, b, :], ALU.mult, ALU.add)
            step(last)
            layernorm(dve, step, T, xn, moments_ready, std_ready)


def node_tables(nc, T, wm1, bm1, table_a, table_b):
    with ExitStack() as ctx:
        def sb(name, shape, dt):
            return ctx.enter_context(nc.sbuf_tensor(name, shape, dt))

        def sem(name):
            return ctx.enter_context(nc.semaphore(name))
        w = sb("wm1_sb", [D, 2, H], fp32)
        b1 = sb("bm1_sb", [P, H], fp32)
        a_st = sb("a_st", [BLK, 2, H], fp32)
        rest = sb("rest", [BLK, 2, 2, H], fp32)
        b_st = sb("b_st", [BLK, 2, 3, H], bf16)
        zpad = sb("zpad", [NPAD - N, 3 * H], bf16)
        psX = [ctx.enter_context(nc.psum_tensor(f"psX{i}", [P, 512], fp32)) for i in range(2)]
        psN = [ctx.enter_context(nc.psum_tensor(f"psN{i}", [P, 2, H], fp32)) for i in range(2)]
        loaded = sem("loaded_t")
        x_turned = sem("x_turned_t")
        x_copied = sem("x_copied_t")
        ab_done = sem("ab_done")
        part_ready = sem("part_ready")
        rest_ready = sem("rest_ready")
        a_ready = sem("a_ready")
        b_ready = sem("b_ready")
        zpad_ready = sem("zpad_ready")
        a_out = [sem(f"a_out{i}") for i in range(2)]
        b_out = [sem(f"b_out{i}") for i in range(2)]
        block = ctx.enter_context(nc.Block())

        @block.sync
        def _(sp):
            sp.dma_start(w[:, :, :], wm1.rearrange("(c f) h -> f c h", c=2)).then_inc(loaded, 16)
            sp.dma_start(b1[:, :], bm1.rearrange("(o h) -> o h", o=1).broadcast_to([P, H])).then_inc(loaded, 16)
            sp.wait_ge(zpad_ready, 1)
            sp.dma_start(table_b[N:NPAD, :], zpad[:, :]).then_inc(b_out[0], 16)
            for b in range(NBLK):
                sp.wait_ge(a_ready, b + 1)
                sp.dma_start(table_a[b * BLK:(b + 1) * BLK, :], a_st[:, b % 2, :]).then_inc(a_out[b % 2], 16)
                sp.wait_ge(b_ready, b + 1)
                sp.dma_start(table_b[b * BLK:(b + 1) * BLK, :], b_st[:, b % 2, :, :]).then_inc(b_out[b % 2], 16)
            sp.wait_ge(a_out[0], 16 * 13)
            sp.wait_ge(a_out[1], 16 * 12)
            sp.wait_ge(b_out[0], 16 * 14)
            sp.wait_ge(b_out[1], 16 * 12)

        def tables(pe, b):
            pe.wait_ge(x_copied, b + 1)
            if b >= 2:
                pe.wait_ge(rest_ready, 2 * (b - 1))
                pe.wait_ge(a_ready, b - 1)
            pe.matmul(psN[b % 2][0:BLK, :, :].rearrange("p c h -> p (c h)"), T.x1T[:, b * BLK:(b + 1) * BLK],
                      w[:, :, :].rearrange("p c h -> p (c h)"), start=True, stop=True).then_inc(ab_done, 1)

        @block.tensor
        def _(pe):
            pe.wait_ge(loaded, 32)
            for b in range(NBLK):
                if b >= 2:
                    pe.wait_ge(x_copied, b - 1)
                pe.transpose(psX[b % 2][:, 0:BLK], T.x1[:, b, :], T.ident[0:BLK, 0:BLK]).then_inc(x_turned, 1)
                if b >= 1:
                    tables(pe, b - 1)
            tables(pe, NBLK - 1)

        def parts(act, b):
            s = b % 2
            act.wait_ge(a_ready, b + 1)
            if b >= 2:
                act.wait_ge(b_out[s], 16 * (b // 2) + (16 if s == 0 else 0))
            act.activation(b_st[:, s, 0, :], psN[s][0:BLK, 1, :], ACT.Copy).then_inc(part_ready, 1)
            act.wait_ge(rest_ready, 2 * b + 1)
            act.activation(b_st[:, s, 1, :], rest[:, s, 0, :], ACT.Copy).then_inc(part_ready, 1)
            act.wait_ge(rest_ready, 2 * b + 2)
            act.activation(b_st[:, s, 2, :], rest[:, s, 1, :], ACT.Copy).then_inc(b_ready, 1)

        @block.scalar
        def _(act):
            for b in range(NBLK):
                act.wait_ge(x_turned, b + 1)
                act.activation(T.x1T[:, b * BLK:(b + 1) * BLK], psX[b % 2][:, 0:BLK], ACT.Copy).then_inc(x_copied, 1)
                if b >= 1:
                    parts(act, b - 1)
            parts(act, NBLK - 1)

        @block.vector
        def _(dve):
            dve.memset(zpad[:, :], 0.0).then_inc(zpad_ready, 1)
            dve.wait_ge(loaded, 32)
            for b in range(NBLK):
                s = b % 2
                dve.wait_ge(ab_done, b + 1)
                if b >= 2:
                    dve.wait_ge(a_out[s], 16 * (b // 2))
                dve.tensor_tensor(a_st[:, s, :], psN[s][0:BLK, 0, :], b1[0:BLK, :], ALU.add).then_inc(a_ready, 1)
                dve.wait_ge(part_ready, 2 * b + 1)
                if b >= 2:
                    dve.wait_ge(b_ready, b - 1)
                dve.tensor_tensor(rest[:, s, 0, :], psN[s][0:BLK, 1, :], b_st[:, s, 0, :], ALU.subtract).then_inc(rest_ready, 1)
                dve.wait_ge(part_ready, 2 * b + 2)
                dve.wait_ge(rest_ready, 2 * b + 1)
                dve.tensor_tensor(rest[:, s, 1, :], rest[:, s, 0, :], b_st[:, s, 1, :], ALU.subtract).then_inc(rest_ready, 1)


def messages(nc, T, wm2, bm2, table_a, table_b, scr_dst):
    with ExitStack() as ctx:
        def sb(name, shape, dt):
            return ctx.enter_context(nc.sbuf_tensor(name, shape, dt))

        def sem(name):
            return ctx.enter_context(nc.semaphore(name))
        w = sb("wm2_sb", [P, 2, H], fp32)
        w_hi = sb("wm2_hi", [P, 2, H], f32r)
        w_lo = sb("wm2_lo", [P, 2, H], f32r)
        nb2 = sb("nb2", [P, 2, H], fp32)
        ones = sb("ones_m", [P, P], bf16)
        third = sb("third", [P, 1], fp32)
        third_i = sb("third_i", [P, 1], i32)
        idx = sb("idx", [P, GUN, GT], i32)
        ga = sb("ga", [P, GUN, GT, H], fp32)
        bw = sb("bw", [P, GUN, H], bf16)
        dstb = sb("dstb", [P, GUN, GE], i16)
        hot_t = sb("hot_t", [P, GUN, GE], bf16)
        hot_e = sb("hot_e", [P, GUN, GT, GW], fp32)
        hot_b = sb("hot_b", [P, GUN, GT, GW], bf16)
        h1_hi = sb("h1_hi", [P, 2, 2, GE], f32r)
        h1_lo = sb("h1_lo", [P, 2, 2, GE], f32r)
        h2 = sb("h2", [P, 2, GT, H], fp32)
        ps1 = [[ctx.enter_context(nc.psum_tensor(f"ps1_{i}{k}", [P, GE], fp32)) for k in range(2)] for i in range(2)]
        ps2 = [ctx.enter_context(nc.psum_tensor(f"ps2_{i}", [P, 2, H], fp32)) for i in range(2)]
        psA = [ctx.enter_context(nc.psum_tensor(f"psA_{i}", [P, 3, GW], fp32)) for i in range(2)]
        loaded = sem("loaded_m")
        setup_done = sem("setup_done")
        split_done = sem("split_done")
        idx_ready = sem("idx_ready")
        pool_order = sem("pool_order")
        sp_order = sem("sp_order")
        gathered = [sem(f"gathered{i}") for i in range(GUN)]
        window_in = [sem(f"window_in{i}") for i in range(GUN)]
        dst_in = [sem(f"dst_in{i}") for i in range(GUN)]
        hot_ready = sem("hot_ready_m")
        hot_b_ready = sem("hot_b_ready")
        h1_summed = sem("h1_summed")
        hi_ready = sem("hi_ready")
        lo_ready = sem("lo_ready")
        h2_summed = sem("h2_summed")
        h2_ready = sem("h2_ready")
        agg_summed = sem("agg_summed")
        agg_added = sem("agg_added")
        sweep_done = sem("sweep_done")
        tables_next = sem("tables_next")
        block = ctx.enter_context(nc.Block())
        LAST = GROUPS - GUN

        def sweeps(eng, first, body, end):
            passes = eng.value_load(T.passes_i[0:1, 0:1], min_val=1, max_val=STEPS)
            with eng.Fori(0, passes) as p:
                if first:
                    first(eng.snap(p * GROUPS, min_val=0, max_val=STEPS * GROUPS))
                with eng.Fori(0, LAST, GUN) as i:
                    i = bounded(i, 0, LAST - GUN)
                    body(eng.snap(p * GROUPS + i, min_val=0, max_val=STEPS * GROUPS), i, False)
                body(eng.snap(p * GROUPS + LAST, min_val=0, max_val=STEPS * GROUPS), LAST, True)
                end(p)

        @block.sync
        def _(sp):
            sp.dma_start(w[:, :, :], wm2.rearrange("(c f) h -> f c h", c=2)).then_inc(loaded, 16)
            for c in range(2):
                sp.dma_start(nb2[:, c, :], bm2.rearrange("(o h) -> o h", o=1).broadcast_to([P, H])).then_inc(loaded, 16)
            regs = [sp.alloc_register(f"sp_base{u}") for u in range(GUN)]

            def body(n, i, last):
                sp.reg_load(regs, T.base_i[0:1, bass.ds(i, GUN)])
                for u in range(GUN):
                    base = sp.snap(regs[u], min_val=0, max_val=N + 1)
                    sp.wait_ge(h1_summed, (n + u) * 2 + 2)
                    sp.sem_inc(sp_order, 1)
                    sp.dma_start(bw[0:GWM, u, :], table_b.rearrange("n (c h) -> (n c) h", c=3)[bass.ds(base * 3, GWM), :]).then_inc(window_in[u], 16)
                    sp.dma_start(dstb[0:GWM, u, :], scr_dst.rearrange("(o e) -> o e", o=1)[:, bass.ds((i + u) * GE, GE)].broadcast_to([GWM, GE])).then_inc(dst_in[u], 16)

            def end(p):
                sp.wait_ge(tables_next, p + 1)
                sp.sem_inc(sp_order, 1)
            sweeps(sp, None, body, end)

        @block.gpsimd
        def _(pool):
            pool.iota(third_i[:, :], [[0, 1]], base=0, channel_multiplier=1).then_inc(setup_done, 1)
            pool.memset(ones[:, :], 1.0).then_inc(setup_done, 1)

            def body(n, i, last):
                for u in range(GUN):
                    pool.wait_ge(idx_ready, n + u + 1)
                    pool.sem_inc(pool_order, 1)
                    for k in range(GT):
                        pool.indirect_dma_start(ga[:, u, k, :], None, table_a,
                                                bass.IndirectOffsetOnAxis(ap=idx[:, u, k:k + 1], axis=0)).then_inc(gathered[u], 16)

            def end(p):
                pool.wait_ge(tables_next, p + 1)
                pool.sem_inc(pool_order, 1)
            sweeps(pool, None, body, end)

        @block.tensor
        def _(pe):
            pe.sem_inc(h1_summed, 2 * GUN)
            pe.wait_ge(split_done, 3)
            pe.wait_ge(setup_done, 3)

            def hidden1(n, u):
                s = u % GUN
                pe.wait_ge(window_in[s], (n if u < GUN else n + GUN) * 4 + 16)
                pe.wait_ge(hot_ready, n + u + 1)
                pe.wait_ge(gathered[s], (n if u < GUN else n + GUN) * 16 + 64)
                pe.wait_ge(lo_ready, (n + u) * 2 + 2)
                for k in range(2):
                    bank = ps1[u % 2][k]
                    pe.matmul(bank[:, :], bw[0:GWM, s, k * P:(k + 1) * P], hot_t[0:GWM, s, :], start=True, stop=True, skip_group_check=True)
                    for t in range(GT):
                        last = pe.matmul(bank[:, t * P:(t + 1) * P], ga[:, s, t, k * P:(k + 1) * P], T.ident[:, :],
                                         is_transpose=True, start=False, stop=True, skip_group_check=True)
                    last.then_inc(h1_summed, 1)

            def hidden2(n, u):
                pe.wait_ge(hi_ready, (n + u) * 2 + 2)
                for q in range(2):
                    pe.wait_ge(h2_ready, (n + u) * 2 + q + 1)
                    tiles = (2 * q, 2 * q + 1)
                    for t in tiles:
                        for k in range(2):
                            hi = h1_hi[:, u % 2, k, t * P:(t + 1) * P]
                            pe.matmul(ps2[q][:, t % 2, :], hi, w_hi[:, k, :], start=(t % 2 == 0 and k == 0), stop=True, skip_group_check=True)
                            pe.matmul(ps2[q][:, t % 2, :], hi, w_lo[:, k, :], start=False, stop=True, skip_group_check=True)
                    if q == 0:
                        pe.wait_ge(lo_ready, (n + u) * 2 + 6)
                    for t in tiles:
                        for k in range(2):
                            last = pe.matmul(ps2[q][:, t % 2, :], h1_lo[:, u % 2, k, t * P:(t + 1) * P], w_hi[:, k, :],
                                             start=False, stop=True, skip_group_check=True)
                    last.then_inc(h2_summed, 1)

            def aggregate(n, u):
                pe.wait_ge(h2_ready, (n + u) * 2 + 4)
                pe.wait_ge(hot_b_ready, n + u + 1)
                pe.wait_ge(agg_added, n + u + 1)
                bank = psA[u % 2]
                for t in range(GT):
                    for k in range(2):
                        pe.matmul(bank[:, k, :], h2[:, u % 2, t, k * P:(k + 1) * P], hot_e[:, u, t, :],
                                  start=(t == 0 and k == 0), stop=True, skip_group_check=True)
                    last = pe.matmul(bank[:, 2, :], ones[:, :], hot_b[:, u, t, :], start=False, stop=True, skip_group_check=True)
                last.then_inc(agg_summed, 1)

            def body(n, i, last):
                for u in range(GUN):
                    hidden2(n, u)
                    if not (last and u == GUN - 1):
                        hidden1(n, u + 1)
                    aggregate(n, u)

            def end(p):
                pe.wait_ge(tables_next, p + 1)
            sweeps(pe, lambda n: hidden1(n, 0), body, end)

        @block.scalar
        def _(act):
            act.sem_inc(h2_summed, 4)

            def indices(i, u):
                act.activation(idx[:, u, :], T.src_idx[:, bass.ds((i + u) * GT, GT)], ACT.Copy).then_inc(idx_ready, 1)

            def high(n, u):
                act.wait_ge(h2_summed, (n + u) * 2 + 2)
                for k in range(2):
                    act.wait_ge(h1_summed, (n + u) * 2 + 2 * GUN + 1 + k)
                    act.activation(h1_hi[:, u % 2, k, :], ps1[u % 2][k][:, :], ACT.Relu).then_inc(hi_ready, 1)

            def counts(n, u):
                act.wait_ge(hot_ready, n + u + 1)
                act.activation(hot_b[:, u, :, :], hot_e[:, u, :, :], ACT.Copy).then_inc(hot_b_ready, 1)

            def first(n):
                for u in range(GUN):
                    act.activation(idx[:, u, :], T.src_idx[:, u * GT:(u + 1) * GT], ACT.Copy).then_inc(idx_ready, 1)

            def body(n, i, last):
                for u in range(GUN):
                    high(n, u)
                    if not last:
                        indices(i + GUN, u)
                    counts(n, u)

            def end(p):
                act.wait_ge(tables_next, p + 1)
            sweeps(act, first, body, end)

        @block.vector
        def _(dve):
            dve.memset(T.agg[:, :, :], 0.0).then_inc(setup_done, 1)
            dve.wait_ge(loaded, 48)
            dve.wait_ge(setup_done, 3)
            dve.tensor_copy(w_hi[:, :, :], w[:, :, :]).then_inc(split_done, 1)
            dve.tensor_scalar(nb2[:, :, :], nb2[:, :, :], -1.0, None, ALU.mult).then_inc(split_done, 1)
            dve.tensor_scalar(third[:, :], third_i[:, :], 21846.0, None, ALU.mult).then_inc(setup_done, 1)
            dve.wait_ge(split_done, 2)
            dve.tensor_tensor(w_lo[:, :, :], w[:, :, :], w_hi[:, :, :].bitcast(fp32), ALU.subtract).then_inc(split_done, 1)
            dve.wait_ge(setup_done, 4)
            dve.tensor_copy(third_i[:, :], third[:, :]).then_inc(setup_done, 1)
            dve.wait_ge(setup_done, 5)
            dve.tensor_single_scalar(third_i[:, :], third_i[:, :], 16, ALU.logical_shift_right).then_inc(setup_done, 1)
            dve.wait_ge(setup_done, 6)
            dve.tensor_copy(third[:, :], third_i[:, :]).then_inc(setup_done, 1)
            dve.wait_ge(setup_done, 7)
            dve.sem_inc(lo_ready, 4)
            dve.sem_inc(h2_ready, 2)
            dve.sem_inc(agg_added, 2)
            regs = [dve.alloc_register(f"dve_base{u}") for u in range(GUN)]

            def one_hots(n, i, u):
                s = u % GUN
                dve.wait_ge(dst_in[s], (n if u < GUN else n + GUN) * 4 + 16)
                dve.tensor_scalar(hot_t[0:GWM, s, :], dstb[0:GWM, s, :], T.neg_base[0:GWM, bass.ds(i + u, 1)],
                                  third[0:GWM, 0:1], ALU.add, ALU.is_equal)
                dve.tensor_tensor(hot_e[:, s, :, :], T.iota_n[:, 0:GW].rearrange("p (o w) -> p o w", o=1).broadcast_to([P, GT, GW]),
                                  T.edge_keys[:, 3, bass.ds((i + u) * GT, GT)].rearrange("p (t o) -> p t o", o=1).broadcast_to([P, GT, GW]),
                                  ALU.is_equal).then_inc(hot_ready, 1)

            def low(n, u):
                for k in range(2):
                    dve.wait_ge(hi_ready, (n + u) * 2 + 1 + k)
                    dve.scalar_tensor_tensor(h1_lo[:, u % 2, k, :], ps1[u % 2][k][:, :], 0.0, h1_hi[:, u % 2, k, :].bitcast(fp32),
                                             ALU.max, ALU.subtract).then_inc(lo_ready, 1)

            def first(n):
                one_hots(n, 0, 0)
                one_hots(n, 0, 1)
                low(n, 0)

            def body(n, i, last):
                dve.reg_load(regs, T.base_i[0:1, bass.ds(i, GUN)])
                for u in range(GUN):
                    if not (last and u >= GUN - 2):
                        one_hots(n, i, u + 2)
                    for q in range(2):
                        dve.wait_ge(h2_summed, (n + u) * 2 + q + 5)
                        dve.tensor_tensor(h2[:, u % 2, 2 * q:2 * q + 2, :], ps2[q][:, :, :], nb2[:, :, :], ALU.max).then_inc(h2_ready, 1)
                    if not (last and u == GUN - 1):
                        low(n, u + 1)
                    dve.wait_ge(agg_summed, n + u + 1)
                    dve.wait_ge(agg_added, n + u + 2)
                    at = T.agg[:, :, bass.ds(dve.snap(regs[u], min_val=0, max_val=N + 1), GW)]
                    dve.tensor_tensor(at, psA[u % 2][:, :, :], at, ALU.add).then_inc(agg_added, 1)

            def end(p):
                dve.wait_ge(agg_added, (p + 1) * GROUPS + 2)
                dve.tensor_scalar(T.edge_keys[:, 3, 0:TILES], T.edge_keys[:, 3, 0:TILES], -float(GW), None, ALU.add).then_inc(sweep_done, 1)
                dve.tensor_scalar(T.neg_base[:, :], T.neg_base[:, :], -float(GW), None, ALU.add).then_inc(sweep_done, 1)
                dve.tensor_scalar(T.base_row[:, :], T.base_row[:, :], float(GW), float(N + 1), ALU.add, ALU.min).then_inc(sweep_done, 1)
                dve.wait_ge(sweep_done, p * 4 + 3)
                dve.tensor_copy(T.base_i[:, :], T.base_row[:, :]).then_inc(sweep_done, 1)
                dve.wait_ge(sweep_done, p * 4 + 4)
                dve.sem_inc(tables_next, 1)
            sweeps(dve, first, body, end)


def update_nodes(nc, T, bm2, wm3, bm3, wn1, bn1, wn2, bn2, out):
    with ExitStack() as ctx:
        def sb(name, shape, dt):
            return ctx.enter_context(nc.sbuf_tensor(name, shape, dt))

        def sem(name):
            return ctx.enter_context(nc.semaphore(name))
        b2 = sb("b2_u", [P, 2], fp32)
        w3 = sb("w3_u", [P, 2, D], fp32)
        b3 = sb("b3_u", [D, 1], fp32)
        wa = sb("wa_u", [P, 2, H], fp32)
        ba = sb("ba_u", [P, 2], fp32)
        wb = sb("wb_u", [P, 2, D], fp32)
        bb = sb("bb_u", [P, D], fp32)
        inv = sb("inv", [P, N], fp32)
        has = sb("has", [P, N], fp32)
        msg = sb("msg", [D, N], fp32)
        u1 = sb("u1", [P, 2, N], fp32)
        psM = [ctx.enter_context(nc.psum_tensor(f"psM{i}", [P, 512], fp32)) for i in range(2)]
        psU = [ctx.enter_context(nc.psum_tensor(f"psU{i}", [P, 512], fp32)) for i in range(4)]
        psV = [ctx.enter_context(nc.psum_tensor(f"psV{i}", [P, 512], fp32)) for i in range(2)]
        loaded = sem("loaded_u")
        mean_ready = sem("mean_ready")
        msg_done = sem("msg_done")
        msg_ready = sem("msg_ready")
        u1_done = sem("u1_done")
        u1_ready = sem("u1_ready")
        u2_done = sem("u2_done")
        u2_read = sem("u2_read")
        moments_ready = sem("moments_u")
        std_ready = sem("std_u")
        rows_ready = sem("rows_ready")
        out_done = sem("out_done")
        chain = Counted(ctx, nc, "chain_u")
        block = ctx.enter_context(nc.Block())
        cuts = [(a, min(N, a + 512)) for a in range(0, N, 512)]

        @block.sync
        def _(sp):
            with nc.allow_non_contiguous_dma(reason="biases to partitions"):
                sp.dma_start(b2[:, :], bm2.rearrange("(c f) -> f c", c=2), allow_slow_non_contiguous=True).then_inc(loaded, 16)
                sp.dma_start(b3[:, :], bm3.rearrange("(f o) -> f o", o=1), allow_slow_non_contiguous=True).then_inc(loaded, 16)
                sp.dma_start(ba[:, :], bn1.rearrange("(c f) -> f c", c=2), allow_slow_non_contiguous=True).then_inc(loaded, 16)
            sp.dma_start(w3[:, :, :], wm3.rearrange("(c f) h -> f c h", c=2)).then_inc(loaded, 16)
            sp.dma_start(wa[:, :, :], wn1.rearrange("(c f) h -> f c h", c=2)).then_inc(loaded, 16)
            sp.dma_start(wb[:, :, :], wn2.rearrange("(c f) h -> f c h", c=2)).then_inc(loaded, 16)
            sp.dma_start(bb[:, :], bn2.rearrange("(o h) -> o h", o=1).broadcast_to([P, D])).then_inc(loaded, 16)
            sp.wait_ge(rows_ready, 1)
            sp.dma_start(out.rearrange("(b n) f -> n b f", b=NBLK), T.x1[:, :, :]).then_inc(out_done, 16)
            sp.wait_ge(out_done, 16)

        @block.tensor
        def _(pe):
            pe.wait_ge(loaded, 112)
            pe.wait_ge(mean_ready, 1)
            for c, (a, z) in enumerate(cuts):
                if c >= 2:
                    pe.wait_ge(msg_ready, c - 1)
                for k in range(2):
                    last = pe.matmul(psM[c % 2][:, 0:z - a], w3[:, k, :], T.agg[:, k, a:z], start=(k == 0), stop=(k == 1))
                last.then_inc(msg_done, 1)
            for c, (a, z) in enumerate(cuts):
                pe.wait_ge(msg_ready, c + 1)
                for m in range(2):
                    n = 2 * c + m
                    if n >= 4:
                        pe.wait_ge(u1_ready, n - 3)
                    pe.matmul(psU[n % 4][:, 0:z - a], wa[:, 0, m * P:(m + 1) * P], T.x1T[:, a:z], start=True, stop=False)
                    pe.matmul(psU[n % 4][:, 0:z - a], wa[:, 1, m * P:(m + 1) * P], msg[:, a:z], start=False, stop=True).then_inc(u1_done, 1)
            pe.wait_ge(u1_ready, 2 * len(cuts))
            for b in range(NBLK):
                if b >= 2:
                    pe.wait_ge(u2_read, b - 1)
                for k in range(2):
                    last = pe.matmul(psV[b % 2][0:BLK, 0:D], u1[:, k, b * BLK:(b + 1) * BLK], wb[:, k, :], start=(k == 0), stop=(k == 1))
                last.then_inc(u2_done, 1)

        @block.scalar
        def _(act):
            act.wait_ge(loaded, 112)
            for c, (a, z) in enumerate(cuts):
                for m in range(2):
                    n = 2 * c + m
                    act.wait_ge(u1_done, n + 1)
                    act.activation(u1[:, m, a:z], psU[n % 4][:, 0:z - a], ACT.Relu, bias=ba[:, m:m + 1]).then_inc(u1_ready, 1)
            act.wait_ge(moments_ready, 1)
            act.activation(T.std[:, :], T.den[:, :], ACT.Sqrt).then_inc(std_ready, 1)

        @block.vector
        def _(dve):
            def step(ins):
                dve.wait_ge(chain.sem, chain.inc(ins))
            dve.tensor_scalar(has[:, :], T.agg[:, 2, 0:N], 1.0, None, ALU.min)
            step(dve.tensor_scalar(inv[:, :], T.agg[:, 2, 0:N], 1.0, None, ALU.max))
            step(dve.reciprocal(inv[:, :], inv[:, :]))
            dve.wait_ge(loaded, 112)
            for k in range(2):
                step(dve.tensor_tensor(T.agg[:, k, 0:N], T.agg[:, k, 0:N], inv[:, :], ALU.mult))
                step(dve.scalar_tensor_tensor(T.agg[:, k, 0:N], has[:, :], b2[:, k:k + 1], T.agg[:, k, 0:N], ALU.mult, ALU.add))
            dve.sem_inc(mean_ready, 1)
            for c, (a, z) in enumerate(cuts):
                dve.wait_ge(msg_done, c + 1)
                dve.scalar_tensor_tensor(msg[:, a:z], has[:, a:z], b3[:, 0:1], psM[c % 2][:, 0:z - a], ALU.mult, ALU.add).then_inc(msg_ready, 1)
            step(dve.tensor_scalar(T.x1[:, :, :], T.x1[:, :, :], 2.0, None, ALU.mult))
            step(dve.tensor_tensor(T.x1[:, :, :], T.x1[:, :, :],
                                   bb[0:BLK, :].rearrange("p (o f) -> p o f", o=1).broadcast_to([BLK, NBLK, D]), ALU.add))
            for b in range(NBLK):
                dve.wait_ge(u2_done, b + 1)
                dve.tensor_tensor(T.x1[:, b, :], T.x1[:, b, :], psV[b % 2][0:BLK, 0:D], ALU.add).then_inc(u2_read, 1)
            dve.wait_ge(u2_read, NBLK)
            layernorm(dve, step, T, T.x1, moments_ready, std_ready)
            dve.sem_inc(rows_ready, 1)


class Tables:
    pass


def gnn_kernel(nc, x, src, dst, w0, att, wm1, bm1, wm2, bm2, wm3, bm3, wn1, bn1, wn2, bn2, out):
    def dram(name, shape, dt):
        return nc.dram_tensor(name, shape, dt, kind="Internal").ap()
    scr_tile = dram("scr_tile", (2, TILES), fp32)
    scr_dst = dram("scr_dst", (TILES * P,), i16)
    scr_win = dram("scr_win", (2 * NWIN,), i32)
    scr_pass = dram("scr_pass", (2, GROUPS), fp32)
    counts = dram("counts", (CROWS * SBLK, SW), fp32)
    table_a = dram("table_a", (N, H), fp32)
    table_b = dram("table_b", (NPAD, 3 * H), bf16)
    with ExitStack() as ctx:
        def sb(name, shape, dt):
            return ctx.enter_context(nc.sbuf_tensor(name, shape, dt))
        T = Tables()
        T.edge_keys = sb("edge_keys", [P, 4, TILES + 2], fp32)
        T.src_idx = sb("src_idx", [P, TILES], i32)
        T.iota_m = sb("iota_m", [P, P], i16)
        T.iota_n = sb("iota_n", [P, SW], i16)
        T.win_key = sb("win_key", [P, NWIN], fp32)
        T.iota_p = sb("iota_p", [P, 1], fp32)
        T.win_tab = sb("win_tab", [1, 2 * NWIN], i32)
        T.base_row = sb("base_row", [1, GROUPS], fp32)
        T.base_i = sb("base_i", [1, GROUPS], i32)
        T.base_all = sb("base_all", [P, GROUPS], fp32)
        T.neg_base = sb("neg_base", [P, GROUPS], fp32)
        T.passes_f = sb("passes_f", [1, 1], fp32)
        T.passes_i = sb("passes_i", [1, 1], i32)
        T.ident = sb("ident", [P, P], fp32)
        T.x1 = sb("x1", [BLK, NBLK, D], fp32)
        T.den = sb("den", [BLK, NBLK], fp32)
        T.std = sb("std", [BLK, NBLK], fp32)
        T.stats = sb("stats", [BLK, NBLK, 6], fp32)
        T.mv = sb("mv", [BLK, NBLK, 2], fp32)
        index_tables(nc, src, dst, T, scr_tile, scr_dst, scr_win, scr_pass)
        count_edges(nc, T, counts)
        attention(nc, T, x, w0, att, counts.rearrange("(r s) n -> r (s n)", s=SBLK))
        T.x1T = sb("x1T", [D, N], fp32)
        T.agg = sb("agg", [P, 3, NPAD], fp32)
        node_tables(nc, T, wm1, bm1, table_a, table_b)
        messages(nc, T, wm2, bm2, table_a, table_b, scr_dst)
        update_nodes(nc, T, bm2, wm3, bm3, wn1, bn1, wn2, bn2, out)


_INS = ["x", "src", "dst", "L0_gnn_kernel", "L0_gnn_kernel_attention", "L1_gnn_Wm1", "L1_gnn_bm1", "L1_gnn_Wm2",
        "L1_gnn_bm2", "L1_gnn_Wm3", "L1_gnn_bm3", "L1_gnn_Wn1", "L1_gnn_bn1", "L1_gnn_Wn2", "L1_gnn_bn2"]


def kernel(**inputs):
    import numpy as np
    import concourse.bacc as bacc
    from concourse import mybir as mb
    from concourse.bass_utils import run_bass_kernel_spmd as run

    nc = bacc.Bacc("TRN2", target_bir_lowering=False, num_devices=1)
    arrays, args = {}, []
    for name in _INS:
        a = np.ascontiguousarray(inputs[name])
        arrays[f"in_{name}"] = a
        args.append(nc.dram_tensor(f"in_{name}", a.shape, mb.dt.from_np(a.dtype), kind="ExternalInput").ap())
    out = nc.dram_tensor("out_0", (N, D), mb.dt.float32, kind="ExternalOutput").ap()
    gnn_kernel(nc, *args, out)
    return run(nc, [arrays], core_ids=[0]).results[0]["out_0"]
```

```python
import concourse.bass as bass
from concourse import mybir
from contextlib import ExitStack

P = 128
N = 3125
D = 128
H = 256
E = 100000
NBLK, BLK = 25, 125
TILES = 784
QROWS, QTILES = 112, 7
REAL_ROWS = E // (QTILES * P)
REST = E - REAL_ROWS * QTILES * P
PAD_DST = N

WIN = 25
SBLK, SW = 5, 625
WM = WIN * SBLK
NWIN = N // WIN
WPB = BLK // WIN
TPT = 4

PR = 4
BPT = 4
TURNS_A = (NBLK - 1) // BPT
BANK_BLKS = 3
CH = -(-NBLK // BANK_BLKS)

GT = 4
GE = GT * P
GROUPS = TILES // GT
GW = 42
GWM = 3 * GW
GUN = 4
TURNS = GROUPS // GUN
NPAD = N + 1 + GW
STEPS = (N + GW) // GW + 1

EPS_ALPHA = 1e-07
EPS_LN = 1e-05
SLOPE = 0.2
CLIP = 2.0

fp32 = mybir.dt.float32
f32r = mybir.dt.float32r
bf16 = mybir.dt.bfloat16
i32 = mybir.dt.int32
i16 = mybir.dt.int16
ALU = mybir.AluOpType
ACT = mybir.ActivationFunctionType
AX = mybir.AxisListType


def bounded(value, low, high):
    return value.with_bounds(min_val=low, max_val=high)


class Counted:

    def __init__(self, ctx, nc, name):
        self.sem = ctx.enter_context(nc.semaphore(name))
        self.n = 0

    def inc(self, instruction, by=1):
        instruction.then_inc(self.sem, by)
        self.n += by
        return self.n


def index_tables(nc, src, dst, T, scr_tile, scr_dst, scr_win, scr_pass):
    with ExitStack() as ctx:
        def sb(name, shape, dt):
            return ctx.enter_context(nc.sbuf_tensor(name, shape, dt))
        EL = QTILES * P
        e_src = sb("e_src", [QROWS, EL], i32)
        e_dst = sb("e_dst", [QROWS, EL], i32)
        e_blk = sb("e_blk", [QROWS, EL], i32)
        keys = sb("keys", [QROWS, 4, EL], fp32)
        blkf = sb("blkf", [QROWS, EL], fp32)
        dst16 = sb("dst16", [QROWS, EL], i16)
        identf = sb("identf1", [P, P], fp32)
        onesf = sb("onesf1", [P, P], fp32)
        mm = sb("mm", [QROWS, 2, QTILES], fp32)
        mmb = sb("mmb", [P, 2, TILES], fp32)
        up1 = sb("up1", [P, TILES], fp32)
        down = sb("down", [P, TILES], fp32)
        edge = sb("edge", [P, 2], fp32)
        junk = sb("junk", [P, TILES], fp32)
        best = sb("best", [P, 2], fp32)
        wtab = sb("wtab", [P, 2], fp32)
        wtabi = sb("wtabi", [P, 2], i32)
        gmm = sb("gmm", [GROUPS // 2, 2, 2, GT], fp32)
        gbt = sb("gbt", [GROUPS // 2, 2, 2], fp32)
        gspan = sb("gspan", [GROUPS // 2, 2], fp32)
        steps = sb("steps", [P, STEPS], fp32)
        gjunk = sb("gjunk", [P, STEPS], fp32)
        gpass = sb("gpass", [GROUPS // 2, 2], fp32)
        prow = sb("prow", [1, GROUPS], fp32)
        psK = [ctx.enter_context(nc.psum_tensor(f"psK{i}", [P, 512], fp32)) for i in range(QTILES)]
        iota_done = ctx.enter_context(nc.semaphore("iota_done"))
        edges_in = ctx.enter_context(nc.semaphore("edges_in"))
        padded = ctx.enter_context(nc.semaphore("padded"))
        keys_ready = ctx.enter_context(nc.semaphore("keys_ready"))
        keys_turned = ctx.enter_context(nc.semaphore("keys_turned"))
        tile_range = ctx.enter_context(nc.semaphore("tile_range"))
        range_out = ctx.enter_context(nc.semaphore("range_out"))
        range_back = ctx.enter_context(nc.semaphore("range_back"))
        dst16_ready = ctx.enter_context(nc.semaphore("dst16_ready"))
        dst16_out = ctx.enter_context(nc.semaphore("dst16_out"))
        windows_ready = ctx.enter_context(nc.semaphore("windows_ready"))
        groups_ready = ctx.enter_context(nc.semaphore("groups_ready"))
        tables_out = ctx.enter_context(nc.semaphore("tables_out"))
        tables_back = ctx.enter_context(nc.semaphore("tables_back"))
        passes_done = ctx.enter_context(nc.semaphore("passes_done"))
        step_done = Counted(ctx, nc, "step_done")
        block = ctx.enter_context(nc.Block())

        @block.gpsimd
        def _(pool):
            pool.memset(e_src[:, :], 0).then_inc(padded, 1)
            pool.memset(e_dst[:, :], PAD_DST).then_inc(padded, 1)
            pool.memset(onesf[:, :], 1.0).then_inc(iota_done, 1)
            pool.wait_ge(iota_done, 1)
            pool.affine_select(out=identf[:, :], in_=onesf[:, :], compare_op=ALU.is_equal, fill=0.0, base=0,
                               pattern=[[-1, P]], channel_multiplier=1).then_inc(iota_done, 1)
            for out, pattern, base, mult in ((up1[:, :], [[1, TILES]], 1, 0), (down[:, :], [[-1, TILES]], TILES, 0),
                                             (edge[:, :], [[WIN, 2]], 0, WIN),
                                             (steps[:, :], [[GW, STEPS]], 0, 0),
                                             (T.iota_m[:, :], [[1, P]], 0, 0),
                                             (T.iota_n[:, :], [[1, SW + 1]], 0, 0),
                                             (T.win_key[:, :], [[WM, NWIN]], 0, 0)):
                pool.iota(out, pattern, base=base, channel_multiplier=mult,
                          allow_small_or_imprecise_dtypes=True).then_inc(iota_done, 1)

        @block.sync
        def _(sp):
            sp.wait_ge(padded, 2)
            for tile, lst in ((e_src, src), (e_dst, dst)):
                sp.dma_start(tile[0:REAL_ROWS, :], lst[0:REAL_ROWS * EL].rearrange("(q n) -> q n", n=EL)).then_inc(edges_in, 16)
                sp.dma_start(tile[REAL_ROWS:REAL_ROWS + 1, 0:REST], lst[REAL_ROWS * EL:E].rearrange("(q n) -> q n", q=1)).then_inc(edges_in, 16)
            sp.wait_ge(tile_range, 1)
            for c in range(2):
                sp.dma_start(scr_tile[c, :].rearrange("(q k) -> q k", k=QTILES), mm[:, c, :]).then_inc(range_out, 16)
            sp.wait_ge(range_out, 32)
            sp.dma_start(mmb[:, :, :], scr_tile.rearrange("c (o t) -> o c t", o=1).broadcast_to([P, 2, TILES])).then_inc(range_back, 16)
            for c in range(2):
                sp.dma_start(gmm[:, c, :, :], scr_tile[c, :].rearrange("(q r k) -> q r k", r=2, k=GT)).then_inc(range_back, 16)
            sp.wait_ge(dst16_ready, 1)
            sp.dma_start(scr_dst.rearrange("(q n) -> q n", n=EL), dst16[:, :]).then_inc(dst16_out, 16)
            sp.wait_ge(windows_ready, 1)
            with nc.allow_non_contiguous_dma(reason="a few hundred words"):
                sp.dma_start(scr_win.rearrange("(q c) -> q c", c=2), wtabi[0:NWIN, :], allow_slow_non_contiguous=True).then_inc(tables_out, 16)
            sp.wait_ge(groups_ready, 1)
            sp.dma_start(scr_pass[0, :].rearrange("(q r) -> q r", r=2), gpass[:, :]).then_inc(tables_out, 16)
            sp.dma_start(scr_pass[1, :].rearrange("(q r) -> q r", r=2), gbt[:, 0, :]).then_inc(tables_out, 16)
            sp.wait_ge(tables_out, 48)
            sp.dma_start(T.win_tab[0:1, :], scr_win.rearrange("(o n) -> o n", o=1)).then_inc(tables_back, 16)
            sp.dma_start(prow[0:1, :], scr_pass[0:1, :]).then_inc(tables_back, 16)
            sp.dma_start(T.base_row[0:1, :], scr_pass[1:2, :]).then_inc(tables_back, 16)
            sp.dma_start(T.base_all[:, :], scr_pass[1:2, :].broadcast_to([P, GROUPS])).then_inc(tables_back, 16)
            sp.wait_ge(dst16_out, 16)

        @block.vector
        def _(dve):
            def step(ins):
                dve.wait_ge(step_done.sem, step_done.inc(ins))
            dve.wait_ge(edges_in, 64)
            dve.tensor_copy(keys[:, 3, :], e_dst[:, :]).then_inc(keys_ready, 1)
            step(dve.tensor_copy(keys[:, 2, :], e_src[:, :]))
            step(dve.tensor_scalar(e_blk[:, :], keys[:, 2, :], 1678.0, None, ALU.mult))
            step(dve.tensor_single_scalar(e_blk[:, :], e_blk[:, :], 20, ALU.logical_shift_right))
            step(dve.tensor_copy(blkf[:, :], e_blk[:, :]))
            dve.scalar_tensor_tensor(keys[:, 1, :], blkf[:, :], -float(SW), keys[:, 2, :], ALU.mult, ALU.add).then_inc(keys_ready, 1)
            dve.wait_ge(keys_ready, 2)
            dve.scalar_tensor_tensor(keys[:, 0, :], keys[:, 3, :], float(SBLK), blkf[:, :], ALU.mult, ALU.add).then_inc(keys_ready, 1)
            by_tile = keys[:, 3, :].rearrange("q (k p) -> q k p", p=P)
            dve.tensor_reduce(mm[:, 0, :], by_tile, AX.X, ALU.min)
            step(dve.tensor_reduce(mm[:, 1, :], by_tile, AX.X, ALU.max))
            dve.tensor_copy(dst16[:, :], keys[:, 3, :]).then_inc(dst16_ready, 1)
            dve.sem_inc(tile_range, 1)
            for k in range(QTILES):
                dve.wait_ge(keys_turned, k + 1)
                dve.tensor_copy(T.edge_keys[:, :, 0:TILES].rearrange("p c (q k) -> p c q k", k=QTILES)[:, :, :, k],
                                psK[k][:, 0:4 * QROWS].rearrange("p (c q) -> p c q", c=4))
            step(dve.memset(T.edge_keys[:, :, TILES:TILES + TPT - 1], -1.0))
            step(dve.tensor_copy(T.src_idx[:, :], T.edge_keys[:, 2, 0:TILES]))
            dve.wait_ge(iota_done, 9)
            dve.wait_ge(range_back, 48)
            step(dve.scalar_tensor_tensor(junk[:, :], mmb[:, 0, :], edge[:, 1:2], up1[:, :], ALU.is_lt, ALU.mult))
            step(dve.tensor_reduce(best[:, 1:2], junk[:, :], AX.X, ALU.max))
            step(dve.scalar_tensor_tensor(junk[:, :], mmb[:, 1, :], edge[:, 0:1], down[:, :], ALU.is_ge, ALU.mult))
            step(dve.tensor_reduce(best[:, 0:1], junk[:, :], AX.X, ALU.max))
            step(dve.tensor_scalar(wtab[:, 0:1], best[:, 0:1], -1.0, float(TILES), ALU.mult, ALU.add))
            step(dve.tensor_scalar(wtab[:, 0:1], wtab[:, 0:1], float(TILES - 1), None, ALU.min))
            step(dve.tensor_scalar(wtab[:, 1:2], wtab[:, 0:1], 1.0, None, ALU.add))
            step(dve.tensor_tensor(wtab[:, 1:2], best[:, 1:2], wtab[:, 1:2], ALU.max))
            step(dve.tensor_copy(wtabi[:, :], wtab[:, :]))
            dve.sem_inc(windows_ready, 1)
            step(dve.tensor_reduce(gbt[:, 0, :], gmm[:, 0, :, :], AX.X, ALU.min))
            step(dve.tensor_reduce(gbt[:, 1, :], gmm[:, 1, :, :], AX.X, ALU.max))
            step(dve.tensor_tensor(gspan[:, :], gbt[:, 1, :], gbt[:, 0, :], ALU.subtract))
            for r in range(2):
                step(dve.tensor_scalar(gjunk[0:GROUPS // 2, :], steps[0:GROUPS // 2, :], gspan[:, r:r + 1], 0.0, ALU.is_le, ALU.add,
                                       accum_out=gpass[:, r:r + 1]))
            dve.sem_inc(groups_ready, 1)
            dve.wait_ge(tables_back, 64)
            step(dve.tensor_copy(T.base_i[0:1, :], T.base_row[0:1, :]))
            step(dve.tensor_reduce(T.passes_f[0:1, :], prow[0:1, :], AX.X, ALU.max))
            step(dve.tensor_copy(T.passes_i[0:1, :], T.passes_f[0:1, :]))
            step(dve.tensor_tensor(T.edge_keys[:, 3, 0:TILES].rearrange("p (g k) -> p g k", k=GT),
                                   T.edge_keys[:, 3, 0:TILES].rearrange("p (g k) -> p g k", k=GT),
                                   T.base_all[:, :].rearrange("p (g o) -> p g o", o=1).broadcast_to([P, GROUPS, GT]), ALU.subtract))
            step(dve.tensor_scalar(T.neg_base[:, :], T.base_all[:, :], -1.0, None, ALU.mult))

        @block.tensor
        def _(pe):
            pe.wait_ge(iota_done, 2)
            pe.wait_ge(keys_ready, 3)
            for k in range(QTILES):
                for c in range(4):
                    last = pe.transpose(psK[k][:, c * QROWS:(c + 1) * QROWS], keys[:, c, k * P:(k + 1) * P], identf[0:QROWS, 0:QROWS])
                last.then_inc(keys_turned, 1)

CHUNKS = (0, 0, 1, 1, 1, 1, 1, 1, 1, 2)
LEAKY_AT, CLIP_AT, EXP_AT = 0, 0, 1

def layernorm(dve, step, T, rows, moments_ready, std_ready):
    for b in range(NBLK):
        last = dve.bn_stats(T.stats[:, b, :], rows[:, b, :])
    step(last)
    for b in range(NBLK):
        last = dve.bn_aggr(T.mv[:, b, :], T.stats[:, b, :])
    step(last)
    step(dve.tensor_scalar(T.den[:, :], T.mv[:, :, 1], EPS_LN, None, ALU.add))
    dve.sem_inc(moments_ready, 1)
    dve.wait_ge(std_ready, 1)
    step(dve.reciprocal(T.den[:, :], T.std[:, :]))
    for b in range(NBLK):
        last = dve.tensor_scalar(rows[:, b, :], rows[:, b, :], T.mv[:, b, 0:1], T.den[:, b:b + 1], ALU.subtract, ALU.mult)
    step(last)



def attention(nc, T, x, w0, att):
    with ExitStack() as ctx:
        def sb(name, shape, dt):
            return ctx.enter_context(nc.sbuf_tensor(name, shape, dt))

        def sem(name):
            return ctx.enter_context(nc.semaphore(name))
        W2 = D + 1
        SWE, WME = SW + 1, WM + 1
        HALF = SWE // 2
        xn = T.x1
        w_sb = sb("w_sb", [D, D], fp32)
        wT = sb("wT", [D, D], fp32)
        att_sb = sb("att_sb", [D, 2], fp32)
        ones = sb("ones_a", [P, P], fp32)
        wk = sb("wk", [D, D + 2], fp32)
        a1b = sb("a1b", [D, P], fp32)
        hx = sb("hx", [BLK, NBLK + 1, D + 2], fp32)
        s1r = sb("s1r", [P, N], fp32)
        s2s = sb("s2s", [BLK, NBLK], fp32)
        cnt = sb("cnt", [P, 2, N], fp32)
        xT = cnt[:, 0, :]
        pr = sb("pr", [BLK, PR, N], fp32)
        acc = sb("acc", [BLK, NBLK, W2], fp32)
        hot_m = sb("hot_m", [P, TPT, WME], bf16)
        hot_n = sb("hot_n", [P, TPT, SWE], bf16)
        zeros = sb("zeros", [P, HALF], bf16)
        stage = sb("stage", [P, 2, SWE], fp32)
        psC = [ctx.enter_context(nc.psum_tensor(f"psC{i}", [P, 2, 512], fp32)) for i in range(2)]
        psT = [psC[i // 2][:, i % 2, :] for i in range(4)]
        psO = [ctx.enter_context(nc.psum_tensor(f"psO{i}", [P, 512], fp32)) for i in range(2)]
        loaded = sem("loaded")
        set_up = Counted(ctx, nc, "set_up")
        ones_ready = sem("ones_ready")
        k_turned = sem("k_turned")
        k_copied = sem("k_copied")
        ka_done = sem("ka_done")
        wk_ready = sem("wk_ready")
        x_turned = sem("x_turned")
        x_copied = sem("x_copied")
        h_done = sem("h_done")
        h_copied = sem("h_copied")
        s1_done = sem("s1_done")
        s1_copied = sem("s1_copied")
        zeros_ready = sem("zeros_ready")
        hot_ready = [sem(f"hot_ready{i}") for i in range(TPT)]
        hot_free = [sem(f"hot_free{i}") for i in range(TPT)]
        window_summed = sem("window_summed")
        bank_read = sem("bank_read")
        stage_out = [sem(f"stage_out{i}") for i in range(2)]
        sp_order = sem("sp_order_a")
        pool_order = sem("pool_order_a")
        low_ready = sem("low_ready")
        leaky_ready = sem("leaky_ready")
        clip_ready = sem("clip_ready")
        exp_ready = sem("exp_ready")
        prob_ready = sem("prob_ready")
        chunk_done = sem("chunk_done")
        chunk_added = sem("chunk_added")
        moments_ready = sem("moments_ready")
        std_ready = sem("std_ready")
        chain = Counted(ctx, nc, "chain_a")
        block = ctx.enter_context(nc.Block())

        def chunk(c):
            return list(range(c * BANK_BLKS, min(NBLK, (c + 1) * BANK_BLKS)))

        def chunks_at(v, u):
            in_pair = (v % 2) * WPB + u
            start = sum(CHUNKS[:in_pair])
            return range(start, start + CHUNKS[in_pair]) if v >= 0 else ()

        def blocks(eng, body):
            body(0, -1)
            with eng.Fori(0, TURNS_A, 1) as t:
                t = bounded(t, 0, TURNS_A - 1)
                for v in range(BPT):
                    body(t, v)

        def windows(eng, tag, window, tile_aps, tile):
            turn = eng.alloc_register(f"{tag}_turn")
            eng.reg_mov(turn, 1)
            regs = [eng.alloc_register(f"{tag}_win{i}") for i in range(2 * WPB)]

            def body(t, v):
                eng.reg_load(regs, T.win_tab[0:1, bass.ds(t * (BPT * WPB * 2) + (v + 1) * WPB * 2, 2 * WPB)])
                for u in range(WPB):
                    first = eng.snap(regs[2 * u], min_val=0, max_val=TILES - 1)
                    end = eng.snap(regs[2 * u + 1], min_val=1, max_val=TILES)
                    before, after = window(t, v, u)
                    before()
                    with eng.Fori(first, end, TPT) as n:
                        n = bounded(n, 0, TILES - 1)
                        now = eng.snap(turn, min_val=1, max_val=10**6)
                        aps = tile_aps(n, t, v, u)
                        for s in range(TPT):
                            tile(s, now, aps, v, u)
                        eng.reg_add(turn, turn, 1)
                    after()
            return body

        @block.sync
        def _(sp):
            sp.dma_start(w_sb[:, :], w0).then_inc(loaded, 16)
            sp.dma_start(att_sb[:, :], att.rearrange("(c f) o -> f (c o)", c=2), allow_slow_non_contiguous=True).then_inc(loaded, 16)
            sp.dma_start(xn[:, :, :], x.rearrange("(b n) f -> n b f", b=NBLK)).then_inc(loaded, 16)
            for s in range(2):
                sp.sem_inc(stage_out[s], 16)
            sp.wait_ge(s1_copied, 7)

            def body(t, v):
                for u in range(WPB):
                    w = (v + 1) * WPB + u
                    if u == 0:
                        sp.wait_ge(prob_ready, t * BPT + v + 2)
                        sp.sem_inc(sp_order, 1)
                    sp.wait_ge(bank_read, t * (BPT * WPB) + w + 3)
                    sp.sem_inc(sp_order, 1)
                    sp.dma_start(cnt[u * WIN:(u + 1) * WIN, (v + 1) % 2, :], stage[0:WM, w % 2, 0:SW]).then_inc(stage_out[w % 2], 16)
            blocks(sp, body)

        @block.gpsimd
        def _(pool):
            pool.memset(ones[:, :], 1.0).then_inc(ones_ready, 1)
            pool.memset(pr[:, 0, :], 0.0).then_inc(ones_ready, 1)
            pool.memset(hx[:, 0, :], 0.0).then_inc(ones_ready, 1)
            pool.wait_ge(ones_ready, 1)
            pool.affine_select(out=T.ident[:, :], in_=ones[:, :], compare_op=ALU.is_equal, fill=0.0, base=0,
                               pattern=[[-1, P]], channel_multiplier=1).then_inc(ones_ready, 1)
            pool.sem_inc(prob_ready, 2)

            def body(t, v):
                last = (v + 2) * WPB - 1
                for s in range(2):
                    stored = (last - s) // 2 + 1
                    pool.wait_ge(stage_out[s], t * (BPT * WPB * 8) + 16 * stored + 16)
                    pool.sem_inc(pool_order, 1)
                pool.wait_ge(exp_ready, t * BPT + v + 2)
                pool.sem_inc(pool_order, 1)
                slot = pr[:, (v + 2) % PR, :]
                pool.tensor_tensor(slot, slot, cnt[0:BLK, (v + 1) % 2, :], ALU.mult).then_inc(prob_ready, 1)
            blocks(pool, body)

        @block.tensor
        def _(pe):
            pe.wait_ge(loaded, 48)
            pe.wait_ge(ones_ready, 4)
            pe.transpose(psT[0][:, 0:P], w_sb[:, :], T.ident[:, :]).then_inc(k_turned, 1)
            pe.wait_ge(k_copied, 1)
            pe.matmul(psT[0][:, 256:258], wT[:, :], att_sb[:, :], start=True, stop=True).then_inc(ka_done, 1)
            for b in range(NBLK):
                if b >= 3:
                    pe.wait_ge(x_copied, b - 2)
                pe.transpose(psT[1 + b % 3][:, 0:BLK], xn[:, b, :], T.ident[0:BLK, 0:BLK]).then_inc(x_turned, 1)
            pe.wait_ge(wk_ready, 3)
            pe.wait_ge(x_copied, NBLK)
            for b in range(NBLK):
                if b >= 4:
                    pe.wait_ge(h_copied, b - 3)
                pe.matmul(psT[b % 4][0:BLK, 0:D + 2], xT[:, b * BLK:(b + 1) * BLK], wk[:, :], start=True, stop=True).then_inc(h_done, 1)
            pe.wait_ge(h_copied, NBLK)
            for c in range(7):
                n0, n1 = c * 512, min(N, (c + 1) * 512)
                if c >= 4:
                    pe.wait_ge(s1_copied, c - 3)
                pe.matmul(psT[c % 4][:, 0:n1 - n0], a1b[:, :], xT[:, n0:n1], start=True, stop=True).then_inc(s1_done, 1)
            pe.wait_ge(s1_copied, 7)
            pe.wait_ge(set_up.sem, 2)
            pe.wait_ge(zeros_ready, 1)
            for s in range(TPT):
                pe.sem_inc(hot_free[s], 1)
            pe.sem_inc(chunk_done, CH)

            def sum_chunk(t, v, c):
                n = (v // 2) * CH + c
                if c == 0:
                    pe.wait_ge(prob_ready, t * BPT + 2 * (v // 2) + 3)
                pe.wait_ge(chunk_added, t * (2 * CH) + n + 1)
                first = (v // 2) * 2
                for a, b in enumerate(chunk(c)):
                    for k in range(2):
                        last = pe.matmul(psO[n % 2][0:BLK, a * W2:(a + 1) * W2], pr[:, (first + k) % PR, b * BLK:(b + 1) * BLK],
                                         hx[:, bass.ds(t * BPT + first + k, 1), 0:W2].rearrange("p o w -> p (o w)"), start=(k == 0), stop=(k == 1))
                last.then_inc(chunk_done, 1)

            def window(t, v, u):
                w = (v + 1) * WPB + u
                bank = psC[w % 2]

                def before():
                    for c in chunks_at(v, u):
                        sum_chunk(t, v, c)
                    pe.wait_ge(bank_read, t * (BPT * WPB) + w + 1)
                    for k in range(2):
                        pe.matmul(bank[0:WME, k, 0:HALF], zeros[:, 0:WME], zeros[:, :], start=True, stop=True, skip_group_check=True)

                def after():
                    pe.matmul(bank[0:WME, 1, 0:8], zeros[:, 0:WME], zeros[:, 0:8], start=False, stop=True,
                              skip_group_check=True).then_inc(window_summed, 1)
                return before, after

            def tile(s, now, aps, v, u):
                pe.wait_ge(hot_ready[s], now)
                bank = psC[((v + 1) * WPB + u) % 2]
                for k in range(2):
                    last = pe.matmul(bank[0:WME, k, 0:HALF], hot_m[:, s, :], hot_n[:, s, k * HALF:(k + 1) * HALF],
                                     start=False, stop=True, skip_group_check=True)
                last.then_inc(hot_free[s], 1)
            blocks(pe, windows(pe, "pe", window, lambda n, t, v, u: None, tile))
            for c in range(CH):
                sum_chunk(TURNS_A, 0, c)

        @block.scalar
        def _(act):
            for b in range(NBLK):
                act.wait_ge(x_turned, b + 1)
                act.activation(xT[:, b * BLK:(b + 1) * BLK], psT[1 + b % 3][:, 0:BLK], ACT.Copy).then_inc(x_copied, 1)
            for c in range(7):
                n0, n1 = c * 512, min(N, (c + 1) * 512)
                act.wait_ge(s1_done, c + 1)
                act.activation(s1r[:, n0:n1], psT[c % 4][:, 0:n1 - n0], ACT.Copy).then_inc(s1_copied, 1)
            act.wait_ge(s1_copied, 7)
            act.wait_ge(set_up.sem, 2)
            act.sem_inc(bank_read, 2)

            def body(t, v):
                slot = pr[:, (v + 2) % PR, :]
                if v >= 0:
                    act.wait_ge(chunk_done, t * (2 * CH) + (v // 2) * CH + CH)
                act.activation(slot, s1r[0:BLK, :], ACT.Identity, bias=s2s[:, bass.ds(t * BPT + v + 1, 1)], scale=SLOPE).then_inc(low_ready, 1)
                for u in range(WPB):
                    w = (v + 1) * WPB + u
                    act.wait_ge(window_summed, t * (BPT * WPB) + w + 1)
                    act.wait_ge(stage_out[w % 2], t * (BPT * WPB * 8) + 16 * (w // 2) + 16)
                    act.activation(stage[0:WME, w % 2, :].rearrange("p (k n) -> p k n", k=2), psC[w % 2][0:WME, :, 0:HALF], ACT.Copy).then_inc(bank_read, 1)
                    if u == EXP_AT:
                        act.wait_ge(clip_ready, t * BPT + v + 2)
                        act.activation(slot, slot, ACT.Exp).then_inc(exp_ready, 1)
            blocks(act, body)
            act.wait_ge(moments_ready, 1)
            act.activation(T.std[:, :], T.den[:, :], ACT.Sqrt).then_inc(std_ready, 1)

        @block.vector
        def _(dve):
            def step(ins):
                dve.wait_ge(chain.sem, chain.inc(ins))
            dve.memset(zeros[:, :], 0.0).then_inc(zeros_ready, 1)
            dve.wait_ge(k_turned, 1)
            dve.tensor_copy(wT[:, :], psT[0][:, 0:P]).then_inc(k_copied, 1)
            dve.tensor_copy(wk[:, 0:D], w_sb[:, :]).then_inc(wk_ready, 1)
            dve.wait_ge(ka_done, 1)
            dve.tensor_copy(wk[:, D:D + 2], psT[0][:, 256:258]).then_inc(wk_ready, 1)
            dve.wait_ge(wk_ready, 2)
            dve.wait_ge(ones_ready, 4)
            dve.tensor_scalar(a1b[:, :], ones[:, :], wk[:, D:D + 1], None, ALU.mult).then_inc(wk_ready, 1)
            for b in range(NBLK):
                dve.wait_ge(h_done, b + 1)
                dve.tensor_copy(hx[:, b + 1, :], psT[b % 4][0:BLK, 0:D + 2]).then_inc(h_copied, 1)
            dve.wait_ge(h_copied, NBLK)
            set_up.inc(dve.tensor_scalar(s2s[:, :], hx[:, 1:NBLK + 1, D + 1], SLOPE, None, ALU.mult))
            set_up.inc(dve.memset(hx[:, :, D:D + 1], 1.0))
            dve.wait_ge(s1_copied, 7)
            step(dve.memset(acc[:, :, :], 0.0))
            dve.sem_inc(chunk_added, 2)

            def add_chunk(t, v, c):
                n = (v // 2) * CH + c
                blks = chunk(c)
                dve.wait_ge(chunk_done, t * (2 * CH) + n + 1 + CH)
                part = acc[:, blks[0]:blks[-1] + 1, :]
                dve.tensor_tensor(part, psO[n % 2][0:BLK, 0:len(blks) * W2].rearrange("p (b w) -> p b w", w=W2),
                                  part, ALU.add).then_inc(chunk_added, 1)

            def window(t, v, u):
                slot = pr[:, (v + 2) % PR, :]

                def before():
                    dve.lower_ap(T.win_key[:, bass.ds(t * (BPT * WPB) + (v + 1) * WPB + u, 1)])

                def after():
                    if u == LEAKY_AT:
                        dve.wait_ge(low_ready, t * BPT + v + 2)
                        dve.scalar_tensor_tensor(slot, s1r[0:BLK, :], hx[:, bass.ds(t * BPT + v + 2, 1), D + 1:D + 2].rearrange("p o w -> p (o w)"), slot, ALU.add, ALU.max).then_inc(leaky_ready, 1)
                    if u == CLIP_AT:
                        dve.wait_ge(leaky_ready, t * BPT + v + 2)
                        dve.tensor_scalar(slot, slot, -CLIP, CLIP, ALU.max, ALU.min).then_inc(clip_ready, 1)
                    for c in chunks_at(v, u):
                        add_chunk(t, v, c)
                return before, after

            def tile_aps(n, t, v, u):
                keys = T.edge_keys[:, 0:2, bass.ds(n, TPT)]
                dve.lower_ap(keys)
                return keys, T.win_key[:, bass.ds(t * (BPT * WPB) + (v + 1) * WPB + u, 1)]

            def tile(s, now, aps, v, u):
                keys, key0 = aps
                dve.wait_ge(hot_free[s], now)
                dve.tensor_scalar(hot_m[:, s, :], T.iota_m[:, 0:WME], key0, keys[:, 0, s:s + 1], ALU.add, ALU.is_equal)
                dve.tensor_scalar(hot_n[:, s, :], T.iota_n[:, :], keys[:, 1, s:s + 1], None, ALU.is_equal).then_inc(hot_ready[s], 1)
            blocks(dve, windows(dve, "dve", window, tile_aps, tile))
            for c in range(CH):
                add_chunk(TURNS_A, 0, c)
            dve.wait_ge(chunk_added, (2 * TURNS_A + 1) * CH + 2)
            step(dve.tensor_scalar(T.den[:, :], acc[:, :, D], EPS_ALPHA, None, ALU.add))
            step(dve.reciprocal(T.den[:, :], T.den[:, :]))
            for b in range(NBLK):
                last = dve.scalar_tensor_tensor(xn[:, b, :], acc[:, b, 0:D], T.den[:, b:b + 1], xn[:, b, :], ALU.mult, ALU.add)
            step(last)
            layernorm(dve, step, T, xn, moments_ready, std_ready)


def node_tables(nc, T, wm1, bm1, table_a, table_b):
    with ExitStack() as ctx:
        def sb(name, shape, dt):
            return ctx.enter_context(nc.sbuf_tensor(name, shape, dt))

        def sem(name):
            return ctx.enter_context(nc.semaphore(name))
        w = sb("wm1_sb", [D, 2, H], fp32)
        b1 = sb("bm1_sb", [P, H], fp32)
        a_st = sb("a_st", [BLK, 2, H], fp32)
        rest = sb("rest", [BLK, 2, 2, H], fp32)
        b_st = sb("b_st", [BLK, 2, 3, H], bf16)
        zpad = sb("zpad", [NPAD - N, 3 * H], bf16)
        psX = [ctx.enter_context(nc.psum_tensor(f"psX{i}", [P, 512], fp32)) for i in range(2)]
        psN = [ctx.enter_context(nc.psum_tensor(f"psN{i}", [P, 2, H], fp32)) for i in range(2)]
        loaded = sem("loaded_t")
        x_turned = sem("x_turned_t")
        x_copied = sem("x_copied_t")
        ab_done = sem("ab_done")
        part_ready = sem("part_ready")
        rest_ready = sem("rest_ready")
        a_ready = sem("a_ready")
        b_ready = sem("b_ready")
        zpad_ready = sem("zpad_ready")
        a_out = [sem(f"a_out{i}") for i in range(2)]
        b_out = [sem(f"b_out{i}") for i in range(2)]
        block = ctx.enter_context(nc.Block())

        @block.sync
        def _(sp):
            sp.dma_start(w[:, :, :], wm1.rearrange("(c f) h -> f c h", c=2)).then_inc(loaded, 16)
            sp.dma_start(b1[:, :], bm1.rearrange("(o h) -> o h", o=1).broadcast_to([P, H])).then_inc(loaded, 16)
            sp.wait_ge(zpad_ready, 1)
            sp.dma_start(table_b[N:NPAD, :], zpad[:, :]).then_inc(b_out[0], 16)
            for b in range(NBLK):
                sp.wait_ge(a_ready, b + 1)
                sp.dma_start(table_a[b * BLK:(b + 1) * BLK, :], a_st[:, b % 2, :]).then_inc(a_out[b % 2], 16)
                sp.wait_ge(b_ready, b + 1)
                sp.dma_start(table_b[b * BLK:(b + 1) * BLK, :], b_st[:, b % 2, :, :]).then_inc(b_out[b % 2], 16)
            sp.wait_ge(a_out[0], 16 * 13)
            sp.wait_ge(a_out[1], 16 * 12)
            sp.wait_ge(b_out[0], 16 * 14)
            sp.wait_ge(b_out[1], 16 * 12)

        def tables(pe, b):
            pe.wait_ge(x_copied, b + 1)
            if b >= 2:
                pe.wait_ge(rest_ready, 2 * (b - 1))
                pe.wait_ge(a_ready, b - 1)
            pe.matmul(psN[b % 2][0:BLK, :, :].rearrange("p c h -> p (c h)"), T.x1T[:, b * BLK:(b + 1) * BLK],
                      w[:, :, :].rearrange("p c h -> p (c h)"), start=True, stop=True).then_inc(ab_done, 1)

        @block.tensor
        def _(pe):
            pe.wait_ge(loaded, 32)
            for b in range(NBLK):
                if b >= 2:
                    pe.wait_ge(x_copied, b - 1)
                pe.transpose(psX[b % 2][:, 0:BLK], T.x1[:, b, :], T.ident[0:BLK, 0:BLK]).then_inc(x_turned, 1)
                if b >= 1:
                    tables(pe, b - 1)
            tables(pe, NBLK - 1)

        def parts(act, b):
            s = b % 2
            act.wait_ge(a_ready, b + 1)
            if b >= 2:
                act.wait_ge(b_out[s], 16 * (b // 2) + (16 if s == 0 else 0))
            act.activation(b_st[:, s, 0, :], psN[s][0:BLK, 1, :], ACT.Copy).then_inc(part_ready, 1)
            act.wait_ge(rest_ready, 2 * b + 1)
            act.activation(b_st[:, s, 1, :], rest[:, s, 0, :], ACT.Copy).then_inc(part_ready, 1)
            act.wait_ge(rest_ready, 2 * b + 2)
            act.activation(b_st[:, s, 2, :], rest[:, s, 1, :], ACT.Copy).then_inc(b_ready, 1)

        @block.scalar
        def _(act):
            for b in range(NBLK):
                act.wait_ge(x_turned, b + 1)
                act.activation(T.x1T[:, b * BLK:(b + 1) * BLK], psX[b % 2][:, 0:BLK], ACT.Copy).then_inc(x_copied, 1)
                if b >= 1:
                    parts(act, b - 1)
            parts(act, NBLK - 1)

        @block.vector
        def _(dve):
            dve.memset(zpad[:, :], 0.0).then_inc(zpad_ready, 1)
            dve.wait_ge(loaded, 32)
            for b in range(NBLK):
                s = b % 2
                dve.wait_ge(ab_done, b + 1)
                if b >= 2:
                    dve.wait_ge(a_out[s], 16 * (b // 2))
                dve.tensor_tensor(a_st[:, s, :], psN[s][0:BLK, 0, :], b1[0:BLK, :], ALU.add).then_inc(a_ready, 1)
                dve.wait_ge(part_ready, 2 * b + 1)
                if b >= 2:
                    dve.wait_ge(b_ready, b - 1)
                dve.tensor_tensor(rest[:, s, 0, :], psN[s][0:BLK, 1, :], b_st[:, s, 0, :], ALU.subtract).then_inc(rest_ready, 1)
                dve.wait_ge(part_ready, 2 * b + 2)
                dve.wait_ge(rest_ready, 2 * b + 1)
                dve.tensor_tensor(rest[:, s, 1, :], rest[:, s, 0, :], b_st[:, s, 1, :], ALU.subtract).then_inc(rest_ready, 1)


def messages(nc, T, wm2, bm2, table_a, table_b, scr_dst):
    with ExitStack() as ctx:
        def sb(name, shape, dt):
            return ctx.enter_context(nc.sbuf_tensor(name, shape, dt))

        def sem(name):
            return ctx.enter_context(nc.semaphore(name))
        w = sb("wm2_sb", [P, 2, H], fp32)
        w_hi = sb("wm2_hi", [P, 2, H], f32r)
        w_lo = sb("wm2_lo", [P, 2, H], f32r)
        nb2 = sb("nb2", [P, 2, H], fp32)
        ones = sb("ones_m", [P, P], bf16)
        third = sb("third", [P, 1], fp32)
        third_i = sb("third_i", [P, 1], i32)
        idx = sb("idx", [P, GUN, GT], i32)
        ga = sb("ga", [P, GUN, GT, H], fp32)
        bw = sb("bw", [P, GUN, H], bf16)
        dstb = sb("dstb", [P, GUN, GE], i16)
        hot_t = sb("hot_t", [P, GUN, GE], bf16)
        hot_e = sb("hot_e", [P, GUN, GT, GW], fp32)
        hot_b = sb("hot_b", [P, GUN, GT, GW], bf16)
        h1_hi = sb("h1_hi", [P, 2, 2, GE], f32r)
        h1_lo = sb("h1_lo", [P, 2, 2, GE], f32r)
        h2 = sb("h2", [P, 2, GT, H], fp32)
        ps1 = [[ctx.enter_context(nc.psum_tensor(f"ps1_{i}{k}", [P, GE], fp32)) for k in range(2)] for i in range(2)]
        ps2 = [ctx.enter_context(nc.psum_tensor(f"ps2_{i}", [P, 2, H], fp32)) for i in range(2)]
        psA = [ctx.enter_context(nc.psum_tensor(f"psA_{i}", [P, 3, GW], fp32)) for i in range(2)]
        loaded = sem("loaded_m")
        setup_done = sem("setup_done")
        split_done = sem("split_done")
        idx_ready = sem("idx_ready")
        pool_order = sem("pool_order")
        sp_order = sem("sp_order")
        gathered = [sem(f"gathered{i}") for i in range(GUN)]
        window_in = [sem(f"window_in{i}") for i in range(GUN)]
        dst_in = [sem(f"dst_in{i}") for i in range(GUN)]
        hot_ready = sem("hot_ready_m")
        hot_b_ready = sem("hot_b_ready")
        h1_summed = sem("h1_summed")
        hi_ready = sem("hi_ready")
        lo_ready = sem("lo_ready")
        h2_summed = sem("h2_summed")
        h2_ready = sem("h2_ready")
        agg_summed = sem("agg_summed")
        agg_added = sem("agg_added")
        sweep_done = sem("sweep_done")
        tables_next = sem("tables_next")
        block = ctx.enter_context(nc.Block())
        LAST = GROUPS - GUN

        def sweeps(eng, first, body, end):
            passes = eng.value_load(T.passes_i[0:1, 0:1], min_val=1, max_val=STEPS)
            with eng.Fori(0, passes) as p:
                if first:
                    first(eng.snap(p * GROUPS, min_val=0, max_val=STEPS * GROUPS))
                with eng.Fori(0, LAST, GUN) as i:
                    i = bounded(i, 0, LAST - GUN)
                    body(eng.snap(p * GROUPS + i, min_val=0, max_val=STEPS * GROUPS), i, False)
                body(eng.snap(p * GROUPS + LAST, min_val=0, max_val=STEPS * GROUPS), LAST, True)
                end(p)

        @block.sync
        def _(sp):
            sp.dma_start(w[:, :, :], wm2.rearrange("(c f) h -> f c h", c=2)).then_inc(loaded, 16)
            for c in range(2):
                sp.dma_start(nb2[:, c, :], bm2.rearrange("(o h) -> o h", o=1).broadcast_to([P, H])).then_inc(loaded, 16)
            regs = [sp.alloc_register(f"sp_base{u}") for u in range(GUN)]

            def body(n, i, last):
                sp.reg_load(regs, T.base_i[0:1, bass.ds(i, GUN)])
                for u in range(GUN):
                    base = sp.snap(regs[u], min_val=0, max_val=N + 1)
                    sp.wait_ge(h1_summed, (n + u) * 2 + 2)
                    sp.sem_inc(sp_order, 1)
                    sp.dma_start(bw[0:GWM, u, :], table_b.rearrange("n (c h) -> (n c) h", c=3)[bass.ds(base * 3, GWM), :]).then_inc(window_in[u], 16)
                    sp.dma_start(dstb[0:GWM, u, :], scr_dst.rearrange("(o e) -> o e", o=1)[:, bass.ds((i + u) * GE, GE)].broadcast_to([GWM, GE])).then_inc(dst_in[u], 16)

            def end(p):
                sp.wait_ge(tables_next, p + 1)
                sp.sem_inc(sp_order, 1)
            sweeps(sp, None, body, end)

        @block.gpsimd
        def _(pool):
            pool.iota(third_i[:, :], [[0, 1]], base=0, channel_multiplier=1).then_inc(setup_done, 1)
            pool.memset(ones[:, :], 1.0).then_inc(setup_done, 1)

            def body(n, i, last):
                for u in range(GUN):
                    pool.wait_ge(idx_ready, n + u + 1)
                    pool.sem_inc(pool_order, 1)
                    for k in range(GT):
                        pool.indirect_dma_start(ga[:, u, k, :], None, table_a,
                                                bass.IndirectOffsetOnAxis(ap=idx[:, u, k:k + 1], axis=0)).then_inc(gathered[u], 16)

            def end(p):
                pool.wait_ge(tables_next, p + 1)
                pool.sem_inc(pool_order, 1)
            sweeps(pool, None, body, end)

        @block.tensor
        def _(pe):
            pe.sem_inc(h1_summed, 2 * GUN)
            pe.wait_ge(split_done, 3)
            pe.wait_ge(setup_done, 3)

            def hidden1(n, u):
                s = u % GUN
                pe.wait_ge(window_in[s], (n if u < GUN else n + GUN) * 4 + 16)
                pe.wait_ge(hot_ready, n + u + 1)
                pe.wait_ge(gathered[s], (n if u < GUN else n + GUN) * 16 + 64)
                pe.wait_ge(lo_ready, (n + u) * 2 + 2)
                for k in range(2):
                    bank = ps1[u % 2][k]
                    pe.matmul(bank[:, :], bw[0:GWM, s, k * P:(k + 1) * P], hot_t[0:GWM, s, :], start=True, stop=True, skip_group_check=True)
                    for t in range(GT):
                        last = pe.matmul(bank[:, t * P:(t + 1) * P], ga[:, s, t, k * P:(k + 1) * P], T.ident[:, :],
                                         is_transpose=True, start=False, stop=True, skip_group_check=True)
                    last.then_inc(h1_summed, 1)

            def hidden2(n, u):
                pe.wait_ge(hi_ready, (n + u) * 2 + 2)
                for q in range(2):
                    pe.wait_ge(h2_ready, (n + u) * 2 + q + 1)
                    tiles = (2 * q, 2 * q + 1)
                    for t in tiles:
                        for k in range(2):
                            hi = h1_hi[:, u % 2, k, t * P:(t + 1) * P]
                            pe.matmul(ps2[q][:, t % 2, :], hi, w_hi[:, k, :], start=(t % 2 == 0 and k == 0), stop=True, skip_group_check=True)
                            pe.matmul(ps2[q][:, t % 2, :], hi, w_lo[:, k, :], start=False, stop=True, skip_group_check=True)
                    if q == 0:
                        pe.wait_ge(lo_ready, (n + u) * 2 + 6)
                    for t in tiles:
                        for k in range(2):
                            last = pe.matmul(ps2[q][:, t % 2, :], h1_lo[:, u % 2, k, t * P:(t + 1) * P], w_hi[:, k, :],
                                             start=False, stop=True, skip_group_check=True)
                    last.then_inc(h2_summed, 1)

            def aggregate(n, u):
                pe.wait_ge(h2_ready, (n + u) * 2 + 4)
                pe.wait_ge(hot_b_ready, n + u + 1)
                pe.wait_ge(agg_added, n + u + 1)
                bank = psA[u % 2]
                for t in range(GT):
                    for k in range(2):
                        pe.matmul(bank[:, k, :], h2[:, u % 2, t, k * P:(k + 1) * P], hot_e[:, u, t, :],
                                  start=(t == 0 and k == 0), stop=True, skip_group_check=True)
                    last = pe.matmul(bank[:, 2, :], ones[:, :], hot_b[:, u, t, :], start=False, stop=True, skip_group_check=True)
                last.then_inc(agg_summed, 1)

            def body(n, i, last):
                for u in range(GUN):
                    hidden2(n, u)
                    if not (last and u == GUN - 1):
                        hidden1(n, u + 1)
                    aggregate(n, u)

            def end(p):
                pe.wait_ge(tables_next, p + 1)
            sweeps(pe, lambda n: hidden1(n, 0), body, end)

        @block.scalar
        def _(act):
            act.sem_inc(h2_summed, 4)

            def indices(i, u):
                act.activation(idx[:, u, :], T.src_idx[:, bass.ds((i + u) * GT, GT)], ACT.Copy).then_inc(idx_ready, 1)

            def high(n, u):
                act.wait_ge(h2_summed, (n + u) * 2 + 2)
                for k in range(2):
                    act.wait_ge(h1_summed, (n + u) * 2 + 2 * GUN + 1 + k)
                    act.activation(h1_hi[:, u % 2, k, :], ps1[u % 2][k][:, :], ACT.Relu).then_inc(hi_ready, 1)

            def counts(n, u):
                act.wait_ge(hot_ready, n + u + 1)
                act.activation(hot_b[:, u, :, :], hot_e[:, u, :, :], ACT.Copy).then_inc(hot_b_ready, 1)

            def first(n):
                for u in range(GUN):
                    act.activation(idx[:, u, :], T.src_idx[:, u * GT:(u + 1) * GT], ACT.Copy).then_inc(idx_ready, 1)

            def body(n, i, last):
                for u in range(GUN):
                    high(n, u)
                    if not last:
                        indices(i + GUN, u)
                    counts(n, u)

            def end(p):
                act.wait_ge(tables_next, p + 1)
            sweeps(act, first, body, end)

        @block.vector
        def _(dve):
            dve.memset(T.agg[:, :, :], 0.0).then_inc(setup_done, 1)
            dve.wait_ge(loaded, 48)
            dve.wait_ge(setup_done, 3)
            dve.tensor_copy(w_hi[:, :, :], w[:, :, :]).then_inc(split_done, 1)
            dve.tensor_scalar(nb2[:, :, :], nb2[:, :, :], -1.0, None, ALU.mult).then_inc(split_done, 1)
            dve.tensor_scalar(third[:, :], third_i[:, :], 21846.0, None, ALU.mult).then_inc(setup_done, 1)
            dve.wait_ge(split_done, 2)
            dve.tensor_tensor(w_lo[:, :, :], w[:, :, :], w_hi[:, :, :].bitcast(fp32), ALU.subtract).then_inc(split_done, 1)
            dve.wait_ge(setup_done, 4)
            dve.tensor_copy(third_i[:, :], third[:, :]).then_inc(setup_done, 1)
            dve.wait_ge(setup_done, 5)
            dve.tensor_single_scalar(third_i[:, :], third_i[:, :], 16, ALU.logical_shift_right).then_inc(setup_done, 1)
            dve.wait_ge(setup_done, 6)
            dve.tensor_copy(third[:, :], third_i[:, :]).then_inc(setup_done, 1)
            dve.wait_ge(setup_done, 7)
            dve.sem_inc(lo_ready, 4)
            dve.sem_inc(h2_ready, 2)
            dve.sem_inc(agg_added, 2)
            regs = [dve.alloc_register(f"dve_base{u}") for u in range(GUN)]

            def one_hots(n, i, u):
                s = u % GUN
                dve.wait_ge(dst_in[s], (n if u < GUN else n + GUN) * 4 + 16)
                dve.tensor_scalar(hot_t[0:GWM, s, :], dstb[0:GWM, s, :], T.neg_base[0:GWM, bass.ds(i + u, 1)],
                                  third[0:GWM, 0:1], ALU.add, ALU.is_equal)
                dve.tensor_tensor(hot_e[:, s, :, :], T.iota_n[:, 0:GW].rearrange("p (o w) -> p o w", o=1).broadcast_to([P, GT, GW]),
                                  T.edge_keys[:, 3, bass.ds((i + u) * GT, GT)].rearrange("p (t o) -> p t o", o=1).broadcast_to([P, GT, GW]),
                                  ALU.is_equal).then_inc(hot_ready, 1)

            def low(n, u):
                for k in range(2):
                    dve.wait_ge(hi_ready, (n + u) * 2 + 1 + k)
                    dve.scalar_tensor_tensor(h1_lo[:, u % 2, k, :], ps1[u % 2][k][:, :], 0.0, h1_hi[:, u % 2, k, :].bitcast(fp32),
                                             ALU.max, ALU.subtract).then_inc(lo_ready, 1)

            def first(n):
                one_hots(n, 0, 0)
                one_hots(n, 0, 1)
                low(n, 0)

            def body(n, i, last):
                dve.reg_load(regs, T.base_i[0:1, bass.ds(i, GUN)])
                for u in range(GUN):
                    at = T.agg[:, :, bass.ds(dve.snap(regs[u], min_val=0, max_val=N + 1), GW)]
                    dve.lower_ap(at)
                    if not (last and u >= GUN - 2):
                        one_hots(n, i, u + 2)
                    for q in range(2):
                        dve.wait_ge(h2_summed, (n + u) * 2 + q + 5)
                        dve.tensor_tensor(h2[:, u % 2, 2 * q:2 * q + 2, :], ps2[q][:, :, :], nb2[:, :, :], ALU.max).then_inc(h2_ready, 1)
                    if not (last and u == GUN - 1):
                        low(n, u + 1)
                    dve.wait_ge(agg_summed, n + u + 1)
                    dve.wait_ge(agg_added, n + u + 2)
                    dve.tensor_tensor(at, psA[u % 2][:, :, :], at, ALU.add).then_inc(agg_added, 1)

            def end(p):
                dve.wait_ge(agg_added, (p + 1) * GROUPS + 2)
                dve.tensor_scalar(T.edge_keys[:, 3, 0:TILES], T.edge_keys[:, 3, 0:TILES], -float(GW), None, ALU.add).then_inc(sweep_done, 1)
                dve.tensor_scalar(T.neg_base[:, :], T.neg_base[:, :], -float(GW), None, ALU.add).then_inc(sweep_done, 1)
                dve.tensor_scalar(T.base_row[:, :], T.base_row[:, :], float(GW), float(N + 1), ALU.add, ALU.min).then_inc(sweep_done, 1)
                dve.wait_ge(sweep_done, p * 4 + 3)
                dve.tensor_copy(T.base_i[:, :], T.base_row[:, :]).then_inc(sweep_done, 1)
                dve.wait_ge(sweep_done, p * 4 + 4)
                dve.sem_inc(tables_next, 1)
            sweeps(dve, first, body, end)


def update_nodes(nc, T, bm2, wm3, bm3, wn1, bn1, wn2, bn2, out):
    with ExitStack() as ctx:
        def sb(name, shape, dt):
            return ctx.enter_context(nc.sbuf_tensor(name, shape, dt))

        def sem(name):
            return ctx.enter_context(nc.semaphore(name))
        b2 = sb("b2_u", [P, 2], fp32)
        w3 = sb("w3_u", [P, 2, D], fp32)
        b3 = sb("b3_u", [D, 1], fp32)
        wa = sb("wa_u", [P, 2, H], fp32)
        ba = sb("ba_u", [P, 2], fp32)
        wb = sb("wb_u", [P, 2, D], fp32)
        bb = sb("bb_u", [P, D], fp32)
        inv = sb("inv", [P, N], fp32)
        has = sb("has", [P, N], fp32)
        msg = sb("msg", [D, N], fp32)
        u1 = sb("u1", [P, 2, N], fp32)
        psM = [ctx.enter_context(nc.psum_tensor(f"psM{i}", [P, 512], fp32)) for i in range(2)]
        psU = [ctx.enter_context(nc.psum_tensor(f"psU{i}", [P, 512], fp32)) for i in range(4)]
        psV = [ctx.enter_context(nc.psum_tensor(f"psV{i}", [P, 512], fp32)) for i in range(2)]
        loaded = sem("loaded_u")
        mean_ready = sem("mean_ready")
        msg_done = sem("msg_done")
        msg_ready = sem("msg_ready")
        u1_done = sem("u1_done")
        u1_ready = sem("u1_ready")
        u2_done = sem("u2_done")
        u2_read = sem("u2_read")
        moments_ready = sem("moments_u")
        std_ready = sem("std_u")
        rows_ready = sem("rows_ready")
        out_done = sem("out_done")
        chain = Counted(ctx, nc, "chain_u")
        block = ctx.enter_context(nc.Block())
        cuts = [(a, min(N, a + 512)) for a in range(0, N, 512)]

        @block.sync
        def _(sp):
            with nc.allow_non_contiguous_dma(reason="biases to partitions"):
                sp.dma_start(b2[:, :], bm2.rearrange("(c f) -> f c", c=2), allow_slow_non_contiguous=True).then_inc(loaded, 16)
                sp.dma_start(b3[:, :], bm3.rearrange("(f o) -> f o", o=1), allow_slow_non_contiguous=True).then_inc(loaded, 16)
                sp.dma_start(ba[:, :], bn1.rearrange("(c f) -> f c", c=2), allow_slow_non_contiguous=True).then_inc(loaded, 16)
            sp.dma_start(w3[:, :, :], wm3.rearrange("(c f) h -> f c h", c=2)).then_inc(loaded, 16)
            sp.dma_start(wa[:, :, :], wn1.rearrange("(c f) h -> f c h", c=2)).then_inc(loaded, 16)
            sp.dma_start(wb[:, :, :], wn2.rearrange("(c f) h -> f c h", c=2)).then_inc(loaded, 16)
            sp.dma_start(bb[:, :], bn2.rearrange("(o h) -> o h", o=1).broadcast_to([P, D])).then_inc(loaded, 16)
            sp.wait_ge(rows_ready, 1)
            sp.dma_start(out.rearrange("(b n) f -> n b f", b=NBLK), T.x1[:, :, :]).then_inc(out_done, 16)
            sp.wait_ge(out_done, 16)

        @block.tensor
        def _(pe):
            pe.wait_ge(loaded, 112)
            pe.wait_ge(mean_ready, 1)
            for c, (a, z) in enumerate(cuts):
                if c >= 2:
                    pe.wait_ge(msg_ready, c - 1)
                for k in range(2):
                    last = pe.matmul(psM[c % 2][:, 0:z - a], w3[:, k, :], T.agg[:, k, a:z], start=(k == 0), stop=(k == 1))
                last.then_inc(msg_done, 1)
            for c, (a, z) in enumerate(cuts):
                pe.wait_ge(msg_ready, c + 1)
                for m in range(2):
                    n = 2 * c + m
                    if n >= 4:
                        pe.wait_ge(u1_ready, n - 3)
                    pe.matmul(psU[n % 4][:, 0:z - a], wa[:, 0, m * P:(m + 1) * P], T.x1T[:, a:z], start=True, stop=False)
                    pe.matmul(psU[n % 4][:, 0:z - a], wa[:, 1, m * P:(m + 1) * P], msg[:, a:z], start=False, stop=True).then_inc(u1_done, 1)
            pe.wait_ge(u1_ready, 2 * len(cuts))
            for b in range(NBLK):
                if b >= 2:
                    pe.wait_ge(u2_read, b - 1)
                for k in range(2):
                    last = pe.matmul(psV[b % 2][0:BLK, 0:D], u1[:, k, b * BLK:(b + 1) * BLK], wb[:, k, :], start=(k == 0), stop=(k == 1))
                last.then_inc(u2_done, 1)

        @block.scalar
        def _(act):
            act.wait_ge(loaded, 112)
            for c, (a, z) in enumerate(cuts):
                for m in range(2):
                    n = 2 * c + m
                    act.wait_ge(u1_done, n + 1)
                    act.activation(u1[:, m, a:z], psU[n % 4][:, 0:z - a], ACT.Relu, bias=ba[:, m:m + 1]).then_inc(u1_ready, 1)
            act.wait_ge(moments_ready, 1)
            act.activation(T.std[:, :], T.den[:, :], ACT.Sqrt).then_inc(std_ready, 1)

        @block.vector
        def _(dve):
            def step(ins):
                dve.wait_ge(chain.sem, chain.inc(ins))
            dve.tensor_scalar(has[:, :], T.agg[:, 2, 0:N], 1.0, None, ALU.min)
            step(dve.tensor_scalar(inv[:, :], T.agg[:, 2, 0:N], 1.0, None, ALU.max))
            step(dve.reciprocal(inv[:, :], inv[:, :]))
            dve.wait_ge(loaded, 112)
            for k in range(2):
                step(dve.tensor_tensor(T.agg[:, k, 0:N], T.agg[:, k, 0:N], inv[:, :], ALU.mult))
                step(dve.scalar_tensor_tensor(T.agg[:, k, 0:N], has[:, :], b2[:, k:k + 1], T.agg[:, k, 0:N], ALU.mult, ALU.add))
            dve.sem_inc(mean_ready, 1)
            for c, (a, z) in enumerate(cuts):
                dve.wait_ge(msg_done, c + 1)
                dve.scalar_tensor_tensor(msg[:, a:z], has[:, a:z], b3[:, 0:1], psM[c % 2][:, 0:z - a], ALU.mult, ALU.add).then_inc(msg_ready, 1)
            step(dve.tensor_scalar(T.x1[:, :, :], T.x1[:, :, :], 2.0, None, ALU.mult))
            step(dve.tensor_tensor(T.x1[:, :, :], T.x1[:, :, :],
                                   bb[0:BLK, :].rearrange("p (o f) -> p o f", o=1).broadcast_to([BLK, NBLK, D]), ALU.add))
            for b in range(NBLK):
                dve.wait_ge(u2_done, b + 1)
                dve.tensor_tensor(T.x1[:, b, :], T.x1[:, b, :], psV[b % 2][0:BLK, 0:D], ALU.add).then_inc(u2_read, 1)
            dve.wait_ge(u2_read, NBLK)
            layernorm(dve, step, T, T.x1, moments_ready, std_ready)
            dve.sem_inc(rows_ready, 1)


class Tables:
    pass


def gnn_kernel(nc, x, src, dst, w0, att, wm1, bm1, wm2, bm2, wm3, bm3, wn1, bn1, wn2, bn2, out):
    def dram(name, shape, dt):
        return nc.dram_tensor(name, shape, dt, kind="Internal").ap()
    scr_tile = dram("scr_tile", (2, TILES), fp32)
    scr_dst = dram("scr_dst", (TILES * P,), i16)
    scr_win = dram("scr_win", (2 * NWIN,), i32)
    scr_pass = dram("scr_pass", (2, GROUPS), fp32)
    table_a = dram("table_a", (N, H), fp32)
    table_b = dram("table_b", (NPAD, 3 * H), bf16)
    with ExitStack() as ctx:
        def sb(name, shape, dt):
            return ctx.enter_context(nc.sbuf_tensor(name, shape, dt))
        T = Tables()
        T.edge_keys = sb("edge_keys", [P, 4, TILES + TPT - 1], fp32)
        T.src_idx = sb("src_idx", [P, TILES], i32)
        T.iota_m = sb("iota_m", [P, P], i16)
        T.iota_n = sb("iota_n", [P, SW + 1], i16)
        T.win_key = sb("win_key", [P, NWIN], fp32)
        T.win_tab = sb("win_tab", [1, 2 * NWIN], i32)
        T.base_row = sb("base_row", [1, GROUPS], fp32)
        T.base_i = sb("base_i", [1, GROUPS], i32)
        T.base_all = sb("base_all", [P, GROUPS], fp32)
        T.neg_base = sb("neg_base", [P, GROUPS], fp32)
        T.passes_f = sb("passes_f", [1, 1], fp32)
        T.passes_i = sb("passes_i", [1, 1], i32)
        T.ident = sb("ident", [P, P], fp32)
        T.x1 = sb("x1", [BLK, NBLK, D], fp32)
        T.den = sb("den", [BLK, NBLK], fp32)
        T.std = sb("std", [BLK, NBLK], fp32)
        T.stats = sb("stats", [BLK, NBLK, 6], fp32)
        T.mv = sb("mv", [BLK, NBLK, 2], fp32)
        index_tables(nc, src, dst, T, scr_tile, scr_dst, scr_win, scr_pass)
        attention(nc, T, x, w0, att)
        T.x1T = sb("x1T", [D, N], fp32)
        T.agg = sb("agg", [P, 3, NPAD], fp32)
        node_tables(nc, T, wm1, bm1, table_a, table_b)
        messages(nc, T, wm2, bm2, table_a, table_b, scr_dst)
        update_nodes(nc, T, bm2, wm3, bm3, wn1, bn1, wn2, bn2, out)


_INS = ["x", "src", "dst", "L0_gnn_kernel", "L0_gnn_kernel_attention", "L1_gnn_Wm1", "L1_gnn_bm1", "L1_gnn_Wm2",
        "L1_gnn_bm2", "L1_gnn_Wm3", "L1_gnn_bm3", "L1_gnn_Wn1", "L1_gnn_bn1", "L1_gnn_Wn2", "L1_gnn_bn2"]


def kernel(**inputs):
    import numpy as np
    import concourse.bacc as bacc
    from concourse import mybir as mb
    from concourse.bass_utils import run_bass_kernel_spmd as run

    nc = bacc.Bacc("TRN2", target_bir_lowering=False, num_devices=1)
    arrays, args = {}, []
    for name in _INS:
        a = np.ascontiguousarray(inputs[name])
        arrays[f"in_{name}"] = a
        args.append(nc.dram_tensor(f"in_{name}", a.shape, mb.dt.from_np(a.dtype), kind="ExternalInput").ap())
    out = nc.dram_tensor("out_0", (N, D), mb.dt.float32, kind="ExternalOutput").ap()
    gnn_kernel(nc, *args, out)
    return run(nc, [arrays], core_ids=[0]).results[0]["out_0"]
```

```python
import concourse.bass as bass
from concourse import mybir
from contextlib import ExitStack

P = 128
N = 3125
D = 128
H = 256
E = 100000
NBLK, BLK = 25, 125
TILES = 784
QROWS, QTILES = 112, 7
REAL_ROWS = E // (QTILES * P)
REST = E - REAL_ROWS * QTILES * P
PAD_DST = N

WIN = 25
SBLK, SW = 5, 625
WM = WIN * SBLK
NWIN = N // WIN
WPB = BLK // WIN
TPT = 6
HG = 3

PR = 4
BPT = 4
TURNS_A = (NBLK - 1) // BPT
BANK_BLKS = 3
CH = -(-NBLK // BANK_BLKS)
CUT_CH = 5
PROB_CUT = CUT_CH * BANK_BLKS * BLK
BANKS_AT = (0, 0, 0, 1, 1, 1, 1, 1, 2, 2)
SCORE_CUTS = ((0, 1564), (1564, N))
LEAKY_AT = ((), (0,), (1,), (), ())
CLIP_AT = ((), (), (0,), (1,), ())
EXP_AT = 3

GT = 4
GE = GT * P
GROUPS = TILES // GT
GW = 42
GWM = 3 * GW
GUN = 4
NPAD = N + 1 + GW
STEPS = (N + GW) // GW + 1

EPS_ALPHA = 1e-07
EPS_LN = 1e-05
SLOPE = 0.2
CLIP = 2.0

fp32 = mybir.dt.float32
f32r = mybir.dt.float32r
bf16 = mybir.dt.bfloat16
i32 = mybir.dt.int32
i16 = mybir.dt.int16
ALU = mybir.AluOpType
ACT = mybir.ActivationFunctionType
AX = mybir.AxisListType


def bounded(value, low, high):
    return value.with_bounds(min_val=low, max_val=high)


class Counted:

    def __init__(self, ctx, nc, name):
        self.sem = ctx.enter_context(nc.semaphore(name))
        self.n = 0

    def inc(self, instruction, by=1):
        instruction.then_inc(self.sem, by)
        self.n += by
        return self.n


def index_tables(nc, src, dst, x, w0, att, T, scr_tile, scr_dst, scr_win, scr_pass):
    with ExitStack() as ctx:
        def sb(name, shape, dt):
            return ctx.enter_context(nc.sbuf_tensor(name, shape, dt))
        EL = QTILES * P
        e_src = sb("e_src", [QROWS, EL], i32)
        e_dst = sb("e_dst", [QROWS, EL], i32)
        e_blk = sb("e_blk", [QROWS, EL], i32)
        keys = sb("keys", [QROWS, 4, EL], fp32)
        blkf = sb("blkf", [QROWS, EL], fp32)
        dst16 = sb("dst16", [QROWS, EL], i16)
        onesf = sb("onesf1", [P, P], fp32)
        mm = sb("mm", [QROWS, 2, QTILES], fp32)
        mmb = sb("mmb", [P, 2, TILES], fp32)
        up1 = sb("up1", [P, TILES], fp32)
        down = sb("down", [P, TILES], fp32)
        edge = sb("edge", [P, 2], fp32)
        junk = sb("junk", [P, TILES], fp32)
        best = sb("best", [P, 2], fp32)
        wtab = sb("wtab", [P, 2], fp32)
        wtabi = sb("wtabi", [P, 2], i32)
        gmm = sb("gmm", [GROUPS // 2, 2, 2, GT], fp32)
        gbt = sb("gbt", [GROUPS // 2, 2, 2], fp32)
        gspan = sb("gspan", [GROUPS // 2, 2], fp32)
        steps = sb("steps", [P, STEPS], fp32)
        gjunk = sb("gjunk", [P, STEPS], fp32)
        gpass = sb("gpass", [GROUPS // 2, 2], fp32)
        prow = sb("prow", [1, GROUPS], fp32)
        w_sb = sb("w_sb", [D, D], fp32)
        wT = sb("wT", [D, D], fp32)
        att_sb = sb("att_sb", [D, 2], fp32)
        wk = sb("wk", [D, D + 2], fp32)
        a1b = sb("a1b", [D, P], fp32)
        xT = sb("xT", [D, N], fp32)
        KB = 3
        psK = [ctx.enter_context(nc.psum_tensor(f"psK{i}", [P, 512], fp32)) for i in range(KB)]
        psT = [ctx.enter_context(nc.psum_tensor(f"psT{i}", [P, 512], fp32)) for i in range(4)]
        keys_read = ctx.enter_context(nc.semaphore("keys_read"))
        loaded = ctx.enter_context(nc.semaphore("loaded"))
        k_turned = ctx.enter_context(nc.semaphore("k_turned"))
        k_copied = ctx.enter_context(nc.semaphore("k_copied"))
        ka_done = ctx.enter_context(nc.semaphore("ka_done"))
        wk_ready = ctx.enter_context(nc.semaphore("wk_ready"))
        x_turned = ctx.enter_context(nc.semaphore("x_turned"))
        x_copied = ctx.enter_context(nc.semaphore("x_copied"))
        h_done = ctx.enter_context(nc.semaphore("h_done"))
        h_copied = ctx.enter_context(nc.semaphore("h_copied"))
        s1_done = ctx.enter_context(nc.semaphore("s1_done"))
        s1_copied = ctx.enter_context(nc.semaphore("s1_copied"))
        iota_done = ctx.enter_context(nc.semaphore("iota_done"))
        edges_in = ctx.enter_context(nc.semaphore("edges_in"))
        padded = ctx.enter_context(nc.semaphore("padded"))
        keys_ready = ctx.enter_context(nc.semaphore("keys_ready"))
        keys_turned = ctx.enter_context(nc.semaphore("keys_turned"))
        tile_range = ctx.enter_context(nc.semaphore("tile_range"))
        range_out = ctx.enter_context(nc.semaphore("range_out"))
        range_back = ctx.enter_context(nc.semaphore("range_back"))
        dst16_ready = ctx.enter_context(nc.semaphore("dst16_ready"))
        dst16_out = ctx.enter_context(nc.semaphore("dst16_out"))
        windows_ready = ctx.enter_context(nc.semaphore("windows_ready"))
        groups_ready = ctx.enter_context(nc.semaphore("groups_ready"))
        tables_out = ctx.enter_context(nc.semaphore("tables_out"))
        tables_back = ctx.enter_context(nc.semaphore("tables_back"))
        passes_done = ctx.enter_context(nc.semaphore("passes_done"))
        step_done = Counted(ctx, nc, "step_done")
        block = ctx.enter_context(nc.Block())

        @block.gpsimd
        def _(pool):
            pool.memset(e_src[:, :], 0).then_inc(padded, 1)
            pool.memset(e_dst[:, :], PAD_DST).then_inc(padded, 1)
            pool.memset(onesf[:, :], 1.0).then_inc(iota_done, 1)
            pool.wait_ge(iota_done, 1)
            pool.affine_select(out=T.ident[:, :], in_=onesf[:, :], compare_op=ALU.is_equal, fill=0.0, base=0,
                               pattern=[[-1, P]], channel_multiplier=1).then_inc(iota_done, 1)
            for out, pattern, base, mult in ((up1[:, :], [[1, TILES]], 1, 0), (down[:, :], [[-1, TILES]], TILES, 0),
                                             (edge[:, :], [[WIN, 2]], 0, WIN),
                                             (steps[:, :], [[GW, STEPS]], 0, 0),
                                             (T.iota_n[:, :], [[1, SW + 1]], 0, 0),
                                             (T.iota_m[:, :], [[1, NWIN * WM + 1]], 0, 0)):
                pool.iota(out, pattern, base=base, channel_multiplier=mult,
                          allow_small_or_imprecise_dtypes=True).then_inc(iota_done, 1)

        @block.sync
        def _(sp):
            sp.wait_ge(padded, 2)
            for tile, lst in ((e_src, src), (e_dst, dst)):
                sp.dma_start(tile[0:REAL_ROWS, :], lst[0:REAL_ROWS * EL].rearrange("(q n) -> q n", n=EL)).then_inc(edges_in, 16)
                sp.dma_start(tile[REAL_ROWS:REAL_ROWS + 1, 0:REST], lst[REAL_ROWS * EL:E].rearrange("(q n) -> q n", q=1)).then_inc(edges_in, 16)
            sp.dma_start(w_sb[:, :], w0).then_inc(loaded, 16)
            sp.dma_start(att_sb[:, :], att.rearrange("(c f) o -> f (c o)", c=2), allow_slow_non_contiguous=True).then_inc(loaded, 16)
            sp.dma_start(T.x1[:, :, :], x.rearrange("(b n) f -> n b f", b=NBLK)).then_inc(loaded, 16)
            sp.wait_ge(tile_range, 1)
            for c in range(2):
                sp.dma_start(scr_tile[c, :].rearrange("(q k) -> q k", k=QTILES), mm[:, c, :]).then_inc(range_out, 16)
            sp.wait_ge(range_out, 32)
            sp.dma_start(mmb[:, :, :], scr_tile.rearrange("c (o t) -> o c t", o=1).broadcast_to([P, 2, TILES])).then_inc(range_back, 16)
            for c in range(2):
                sp.dma_start(gmm[:, c, :, :], scr_tile[c, :].rearrange("(q r k) -> q r k", r=2, k=GT)).then_inc(range_back, 16)
            sp.wait_ge(dst16_ready, 1)
            sp.dma_start(scr_dst.rearrange("(q n) -> q n", n=EL), dst16[:, :]).then_inc(dst16_out, 16)
            sp.wait_ge(windows_ready, 1)
            with nc.allow_non_contiguous_dma(reason="a few hundred words"):
                sp.dma_start(scr_win.rearrange("(q c) -> q c", c=2), wtabi[0:NWIN, :], allow_slow_non_contiguous=True).then_inc(tables_out, 16)
            sp.wait_ge(groups_ready, 1)
            sp.dma_start(scr_pass[0, :].rearrange("(q r) -> q r", r=2), gpass[:, :]).then_inc(tables_out, 16)
            sp.dma_start(scr_pass[1, :].rearrange("(q r) -> q r", r=2), gbt[:, 0, :]).then_inc(tables_out, 16)
            sp.wait_ge(tables_out, 48)
            sp.dma_start(T.win_tab[0:1, :], scr_win.rearrange("(o n) -> o n", o=1)).then_inc(tables_back, 16)
            sp.dma_start(prow[0:1, :], scr_pass[0:1, :]).then_inc(tables_back, 16)
            sp.dma_start(T.base_row[0:1, :], scr_pass[1:2, :]).then_inc(tables_back, 16)
            sp.dma_start(T.base_all[:, :], scr_pass[1:2, :].broadcast_to([P, GROUPS])).then_inc(tables_back, 16)
            sp.wait_ge(dst16_out, 16)

        @block.vector
        def _(dve):
            def step(ins):
                dve.wait_ge(step_done.sem, step_done.inc(ins))
            dve.wait_ge(edges_in, 64)
            dve.tensor_copy(keys[:, 3, :], e_dst[:, :]).then_inc(keys_ready, 1)
            step(dve.tensor_copy(keys[:, 2, :], e_src[:, :]))
            step(dve.tensor_scalar(e_blk[:, :], keys[:, 2, :], 1678.0, None, ALU.mult))
            step(dve.tensor_single_scalar(e_blk[:, :], e_blk[:, :], 20, ALU.logical_shift_right))
            step(dve.tensor_copy(blkf[:, :], e_blk[:, :]))
            dve.scalar_tensor_tensor(keys[:, 1, :], blkf[:, :], -float(SW), keys[:, 2, :], ALU.mult, ALU.add).then_inc(keys_ready, 1)
            dve.wait_ge(keys_ready, 2)
            dve.scalar_tensor_tensor(keys[:, 0, :], keys[:, 3, :], float(SBLK), blkf[:, :], ALU.mult, ALU.add).then_inc(keys_ready, 1)
            by_tile = keys[:, 3, :].rearrange("q (k p) -> q k p", p=P)
            dve.tensor_reduce(mm[:, 0, :], by_tile, AX.X, ALU.min)
            step(dve.tensor_reduce(mm[:, 1, :], by_tile, AX.X, ALU.max))
            dve.tensor_copy(dst16[:, :], keys[:, 3, :]).then_inc(dst16_ready, 1)
            dve.sem_inc(tile_range, 1)
            for k in range(QTILES):
                dve.wait_ge(keys_turned, k + 1)
                dve.tensor_copy(T.edge_keys[:, :, 0:TILES].rearrange("p c (q k) -> p c q k", k=QTILES)[:, :, :, k],
                                psK[k % KB][:, 0:4 * QROWS].rearrange("p (c q) -> p c q", c=4)).then_inc(keys_read, 1)
            dve.wait_ge(k_turned, 1)
            dve.tensor_copy(wT[:, :], psT[0][:, 0:P]).then_inc(k_copied, 1)
            dve.tensor_copy(wk[:, 0:D], w_sb[:, :]).then_inc(wk_ready, 1)
            dve.wait_ge(ka_done, 1)
            dve.tensor_copy(wk[:, D:D + 2], psT[0][:, 256:258]).then_inc(wk_ready, 1)
            dve.wait_ge(wk_ready, 2)
            dve.tensor_scalar(a1b[:, :], onesf[:, :], wk[:, D:D + 1], None, ALU.mult).then_inc(wk_ready, 1)
            step(dve.memset(T.edge_keys[:, :, TILES:TILES + TPT - 1], -1.0))
            step(dve.tensor_copy(T.row_keys[:, :], T.edge_keys[:, 0, :]))
            step(dve.tensor_copy(T.src_idx[:, :], T.edge_keys[:, 2, 0:TILES]))
            dve.wait_ge(iota_done, 7)
            dve.wait_ge(range_back, 48)
            step(dve.scalar_tensor_tensor(junk[:, :], mmb[:, 0, :], edge[:, 1:2], up1[:, :], ALU.is_lt, ALU.mult))
            step(dve.tensor_reduce(best[:, 1:2], junk[:, :], AX.X, ALU.max))
            step(dve.scalar_tensor_tensor(junk[:, :], mmb[:, 1, :], edge[:, 0:1], down[:, :], ALU.is_ge, ALU.mult))
            step(dve.tensor_reduce(best[:, 0:1], junk[:, :], AX.X, ALU.max))
            step(dve.tensor_scalar(wtab[:, 0:1], best[:, 0:1], -1.0, float(TILES), ALU.mult, ALU.add))
            step(dve.tensor_scalar(wtab[:, 0:1], wtab[:, 0:1], float(TILES - 1), None, ALU.min))
            step(dve.tensor_scalar(wtab[:, 1:2], wtab[:, 0:1], 1.0, None, ALU.add))
            step(dve.tensor_tensor(wtab[:, 1:2], best[:, 1:2], wtab[:, 1:2], ALU.max))
            step(dve.tensor_copy(wtabi[:, :], wtab[:, :]))
            dve.sem_inc(windows_ready, 1)
            step(dve.tensor_reduce(gbt[:, 0, :], gmm[:, 0, :, :], AX.X, ALU.min))
            step(dve.tensor_reduce(gbt[:, 1, :], gmm[:, 1, :, :], AX.X, ALU.max))
            step(dve.tensor_tensor(gspan[:, :], gbt[:, 1, :], gbt[:, 0, :], ALU.subtract))
            for r in range(2):
                step(dve.tensor_scalar(gjunk[0:GROUPS // 2, :], steps[0:GROUPS // 2, :], gspan[:, r:r + 1], 0.0, ALU.is_le, ALU.add,
                                       accum_out=gpass[:, r:r + 1]))
            dve.sem_inc(groups_ready, 1)
            dve.wait_ge(tables_back, 64)
            step(dve.tensor_copy(T.base_i[0:1, :], T.base_row[0:1, :]))
            step(dve.tensor_reduce(T.passes_f[0:1, :], prow[0:1, :], AX.X, ALU.max))
            step(dve.tensor_copy(T.passes_i[0:1, :], T.passes_f[0:1, :]))
            step(dve.tensor_tensor(T.edge_keys[:, 3, 0:TILES].rearrange("p (g k) -> p g k", k=GT),
                                   T.edge_keys[:, 3, 0:TILES].rearrange("p (g k) -> p g k", k=GT),
                                   T.base_all[:, :].rearrange("p (g o) -> p g o", o=1).broadcast_to([P, GROUPS, GT]), ALU.subtract))
            step(dve.tensor_scalar(T.neg_base[:, :], T.base_all[:, :], -1.0, None, ALU.mult))

        @block.tensor
        def _(pe):
            pe.wait_ge(iota_done, 2)
            pe.wait_ge(keys_ready, 3)
            for k in range(QTILES):
                if k >= KB:
                    pe.wait_ge(keys_read, k - KB + 1)
                for c in range(4):
                    last = pe.transpose(psK[k % KB][:, c * QROWS:(c + 1) * QROWS], keys[:, c, k * P:(k + 1) * P], T.ident[0:QROWS, 0:QROWS])
                last.then_inc(keys_turned, 1)
            pe.wait_ge(loaded, 48)
            pe.transpose(psT[0][:, 0:P], w_sb[:, :], T.ident[:, :]).then_inc(k_turned, 1)
            for b in range(NBLK):
                if b >= 3:
                    pe.wait_ge(x_copied, b - 2)
                pe.transpose(psT[1 + b % 3][:, 0:BLK], T.x1[:, b, :], T.ident[0:BLK, 0:BLK]).then_inc(x_turned, 1)
                if b == 3:
                    pe.wait_ge(k_copied, 1)
                    pe.matmul(psT[0][:, 256:258], wT[:, :], att_sb[:, :], start=True, stop=True).then_inc(ka_done, 1)
            pe.wait_ge(wk_ready, 3)
            pe.wait_ge(x_copied, NBLK)
            for b in range(NBLK):
                if b >= 4:
                    pe.wait_ge(h_copied, b - 3)
                pe.matmul(psT[b % 4][0:BLK, 0:D + 2], xT[:, b * BLK:(b + 1) * BLK], wk[:, :], start=True, stop=True).then_inc(h_done, 1)
            pe.wait_ge(h_copied, NBLK)
            for c in range(7):
                n0, n1 = c * 512, min(N, (c + 1) * 512)
                if c >= 4:
                    pe.wait_ge(s1_copied, c - 3)
                pe.matmul(psT[c % 4][:, 0:n1 - n0], a1b[:, :], xT[:, n0:n1], start=True, stop=True).then_inc(s1_done, 1)

        @block.scalar
        def _(act):
            for b in range(NBLK):
                act.wait_ge(x_turned, b + 1)
                act.activation(xT[:, b * BLK:(b + 1) * BLK], psT[1 + b % 3][:, 0:BLK], ACT.Copy).then_inc(x_copied, 1)
            for b in range(NBLK):
                act.wait_ge(h_done, b + 1)
                act.activation(T.hx[:, b + 1, :], psT[b % 4][0:BLK, 0:D + 2], ACT.Copy).then_inc(h_copied, 1)
            for c in range(7):
                n0, n1 = c * 512, min(N, (c + 1) * 512)
                act.wait_ge(s1_done, c + 1)
                act.activation(T.s1r[:, n0:n1], psT[c % 4][:, 0:n1 - n0], ACT.Copy).then_inc(s1_copied, 1)
            act.activation(T.s2s[:, :], T.hx[:, 1:NBLK + 1, D + 1], ACT.Copy, scale=SLOPE)
            act.activation(T.hx[:, :, D:D + 1], onesf[0:BLK, 0:NBLK + 1].rearrange("p (b o) -> p b o", o=1), ACT.Copy)


def layernorm(dve, step, T, rows, moments_ready, std_ready, cuts, cut_ready):
    for b in range(NBLK):
        last = dve.bn_aggr(T.mv[:, b, :], T.stats[:, b, :])
    step(last)
    step(dve.tensor_scalar(T.den[:, :], T.mv[:, :, 1], EPS_LN, None, ALU.add))
    dve.sem_inc(moments_ready, 1)
    dve.wait_ge(std_ready, 1)
    step(dve.reciprocal(T.den[:, :], T.std[:, :]))
    for a, z in cuts:
        for b in range(a // BLK, z // BLK):
            last = dve.tensor_scalar(rows[:, b, :], rows[:, b, :], T.mv[:, b, 0:1], T.den[:, b:b + 1], ALU.subtract, ALU.mult)
        last.then_inc(cut_ready, 1)


def attention(nc, T):
    with ExitStack() as ctx:
        def sb(name, shape, dt):
            return ctx.enter_context(nc.sbuf_tensor(name, shape, dt))

        def sem(name):
            return ctx.enter_context(nc.semaphore(name))
        W2 = D + 1
        SWE, WME = SW + 1, WM + 1
        HALF = SWE // 2
        xn = T.x1
        hx, s1r = T.hx, T.s1r
        cnt = sb("cnt", [P, 2, N], fp32)
        pr = sb("pr", [BLK, PR, N], fp32)
        acc = sb("acc", [BLK, NBLK, W2], fp32)
        hot_m = sb("hot_m", [P, TPT, WME], bf16)
        hot_n = sb("hot_n", [P, TPT, SWE], bf16)
        zeros = sb("zeros", [P, HALF], bf16)
        stage = sb("stage", [P, 2, SWE], fp32)
        psC = [ctx.enter_context(nc.psum_tensor(f"psC{i}", [P, 2, 512], fp32)) for i in range(2)]
        psO = [ctx.enter_context(nc.psum_tensor(f"psO{i}", [P, 512], fp32)) for i in range(2)]
        cleared = sem("cleared")
        zeros_ready = sem("zeros_ready")
        hot_ready = [sem(f"hot_ready{i}") for i in range(TPT)]
        hot_free = [sem(f"hot_free{i}") for i in range(TPT // HG)]
        window_summed = sem("window_summed")
        bank_read = sem("bank_read")
        stage_out = [sem(f"stage_out{i}") for i in range(2)]
        sp_order = sem("sp_order_a")
        pool_order = sem("pool_order_a")
        low_ready = sem("low_ready")
        leaky_ready = sem("leaky_ready")
        clip_ready = sem("clip_ready")
        exp_ready = sem("exp_ready")
        prob_ready = sem("prob_ready")
        chunk_done = sem("chunk_done")
        chunk_added = sem("chunk_added")
        moments_ready = sem("moments_ready")
        std_ready = sem("std_ready")
        rows_ready = sem("rows_ready_a")
        chain = Counted(ctx, nc, "chain_a")
        block = ctx.enter_context(nc.Block())

        def chunk(c):
            return list(range(c * BANK_BLKS, min(NBLK, (c + 1) * BANK_BLKS)))

        def chunks_at(v, u):
            in_pair = (v % 2) * WPB + u
            start = sum(BANKS_AT[:in_pair])
            return range(start, start + BANKS_AT[in_pair]) if v >= 0 else ()

        def blocks(eng, body):
            body(0, -1)
            with eng.Fori(0, TURNS_A, 1) as t:
                t = bounded(t, 0, TURNS_A - 1)
                for v in range(BPT):
                    body(t, v)

        def windows(eng, tag, window, tile_aps, tile):
            turn = eng.alloc_register(f"{tag}_turn")
            eng.reg_mov(turn, 1)
            regs = [eng.alloc_register(f"{tag}_win{i}") for i in range(2 * WPB)]

            def body(t, v):
                eng.reg_load(regs, T.win_tab[0:1, bass.ds(t * (BPT * WPB * 2) + (v + 1) * WPB * 2, 2 * WPB)])
                for u in range(WPB):
                    first = eng.snap(regs[2 * u], min_val=0, max_val=TILES - 1)
                    end = eng.snap(regs[2 * u + 1], min_val=1, max_val=TILES)
                    before, after = window(t, v, u)
                    before()
                    with eng.Fori(first, end, TPT) as n:
                        n = bounded(n, 0, TILES - 1)
                        now = eng.snap(turn, min_val=1, max_val=10**6)
                        aps = tile_aps(n, t, v, u)
                        for s in range(TPT):
                            tile(s, now, aps, v, u)
                        eng.reg_add(turn, turn, 1)
                    after()
            return body

        @block.sync
        def _(sp):
            for s in range(2):
                sp.sem_inc(stage_out[s], 16)

            def body(t, v):
                for u in range(WPB):
                    w = (v + 1) * WPB + u
                    if u == 0:
                        sp.wait_ge(prob_ready, (t * BPT + v + 2) * 2)
                        sp.sem_inc(sp_order, 1)
                    sp.wait_ge(bank_read, t * (BPT * WPB) + w + 3)
                    sp.sem_inc(sp_order, 1)
                    sp.dma_start(cnt[u * WIN:(u + 1) * WIN, (v + 1) % 2, :], stage[0:WM, w % 2, 0:SW]).then_inc(stage_out[w % 2], 16)
            blocks(sp, body)

        @block.gpsimd
        def _(pool):
            pool.memset(pr[:, 0, :], 0.0).then_inc(cleared, 1)
            pool.memset(hx[:, 0, :], 0.0).then_inc(cleared, 1)
            pool.memset(acc[:, :, :], 0.0).then_inc(cleared, 1)
            pool.wait_ge(cleared, 3)
            pool.sem_inc(prob_ready, 4)

            def body(t, v):
                last = (v + 2) * WPB - 1
                for s in range(2):
                    stored = (last - s) // 2 + 1
                    pool.wait_ge(stage_out[s], t * (BPT * WPB * 8) + 16 * stored + 16)
                    pool.sem_inc(pool_order, 1)
                pool.wait_ge(exp_ready, t * BPT + v + 2)
                pool.sem_inc(pool_order, 1)
                slot = pr[:, (v + 2) % PR, :]
                for cols in (slice(0, PROB_CUT), slice(PROB_CUT, N)):
                    pool.tensor_tensor(slot[:, cols], slot[:, cols], cnt[0:BLK, (v + 1) % 2, cols], ALU.mult).then_inc(prob_ready, 1)
            blocks(pool, body)

        @block.tensor
        def _(pe):
            pe.wait_ge(zeros_ready, 1)
            for s in range(TPT // HG):
                pe.sem_inc(hot_free[s], 1)
            pe.sem_inc(chunk_done, CH)

            def sum_chunk(t, v, c):
                n = (v // 2) * CH + c
                if c in (0, CUT_CH):
                    pe.wait_ge(prob_ready, (t * BPT + 2 * (v // 2)) * 2 + (5 if c == 0 else 6))
                pe.wait_ge(chunk_added, t * (2 * CH) + n + 1)
                first = (v // 2) * 2
                for a, b in enumerate(chunk(c)):
                    for k in range(2):
                        last = pe.matmul(psO[n % 2][0:BLK, a * W2:(a + 1) * W2], pr[:, (first + k) % PR, b * BLK:(b + 1) * BLK],
                                         hx[:, bass.ds(t * BPT + first + k, 1), 0:W2].rearrange("p o w -> p (o w)"), start=(k == 0), stop=(k == 1))
                last.then_inc(chunk_done, 1)

            def window(t, v, u):
                w = (v + 1) * WPB + u
                bank = psC[w % 2]

                def before():
                    for c in chunks_at(v, u):
                        sum_chunk(t, v, c)
                    pe.wait_ge(bank_read, t * (BPT * WPB) + w + 1)
                    for k in range(2):
                        pe.matmul(bank[0:WME, k, 0:HALF], zeros[:, 0:WME], zeros[:, :], start=True, stop=True, skip_group_check=True)

                def after():
                    pe.matmul(bank[0:WME, 1, 0:8], zeros[:, 0:WME], zeros[:, 0:8], start=False, stop=True,
                              skip_group_check=True).then_inc(window_summed, 1)
                return before, after

            def tile(s, now, aps, v, u):
                pe.wait_ge(hot_ready[s], now)
                bank = psC[((v + 1) * WPB + u) % 2]
                for k in range(2):
                    last = pe.matmul(bank[0:WME, k, 0:HALF], hot_m[:, s, :], hot_n[:, s, k * HALF:(k + 1) * HALF],
                                     start=False, stop=True, skip_group_check=True)
                if s % HG == HG - 1:
                    last.then_inc(hot_free[s // HG], 1)
            blocks(pe, windows(pe, "pe", window, lambda n, t, v, u: None, tile))
            for c in range(CH):
                sum_chunk(TURNS_A, 0, c)

        @block.scalar
        def _(act):
            act.sem_inc(bank_read, 2)

            def body(t, v):
                slot = pr[:, (v + 2) % PR, :]
                if v >= 0:
                    act.wait_ge(chunk_done, t * (2 * CH) + (v // 2) * CH + CH)
                act.activation(slot, s1r[0:BLK, :], ACT.Identity, bias=T.s2s[:, bass.ds(t * BPT + v + 1, 1)], scale=SLOPE).then_inc(low_ready, 1)
                for u in range(WPB):
                    w = (v + 1) * WPB + u
                    act.wait_ge(window_summed, t * (BPT * WPB) + w + 1)
                    act.wait_ge(stage_out[w % 2], t * (BPT * WPB * 8) + 16 * (w // 2) + 16)
                    act.activation(stage[0:WME, w % 2, :].rearrange("p (k n) -> p k n", k=2), psC[w % 2][0:WME, :, 0:HALF], ACT.Copy,
                                   accum_out=T.edges_of[0:WME, bass.ds(t * (BPT * WPB) + w, 1)]).then_inc(bank_read, 1)
                    if u == EXP_AT:
                        act.wait_ge(clip_ready, (t * BPT + v + 2) * 2)
                        act.activation(slot, slot, ACT.Exp).then_inc(exp_ready, 1)
            blocks(act, body)
            act.wait_ge(moments_ready, 1)
            act.activation(T.std[:, :], T.den[:, :], ACT.Sqrt).then_inc(std_ready, 1)

        @block.vector
        def _(dve):
            def step(ins):
                dve.wait_ge(chain.sem, chain.inc(ins))
            dve.memset(zeros[:, :], 0.0).then_inc(zeros_ready, 1)
            dve.sem_inc(chunk_added, 2)

            def add_chunk(t, v, c):
                n = (v // 2) * CH + c
                blks = chunk(c)
                dve.wait_ge(chunk_done, t * (2 * CH) + n + 1 + CH)
                part = acc[:, blks[0]:blks[-1] + 1, :]
                dve.tensor_tensor(part, psO[n % 2][0:BLK, 0:len(blks) * W2].rearrange("p (b w) -> p b w", w=W2),
                                  part, ALU.add).then_inc(chunk_added, 1)

            def window_keys(t, v, u):
                first = (t * (BPT * WPB) + (v + 1) * WPB + u) * WM
                return T.iota_m[:, bass.ds(first, WME)].rearrange("p (o m) -> p o m", o=1).broadcast_to([P, HG, WME])

            def window(t, v, u):
                slot = pr[:, (v + 2) % PR, :]

                def before():
                    dve.lower_ap(window_keys(t, v, u))

                def after():
                    for part in LEAKY_AT[u]:
                        cols = slice(*SCORE_CUTS[part])
                        if part == 0:
                            dve.wait_ge(low_ready, t * BPT + v + 2)
                        dve.scalar_tensor_tensor(slot[:, cols], s1r[0:BLK, cols], hx[:, bass.ds(t * BPT + v + 2, 1), D + 1:D + 2].rearrange("p o w -> p (o w)"),
                                                 slot[:, cols], ALU.add, ALU.max).then_inc(leaky_ready, 1)
                    for part in CLIP_AT[u]:
                        cols = slice(*SCORE_CUTS[part])
                        dve.wait_ge(leaky_ready, (t * BPT + v + 1) * 2 + part + 1)
                        dve.tensor_scalar(slot[:, cols], slot[:, cols], -CLIP, CLIP, ALU.max, ALU.min).then_inc(clip_ready, 1)
                    for c in chunks_at(v, u):
                        add_chunk(t, v, c)
                return before, after

            def tile_aps(n, t, v, u):
                keys = [T.row_keys[:, bass.ds(n, TPT)][:, s:s + HG].rearrange("p (s o) -> p s o", o=1).broadcast_to([P, HG, WME])
                        for s in range(0, TPT, HG)]
                rests = T.edge_keys[:, 1, bass.ds(n, TPT)]
                for ap in keys:
                    dve.lower_ap(ap)
                dve.lower_ap(rests)
                return keys, rests, window_keys(t, v, u)

            def tile(s, now, aps, v, u):
                keys, rests, rows = aps
                if s % HG == 0:
                    dve.wait_ge(hot_free[s // HG], now)
                    dve.tensor_tensor(hot_m[:, s:s + HG, :], rows, keys[s // HG], ALU.is_equal)
                dve.tensor_scalar(hot_n[:, s, :], T.iota_n[:, :], rests[:, s:s + 1], None, ALU.is_equal).then_inc(hot_ready[s], 1)
            blocks(dve, windows(dve, "dve", window, tile_aps, tile))
            for c in range(CH):
                add_chunk(TURNS_A, 0, c)
                dve.wait_ge(chunk_added, 2 * TURNS_A * CH + c + 3)
                blks = chunk(c)
                den = T.den[:, blks[0]:blks[-1] + 1]
                step(dve.tensor_scalar(den, acc[:, blks[0]:blks[-1] + 1, D], EPS_ALPHA, None, ALU.add))
                step(dve.reciprocal(den, den))
                for b in blks:
                    last = dve.scalar_tensor_tensor(xn[:, b, :], acc[:, b, 0:D], T.den[:, b:b + 1], xn[:, b, :], ALU.mult, ALU.add)
                step(last)
                for b in blks:
                    last = dve.bn_stats(T.stats[:, b, :], xn[:, b, :])
                step(last)
            layernorm(dve, step, T, xn, moments_ready, std_ready, [(0, N)], rows_ready)


def node_tables(nc, T, wm1, bm1, table_a, table_b):
    with ExitStack() as ctx:
        def sb(name, shape, dt):
            return ctx.enter_context(nc.sbuf_tensor(name, shape, dt))

        def sem(name):
            return ctx.enter_context(nc.semaphore(name))
        NB = 4
        PAIRS = -(-NBLK // 2)
        DM = 4
        w = sb("wm1_sb", [D, 2, H], fp32)
        b1 = sb("bm1_sb", [P, H], fp32)
        a_st = sb("a_st", [BLK, NB, 2, H], fp32)
        rest = sb("rest", [BLK, NB, 2, 2, H], fp32)
        b_st = sb("b_st", [BLK, NB, 2, 3, H], bf16)
        zpad = sb("zpad", [NPAD - N, 3 * H], bf16)
        psX = [ctx.enter_context(nc.psum_tensor(f"psX{i}", [P, 512], fp32)) for i in range(2)]
        psN = [ctx.enter_context(nc.psum_tensor(f"psN{i}", [P, 2, 2, H], fp32)) for i in range(2)]
        psD = [ctx.enter_context(nc.psum_tensor(f"psD{i}", [P, DM, NWIN], fp32)) for i in range(2)]
        ones = sb("ones_t", [P, P], fp32)
        mask = sb("mask", [P, WIN], fp32)
        spread = sb("spread", [WIN, WIN, NWIN], fp32)
        node_inv = sb("node_inv", [WIN, NWIN], fp32)
        node_has = sb("node_has", [WIN, NWIN], fp32)
        loaded = sem("loaded_t")
        x_turned = sem("x_turned_t")
        x_copied = sem("x_copied_t")
        ab_done = sem("ab_done")
        part_ready = [sem(f"part_ready{i}") for i in range(3)]
        rest_ready = [sem(f"rest_ready{i}") for i in range(2)]
        a_ready = sem("a_ready")
        zpad_ready = sem("zpad_ready")
        mask_ready = sem("mask_ready")
        nodes_summed = sem("nodes_summed")
        spread_ready = sem("spread_ready")
        edges_summed = sem("edges_summed")
        edges_read = sem("edges_read")
        a_out = [sem(f"a_out{i}") for i in range(NB)]
        b_out = [sem(f"b_out{i}") for i in range(NB)]
        z_out = sem("z_out")
        block = ctx.enter_context(nc.Block())

        def pair(g):
            return list(range(2 * g, min(NBLK, 2 * g + 2)))

        @block.sync
        def _(sp):
            sp.dma_start(w[:, :, :], wm1.rearrange("(c f) h -> f c h", c=2)).then_inc(loaded, 16)
            sp.dma_start(b1[:, :], bm1.rearrange("(o h) -> o h", o=1).broadcast_to([P, H])).then_inc(loaded, 16)
            sp.wait_ge(zpad_ready, 1)
            sp.dma_start(table_b[N:NPAD, :], zpad[:, :]).then_inc(z_out, 16)
            for g in range(PAIRS):
                blks = pair(g)
                rows = slice(blks[0] * BLK, (blks[-1] + 1) * BLK)
                sp.wait_ge(a_ready, g + 1)
                sp.dma_start(table_a[rows, :].rearrange("(b p) h -> p b h", p=BLK), a_st[:, g % NB, 0:len(blks), :]).then_inc(a_out[g % NB], 16)
                sp.wait_ge(part_ready[2], g + 1)
                sp.dma_start(table_b[rows, :].rearrange("(b p) h -> p b h", p=BLK),
                             b_st[:, g % NB, 0:len(blks), :, :].rearrange("p b c h -> p b (c h)")).then_inc(b_out[g % NB], 16)
            sp.wait_ge(z_out, 16)
            for s in range(NB):
                stores = (PAIRS - 1 - s) // NB + 1
                sp.wait_ge(a_out[s], 16 * stores)
                sp.wait_ge(b_out[s], 16 * stores)

        @block.gpsimd
        def _(pool):
            pool.memset(ones[:, :], 1.0).then_inc(mask_ready, 1)
            pool.memset(T.agg[:, :, :], 0.0)
            pool.wait_ge(mask_ready, 1)
            pool.affine_select(out=mask[:, :], in_=ones[:, 0:WIN], compare_op=ALU.is_ge, fill=0.0, base=0,
                               pattern=[[-SBLK, WIN]], channel_multiplier=1).then_inc(mask_ready, 1)
            pool.wait_ge(mask_ready, 2)
            pool.affine_select(out=mask[:, :], in_=mask[:, :], compare_op=ALU.is_ge, fill=0.0, base=SBLK - 1,
                               pattern=[[SBLK, WIN]], channel_multiplier=-1).then_inc(mask_ready, 1)

        def some_nodes(c):
            return c * DM, min(WIN, (c + 1) * DM)

        def tables(pe, g):
            pe.wait_ge(x_copied, pair(g)[-1] + 1)
            if g >= 2:
                pe.wait_ge(rest_ready[0], g - 1)
            for i, b in enumerate(pair(g)):
                last = pe.matmul(psN[g % 2][0:BLK, i, :, :].rearrange("p c h -> p (c h)"), T.x1T[:, b * BLK:(b + 1) * BLK],
                                 w[:, :, :].rearrange("p c h -> p (c h)"), start=True, stop=True)
            last.then_inc(ab_done, 1)

        def spread_edges(pe, c):
            a, z = some_nodes(c)
            if c == 0:
                pe.wait_ge(spread_ready, 5)
            if c >= 2:
                pe.wait_ge(edges_read, c - 1)
            pe.matmul(psD[c % 2][:, 0:z - a, :].rearrange("p m w -> p (m w)"), ones[0:WIN, :],
                      spread[:, a:z, :].rearrange("p m w -> p (m w)"), start=True, stop=True).then_inc(edges_summed, 1)

        @block.tensor
        def _(pe):
            pe.wait_ge(mask_ready, 3)
            pe.matmul(psD[0][0:WIN, 0, :], mask[0:WM, :], T.edges_of[0:WM, :], start=True, stop=True).then_inc(nodes_summed, 1)
            pe.wait_ge(loaded, 32)
            for g in range(PAIRS + 1):
                if g < PAIRS:
                    for b in pair(g):
                        if b >= 2:
                            pe.wait_ge(x_copied, b - 1)
                        pe.transpose(psX[b % 2][:, 0:BLK], T.x1[:, b, :], T.ident[0:BLK, 0:BLK]).then_inc(x_turned, 1)
                if g >= 1:
                    tables(pe, g - 1)
                if g % 2 == 1:
                    spread_edges(pe, g // 2)

        @block.scalar
        def _(act):
            for g in range(PAIRS + 3):
                if g < PAIRS:
                    for b in pair(g):
                        act.wait_ge(x_turned, b + 1)
                        act.activation(T.x1T[:, b * BLK:(b + 1) * BLK], psX[b % 2][:, 0:BLK], ACT.Copy).then_inc(x_copied, 1)
                for k in range(3):
                    n = g - 1 - k
                    if not 0 <= n < PAIRS:
                        continue
                    s, i = n % NB, len(pair(n))
                    if k == 0:
                        act.wait_ge(a_ready, n + 1)
                        if n >= NB:
                            act.wait_ge(b_out[s], 16 * (n // NB))
                        source = psN[n % 2][0:BLK, 0:i, 1, :]
                    else:
                        act.wait_ge(rest_ready[k - 1], n + 1)
                        source = rest[:, s, 0:i, k - 1, :]
                    act.activation(b_st[:, s, 0:i, k, :], source, ACT.Copy).then_inc(part_ready[k], 1)
                if g % 2 == 0 and 2 <= g <= PAIRS + 1:
                    c = g // 2 - 1
                    a, z = some_nodes(c)
                    act.wait_ge(edges_summed, c + 1)
                    act.activation(T.inv[:, :].rearrange("p (w m) -> p m w", m=WIN)[:, a:z, :], psD[c % 2][:, 0:z - a, :], ACT.Copy).then_inc(edges_read, 1)

        @block.vector
        def _(dve):
            dve.memset(zpad[:, :], 0.0).then_inc(zpad_ready, 1)
            dve.wait_ge(nodes_summed, 1)
            dve.tensor_scalar(node_has[:, :], psD[0][0:WIN, 0, :], 1.0, None, ALU.min).then_inc(spread_ready, 1)
            dve.tensor_scalar(node_inv[:, :], psD[0][0:WIN, 0, :], 1.0, None, ALU.max).then_inc(spread_ready, 1)
            dve.wait_ge(spread_ready, 2)
            dve.reciprocal(node_inv[:, :], node_inv[:, :]).then_inc(spread_ready, 1)
            dve.wait_ge(spread_ready, 3)
            dve.tensor_tensor(node_inv[:, :], node_inv[:, :], node_has[:, :], ALU.mult).then_inc(spread_ready, 1)
            dve.wait_ge(spread_ready, 4)
            dve.tensor_tensor(spread[:, :, :], node_inv[:, :].rearrange("p (o w) -> p o w", o=1).broadcast_to([WIN, WIN, NWIN]),
                              T.ident[0:WIN, 0:WIN].rearrange("p (m o) -> p m o", o=1).broadcast_to([WIN, WIN, NWIN]), ALU.mult).then_inc(spread_ready, 1)
            dve.wait_ge(loaded, 32)
            for g in range(PAIRS + 1):
                if g < PAIRS:
                    s, i = g % NB, len(pair(g))
                    dve.wait_ge(ab_done, g + 1)
                    if g >= NB:
                        dve.wait_ge(a_out[s], 16 * (g // NB))
                    dve.tensor_tensor(a_st[:, s, 0:i, :], psN[g % 2][0:BLK, 0:i, 0, :],
                                      b1[0:BLK, :].rearrange("p (o h) -> p o h", o=1).broadcast_to([BLK, i, H]), ALU.add).then_inc(a_ready, 1)
                    dve.wait_ge(part_ready[0], g + 1)
                    if g >= NB:
                        dve.wait_ge(part_ready[2], g - NB + 1)
                    dve.tensor_tensor(rest[:, s, 0:i, 0, :], psN[g % 2][0:BLK, 0:i, 1, :], b_st[:, s, 0:i, 0, :], ALU.subtract).then_inc(rest_ready[0], 1)
                if g >= 1:
                    n = g - 1
                    s, i = n % NB, len(pair(n))
                    dve.wait_ge(part_ready[1], n + 1)
                    dve.tensor_tensor(rest[:, s, 0:i, 1, :], rest[:, s, 0:i, 0, :], b_st[:, s, 0:i, 1, :], ALU.subtract).then_inc(rest_ready[1], 1)


def messages(nc, T, wm2, bm2, table_a, table_b, scr_dst, bm3, wm3, bn1, wn1, wn2, bn2):
    with ExitStack() as ctx:
        def sb(name, shape, dt):
            return ctx.enter_context(nc.sbuf_tensor(name, shape, dt))

        def sem(name):
            return ctx.enter_context(nc.semaphore(name))
        BR = 65
        w = sb("wm2_sb", [P, 2, H], fp32)
        w_hi = sb("wm2_hi", [P, 2, H], f32r)
        w_lo = sb("wm2_lo", [P, 2, H], f32r)
        bias = sb("bias", [BR, 2, H], fp32)
        bias_p = sb("bias_p", [BR, 3, 2, H], bf16)
        bias_b = sb("bias_b", [BR, 2, H], bf16)
        ones_b = sb("ones_b", [BR, P], bf16)
        third = sb("third", [P, 1], fp32)
        third_i = sb("third_i", [P, 1], i32)
        idx = sb("idx", [P, GUN, GT], i32)
        ga = sb("ga", [P, GUN, GT, H], fp32)
        bw = sb("bw", [P, GUN, H], bf16)
        dstb = sb("dstb", [P, GUN, GE], i16)
        hot_t = sb("hot_t", [P, GUN, GE], bf16)
        hot_e = sb("hot_e", [P, GUN, GT, GW], bf16)
        h1_hi = sb("h1_hi", [P, 2, 2, GE], f32r)
        h1_lo = sb("h1_lo", [P, 2, 2, GE], f32r)
        h2 = [sb(f"h2_{k}", [P, 2, GT, H], bf16) for k in range(3)]
        rest1 = sb("rest1", [P, 2, GT, H], fp32)
        ps1 = [[ctx.enter_context(nc.psum_tensor(f"ps1_{i}{k}", [P, GE], fp32)) for k in range(2)] for i in range(2)]
        ps2 = [ctx.enter_context(nc.psum_tensor(f"ps2_{i}", [P, 2, H], fp32)) for i in range(2)]
        psA = [ctx.enter_context(nc.psum_tensor(f"psA_{i}", [P, 2, GW], fp32)) for i in range(2)]
        loaded = sem("loaded_m")
        later_in = sem("later_in")
        setup_done = sem("setup_done")
        split_done = sem("split_done")
        idx_ready = sem("idx_ready")
        pool_order = sem("pool_order")
        sp_order = sem("sp_order")
        gathered = [[sem(f"gathered{i}_{k}") for k in range(GT)] for i in range(GUN)]
        window_in = [sem(f"window_in{i}") for i in range(GUN)]
        dst_in = [sem(f"dst_in{i}") for i in range(GUN)]
        hot_ready = sem("hot_ready_m")
        h1_summed = sem("h1_summed")
        hi_ready = sem("hi_ready")
        lo_ready = sem("lo_ready")
        h2_summed = sem("h2_summed")
        part1_ready = sem("part1_ready")
        rest_ready = sem("rest_ready_m")
        part2_ready = sem("part2_ready")
        part3_ready = sem("part3_ready")
        bias_ready = sem("bias_ready")
        chain = Counted(ctx, nc, "chain_m")
        agg_summed = sem("agg_summed")
        agg_added = sem("agg_added")
        sweep_done = sem("sweep_done")
        tables_next = sem("tables_next")
        block = ctx.enter_context(nc.Block())
        LAST = GROUPS - GUN

        def sweeps(eng, start, body, end):
            passes = eng.value_load(T.passes_i[0:1, 0:1], min_val=1, max_val=STEPS)
            with eng.Fori(0, passes) as p:
                n0 = eng.snap(p * GROUPS, min_val=0, max_val=STEPS * GROUPS)
                if start:
                    start(n0)
                body(n0, 0, True, False)
                with eng.Fori(GUN, LAST, GUN) as i:
                    i = bounded(i, GUN, LAST - GUN)
                    body(eng.snap(p * GROUPS + i, min_val=0, max_val=STEPS * GROUPS), i, False, False)
                body(eng.snap(p * GROUPS + LAST, min_val=0, max_val=STEPS * GROUPS), LAST, False, True)
                end(p)

        @block.sync
        def _(sp):
            sp.dma_start(w[:, :, :], wm2.rearrange("(c f) h -> f c h", c=2)).then_inc(loaded, 16)
            for c in range(2):
                sp.dma_start(bias[:, c, :], bm2.rearrange("(o h) -> o h", o=1).broadcast_to([BR, H])).then_inc(loaded, 16)
            with nc.allow_non_contiguous_dma(reason="biases to partitions"):
                sp.dma_start(T.b3[:, :], bm3.rearrange("(f o) -> f o", o=1), allow_slow_non_contiguous=True).then_inc(later_in, 16)
                sp.dma_start(T.ba[:, :], bn1.rearrange("(c f) -> f c", c=2), allow_slow_non_contiguous=True).then_inc(later_in, 16)
            sp.dma_start(T.w3[:, :, :], wm3.rearrange("(c f) h -> f c h", c=2)).then_inc(later_in, 16)
            sp.dma_start(T.wa[:, :, :], wn1.rearrange("(c f) h -> f c h", c=2)).then_inc(later_in, 16)
            sp.dma_start(T.wb[:, :, :], wn2.rearrange("(c f) h -> f c h", c=2)).then_inc(later_in, 16)
            sp.dma_start(T.bb[:, :], bn2.rearrange("(o h) -> o h", o=1).broadcast_to([P, D])).then_inc(later_in, 16)
            regs = [sp.alloc_register(f"sp_base{u}") for u in range(GUN)]

            def body(n, i, first, last):
                sp.reg_load(regs, T.base_i[0:1, bass.ds(i, GUN)])
                for u in range(GUN):
                    base = sp.snap(regs[u], min_val=0, max_val=N + 1)
                    sp.wait_ge(h1_summed, (n + u) * 2 + 2)
                    sp.sem_inc(sp_order, 1)
                    sp.dma_start(bw[0:GWM, u, :], table_b.rearrange("n (c h) -> (n c) h", c=3)[bass.ds(base * 3, GWM), :]).then_inc(window_in[u], 16)
                    sp.dma_start(dstb[0:GWM, u, :], scr_dst.rearrange("(o e) -> o e", o=1)[:, bass.ds((i + u) * GE, GE)].broadcast_to([GWM, GE])).then_inc(dst_in[u], 16)

            def end(p):
                sp.wait_ge(tables_next, p + 1)
                sp.sem_inc(sp_order, 1)
            sweeps(sp, None, body, end)
            sp.wait_ge(later_in, 96)

        @block.gpsimd
        def _(pool):
            pool.iota(third_i[:, :], [[0, 1]], base=0, channel_multiplier=1).then_inc(setup_done, 1)

            def body(n, i, first, last):
                for u in range(GUN):
                    pool.wait_ge(idx_ready, n + u + 1)
                    pool.sem_inc(pool_order, 1)
                    for k in range(GT):
                        pool.indirect_dma_start(ga[:, u, k, :], None, table_a,
                                                bass.IndirectOffsetOnAxis(ap=idx[:, u, k:k + 1], axis=0)).then_inc(gathered[u][k], 16)

            def end(p):
                pool.wait_ge(tables_next, p + 1)
                pool.sem_inc(pool_order, 1)
            sweeps(pool, None, body, end)

        @block.tensor
        def _(pe):
            pe.sem_inc(h1_summed, 2 * GUN)
            pe.wait_ge(split_done, 2)
            pe.wait_ge(bias_ready, 5)
            pe.wait_ge(setup_done, 1)

            def hidden1(n, u):
                s = u % GUN
                pe.wait_ge(window_in[s], (n if u < GUN else n + GUN) * 4 + 16)
                pe.wait_ge(hot_ready, n + u + 1)
                pe.wait_ge(lo_ready, (n + u) * 2 + 2)
                for k in range(2):
                    bank = ps1[u % 2][k]
                    pe.matmul(bank[:, :], bw[0:GWM, s, k * P:(k + 1) * P], hot_t[0:GWM, s, :], start=True, stop=True, skip_group_check=True)
                    for t in range(GT):
                        if k == 0:
                            pe.wait_ge(gathered[s][t], (n if u < GUN else n + GUN) * 4 + 16)
                        last = pe.matmul(bank[:, t * P:(t + 1) * P], ga[:, s, t, k * P:(k + 1) * P], T.ident[:, :],
                                         is_transpose=True, start=False, stop=True, skip_group_check=True)
                    last.then_inc(h1_summed, 1)

            def hidden2(n, u):
                for q in range(2):
                    pe.wait_ge(rest_ready, (n + u) * 2 + q + 1)
                    pe.matmul(ps2[q][:, :, :].rearrange("p t h -> p (t h)"), ones_b[:, :], bias_b[:, :, :].rearrange("p t h -> p (t h)"),
                              start=True, stop=True, skip_group_check=True)
                pe.wait_ge(hi_ready, (n + u) * 2 + 2)
                for q in range(2):
                    tiles = (2 * q, 2 * q + 1)
                    for t in tiles:
                        for k in range(2):
                            hi = h1_hi[:, u % 2, k, t * P:(t + 1) * P]
                            pe.matmul(ps2[q][:, t % 2, :], hi, w_hi[:, k, :], start=False, stop=True, skip_group_check=True)
                            pe.matmul(ps2[q][:, t % 2, :], hi, w_lo[:, k, :], start=False, stop=True, skip_group_check=True)
                    if q == 0:
                        pe.wait_ge(lo_ready, (n + u) * 2 + 6)
                    for t in tiles:
                        for k in range(2):
                            last = pe.matmul(ps2[q][:, t % 2, :], h1_lo[:, u % 2, k, t * P:(t + 1) * P], w_hi[:, k, :],
                                             start=False, stop=True, skip_group_check=True)
                    last.then_inc(h2_summed, 1)

            def aggregate(n, u):
                pe.wait_ge(part3_ready, (n + u) * 2 + 2)
                pe.wait_ge(agg_added, n + u + 1)
                bank = psA[u % 2]
                for t in range(GT):
                    for c in range(3):
                        for k in range(2):
                            last = pe.matmul(bank[:, k, :], h2[c][:, u % 2, t, k * P:(k + 1) * P], hot_e[:, u % GUN, t, :],
                                             start=(t == 0 and c == 0 and k == 0), stop=True, skip_group_check=True)
                last.then_inc(agg_summed, 1)

            def body(n, i, first, last):
                for u in range(GUN):
                    hidden2(n, u)
                    if not (last and u == GUN - 1):
                        hidden1(n, u + 1)
                    if not (first and u == 0):
                        aggregate(n, u - 1)
                if last:
                    aggregate(n, GUN - 1)

            def end(p):
                pe.wait_ge(tables_next, p + 1)
            sweeps(pe, lambda n: hidden1(n, 0), body, end)

        @block.scalar
        def _(act):
            act.sem_inc(h2_summed, 4)
            act.sem_inc(agg_summed, 2)

            def indices(i, u):
                act.activation(idx[:, u, :], T.src_idx[:, bass.ds((i + u) * GT, GT)], ACT.Copy).then_inc(idx_ready, 1)

            def high(n, u):
                act.wait_ge(h2_summed, (n + u) * 2 + 2)
                for k in range(2):
                    act.wait_ge(h1_summed, (n + u) * 2 + 2 * GUN + 1 + k)
                    act.activation(h1_hi[:, u % 2, k, :], ps1[u % 2][k][:, :], ACT.Relu).then_inc(hi_ready, 1)

            def part1(n, u, q):
                act.wait_ge(h2_summed, (n + u) * 2 + q + 5)
                act.activation(h2[0][:, u % 2, 2 * q:2 * q + 2, :], ps2[q][:, :, :], ACT.Relu).then_inc(part1_ready, 1)

            def part2(n, u, q):
                act.wait_ge(rest_ready, (n + u) * 2 + q + 3)
                act.activation(h2[1][:, u % 2, 2 * q:2 * q + 2, :], rest1[:, u % 2, 2 * q:2 * q + 2, :], ACT.Copy).then_inc(part2_ready, 1)

            def start(n):
                for u in range(GUN):
                    act.activation(idx[:, u, :], T.src_idx[:, u * GT:(u + 1) * GT], ACT.Copy).then_inc(idx_ready, 1)
                high(n, 0)

            def body(n, i, first, last):
                for u in range(GUN):
                    act.wait_ge(agg_summed, n + u + 1)
                    part1(n, u, 0)
                    part1(n, u, 1)
                    if not (last and u == GUN - 1):
                        high(n, u + 1)
                    part2(n, u, 0)
                    part2(n, u, 1)
                    if not last:
                        indices(i + GUN, u)

            def end(p):
                act.wait_ge(tables_next, p + 1)
            sweeps(act, start, body, end)

        @block.vector
        def _(dve):
            def step(ins):
                dve.wait_ge(chain.sem, chain.inc(ins))
            dve.memset(bias_b[:, :, :], 0.0).then_inc(bias_ready, 1)
            dve.memset(ones_b[:, :], 1.0).then_inc(bias_ready, 1)
            dve.wait_ge(loaded, 48)
            dve.wait_ge(setup_done, 1)
            dve.tensor_copy(w_hi[:, :, :], w[:, :, :]).then_inc(split_done, 1)
            dve.tensor_scalar(third[:, :], third_i[:, :], 21846.0, None, ALU.mult).then_inc(setup_done, 1)
            dve.wait_ge(split_done, 1)
            dve.tensor_tensor(w_lo[:, :, :], w[:, :, :], w_hi[:, :, :].bitcast(fp32), ALU.subtract).then_inc(split_done, 1)
            dve.wait_ge(bias_ready, 2)
            for k in range(3):
                row = slice(32 * k, 32 * k + 1)
                step(dve.tensor_copy(bias_p[:, k, :, :], bias[:, :, :]))
                dve.tensor_copy(bias_b[row, :, :], bias_p[row, k, :, :]).then_inc(bias_ready, 1)
                step(dve.tensor_tensor(bias[:, :, :], bias[:, :, :], bias_p[:, k, :, :], ALU.subtract))
            dve.wait_ge(setup_done, 2)
            dve.tensor_copy(third_i[:, :], third[:, :]).then_inc(setup_done, 1)
            dve.wait_ge(setup_done, 3)
            dve.tensor_single_scalar(third_i[:, :], third_i[:, :], 16, ALU.logical_shift_right).then_inc(setup_done, 1)
            dve.wait_ge(setup_done, 4)
            dve.tensor_copy(third[:, :], third_i[:, :]).then_inc(setup_done, 1)
            dve.wait_ge(setup_done, 5)
            dve.sem_inc(lo_ready, 4)
            dve.sem_inc(rest_ready, 2)
            dve.sem_inc(agg_added, 2)
            regs = [dve.alloc_register(f"dve_base{u}") for u in range(GUN)]
            before = dve.alloc_register("dve_base_before")

            def one_hots(n, i, u):
                s = u % GUN
                dve.wait_ge(dst_in[s], (n if u < GUN else n + GUN) * 4 + 16)
                dve.tensor_scalar(hot_t[0:GWM, s, :], dstb[0:GWM, s, :], T.neg_base[0:GWM, bass.ds(i + u, 1)],
                                  third[0:GWM, 0:1], ALU.add, ALU.is_equal)
                dve.tensor_tensor(hot_e[:, s, :, :], T.iota_n[:, 0:GW].rearrange("p (o w) -> p o w", o=1).broadcast_to([P, GT, GW]),
                                  T.edge_keys[:, 3, bass.ds((i + u) * GT, GT)].rearrange("p (t o) -> p t o", o=1).broadcast_to([P, GT, GW]),
                                  ALU.is_equal).then_inc(hot_ready, 1)

            def low(n, u):
                for k in range(2):
                    dve.wait_ge(hi_ready, (n + u) * 2 + 1 + k)
                    dve.scalar_tensor_tensor(h1_lo[:, u % 2, k, :], ps1[u % 2][k][:, :], 0.0, h1_hi[:, u % 2, k, :].bitcast(fp32),
                                             ALU.max, ALU.subtract).then_inc(lo_ready, 1)

            def rest(n, u, q):
                dve.wait_ge(part1_ready, (n + u) * 2 + q + 1)
                dve.scalar_tensor_tensor(rest1[:, u % 2, 2 * q:2 * q + 2, :], ps2[q][:, :, :], 0.0, h2[0][:, u % 2, 2 * q:2 * q + 2, :],
                                         ALU.max, ALU.subtract).then_inc(rest_ready, 1)

            def part3(n, u, q):
                dve.wait_ge(part2_ready, (n + u) * 2 + q + 1)
                dve.tensor_tensor(h2[2][:, u % 2, 2 * q:2 * q + 2, :], rest1[:, u % 2, 2 * q:2 * q + 2, :], h2[1][:, u % 2, 2 * q:2 * q + 2, :],
                                  ALU.subtract).then_inc(part3_ready, 1)

            def start(n):
                one_hots(n, 0, 0)
                one_hots(n, 0, 1)
                low(n, 0)

            def body(n, i, first, last):
                if not first:
                    dve.reg_mov(before, regs[GUN - 1])
                dve.reg_load(regs, T.base_i[0:1, bass.ds(i, GUN)])

                def sums_at(u):
                    reg = before if u < 0 else regs[u]
                    return T.agg[:, :, bass.ds(dve.snap(reg, min_val=0, max_val=N + 1), GW)]

                def add_sums(u, at):
                    dve.wait_ge(agg_summed, n + u + 3)
                    dve.wait_ge(agg_added, n + u + 2)
                    dve.tensor_tensor(at, psA[u % 2][:, :, :], at, ALU.add).then_inc(agg_added, 1)

                for u in range(GUN):
                    at = sums_at(u - 1) if not (first and u == 0) else None
                    if at is not None:
                        dve.lower_ap(at)
                    rest(n, u, 0)
                    rest(n, u, 1)
                    if not (last and u == GUN - 1):
                        low(n, u + 1)
                    part3(n, u, 0)
                    part3(n, u, 1)
                    if not (last and u >= GUN - 2):
                        one_hots(n, i, u + 2)
                    if at is not None:
                        add_sums(u - 1, at)
                if last:
                    add_sums(GUN - 1, sums_at(GUN - 1))

            def end(p):
                dve.wait_ge(agg_added, (p + 1) * GROUPS + 2)
                dve.tensor_scalar(T.edge_keys[:, 3, 0:TILES], T.edge_keys[:, 3, 0:TILES], -float(GW), None, ALU.add).then_inc(sweep_done, 1)
                dve.tensor_scalar(T.neg_base[:, :], T.neg_base[:, :], -float(GW), None, ALU.add).then_inc(sweep_done, 1)
                dve.tensor_scalar(T.base_row[:, :], T.base_row[:, :], float(GW), float(N + 1), ALU.add, ALU.min).then_inc(sweep_done, 1)
                dve.wait_ge(sweep_done, p * 4 + 3)
                dve.tensor_copy(T.base_i[:, :], T.base_row[:, :]).then_inc(sweep_done, 1)
                dve.wait_ge(sweep_done, p * 4 + 4)
                dve.sem_inc(tables_next, 1)
            sweeps(dve, start, body, end)


def update_nodes(nc, T, out):
    with ExitStack() as ctx:
        def sb(name, shape, dt):
            return ctx.enter_context(nc.sbuf_tensor(name, shape, dt))

        def sem(name):
            return ctx.enter_context(nc.semaphore(name))
        w3, b3, wa, ba, wb, bb = T.w3, T.b3, T.wa, T.ba, T.wb, T.bb
        has = sb("has", [P, N], fp32)
        msg = sb("msg", [D, N], fp32)
        u1 = sb("u1", [P, 2, N], fp32)
        psM = [ctx.enter_context(nc.psum_tensor(f"psM{i}", [P, 512], fp32)) for i in range(2)]
        psU = [ctx.enter_context(nc.psum_tensor(f"psU{i}", [P, 512], fp32)) for i in range(4)]
        psV = [ctx.enter_context(nc.psum_tensor(f"psV{i}", [P, 512], fp32)) for i in range(2)]
        mean_ready = sem("mean_ready")
        has_ready = sem("has_ready")
        msg_done = sem("msg_done")
        msg_ready = sem("msg_ready")
        u1_done = sem("u1_done")
        u1_ready = sem("u1_ready")
        u2_done = sem("u2_done")
        u2_read = sem("u2_read")
        moments_ready = sem("moments_u")
        std_ready = sem("std_u")
        rows_ready = sem("rows_ready")
        out_done = sem("out_done")
        chain = Counted(ctx, nc, "chain_u")
        block = ctx.enter_context(nc.Block())
        sums_ready = sem("sums_ready")
        CB = 4
        cuts = [(a * BLK, min(NBLK, a + CB) * BLK) for a in range(0, NBLK, CB)]
        CUTS = len(cuts)

        @block.sync
        def _(sp):
            rows = out.rearrange("(b n) f -> n b f", b=NBLK)
            for c, (a, z) in enumerate(cuts):
                sp.wait_ge(rows_ready, c + 1)
                sp.dma_start(rows[:, a // BLK:z // BLK, :], T.x1[:, a // BLK:z // BLK, :]).then_inc(out_done, 16)
            sp.wait_ge(out_done, 16 * CUTS)

        @block.gpsimd
        def _(pool):
            pool.tensor_scalar(T.x1[:, :, :], T.x1[:, :, :], 2.0, None, ALU.mult).then_inc(sums_ready, 1)
            pool.wait_ge(sums_ready, 1)
            pool.tensor_tensor(T.x1[:, :, :], T.x1[:, :, :],
                               bb[0:BLK, :].rearrange("p (o f) -> p o f", o=1).broadcast_to([BLK, NBLK, D]), ALU.add).then_inc(sums_ready, 1)

        @block.tensor
        def _(pe):
            for c in range(CUTS + 2):
                if c < CUTS:
                    a, z = cuts[c]
                    pe.wait_ge(mean_ready, c + 1)
                    if c >= 2:
                        pe.wait_ge(msg_ready, c - 1)
                    for k in range(2):
                        last = pe.matmul(psM[c % 2][:, 0:z - a], w3[:, k, :], T.agg[:, k, a:z], start=(k == 0), stop=(k == 1))
                    last.then_inc(msg_done, 1)
                if 1 <= c <= CUTS:
                    a, z = cuts[c - 1]
                    pe.wait_ge(msg_ready, c)
                    for m in range(2):
                        n = 2 * (c - 1) + m
                        if n >= 4:
                            pe.wait_ge(u1_ready, n - 3)
                        pe.matmul(psU[n % 4][:, 0:z - a], wa[:, 0, m * P:(m + 1) * P], T.x1T[:, a:z], start=True, stop=False)
                        pe.matmul(psU[n % 4][:, 0:z - a], wa[:, 1, m * P:(m + 1) * P], msg[:, a:z], start=False, stop=True).then_inc(u1_done, 1)
                if c >= 2:
                    a, z = cuts[c - 2]
                    pe.wait_ge(u1_ready, 2 * (c - 1))
                    for b in range(a // BLK, z // BLK):
                        if b >= 2:
                            pe.wait_ge(u2_read, b - 1)
                        for k in range(2):
                            last = pe.matmul(psV[b % 2][0:BLK, 0:D], u1[:, k, b * BLK:(b + 1) * BLK], wb[:, k, :], start=(k == 0), stop=(k == 1))
                        last.then_inc(u2_done, 1)

        @block.scalar
        def _(act):
            for c, (a, z) in enumerate(cuts):
                for m in range(2):
                    n = 2 * c + m
                    act.wait_ge(u1_done, n + 1)
                    act.activation(u1[:, m, a:z], psU[n % 4][:, 0:z - a], ACT.Relu, bias=ba[:, m:m + 1]).then_inc(u1_ready, 1)
            act.wait_ge(moments_ready, 1)
            act.activation(T.std[:, :], T.den[:, :], ACT.Sqrt).then_inc(std_ready, 1)

        @block.vector
        def _(dve):
            def step(ins):
                dve.wait_ge(chain.sem, chain.inc(ins))
            for c in range(CUTS + 3):
                if c < CUTS:
                    a, z = cuts[c]
                    for k in range(2):
                        last = dve.tensor_tensor(T.agg[:, k, a:z], T.agg[:, k, a:z], T.inv[:, a:z], ALU.mult)
                    last.then_inc(mean_ready, 1)
                    dve.tensor_scalar(has[:, a:z], T.inv[:, a:z], 0.0, None, ALU.is_gt).then_inc(has_ready, 1)
                if 1 <= c <= CUTS:
                    a, z = cuts[c - 1]
                    dve.wait_ge(has_ready, c)
                    dve.wait_ge(msg_done, c)
                    dve.scalar_tensor_tensor(msg[:, a:z], has[:, a:z], b3[:, 0:1], psM[(c - 1) % 2][:, 0:z - a], ALU.mult, ALU.add).then_inc(msg_ready, 1)
                if c == 3:
                    dve.wait_ge(sums_ready, 2)
                if c >= 3:
                    a, z = cuts[c - 3]
                    for b in range(a // BLK, z // BLK):
                        dve.wait_ge(u2_done, b + 1)
                        dve.tensor_tensor(T.x1[:, b, :], T.x1[:, b, :], psV[b % 2][0:BLK, 0:D], ALU.add).then_inc(u2_read, 1)
                    dve.wait_ge(u2_read, z // BLK)
                    for b in range(a // BLK, z // BLK):
                        last = dve.bn_stats(T.stats[:, b, :], T.x1[:, b, :])
            step(last)
            layernorm(dve, step, T, T.x1, moments_ready, std_ready, cuts, rows_ready)


class Tables:
    pass


def gnn_kernel(nc, x, src, dst, w0, att, wm1, bm1, wm2, bm2, wm3, bm3, wn1, bn1, wn2, bn2, out):
    def dram(name, shape, dt):
        return nc.dram_tensor(name, shape, dt, kind="Internal").ap()
    scr_tile = dram("scr_tile", (2, TILES), fp32)
    scr_dst = dram("scr_dst", (TILES * P,), i16)
    scr_win = dram("scr_win", (2 * NWIN,), i32)
    scr_pass = dram("scr_pass", (2, GROUPS), fp32)
    table_a = dram("table_a", (N, H), fp32)
    table_b = dram("table_b", (NPAD, 3 * H), bf16)
    with ExitStack() as ctx:
        def sb(name, shape, dt):
            return ctx.enter_context(nc.sbuf_tensor(name, shape, dt))
        T = Tables()
        T.edge_keys = sb("edge_keys", [P, 4, TILES + TPT - 1], fp32)
        T.src_idx = sb("src_idx", [P, TILES], i32)
        T.iota_n = sb("iota_n", [P, SW + 1], i16)
        T.win_tab = sb("win_tab", [1, 2 * NWIN], i32)
        T.base_row = sb("base_row", [1, GROUPS], fp32)
        T.base_i = sb("base_i", [1, GROUPS], i32)
        T.base_all = sb("base_all", [P, GROUPS], fp32)
        T.neg_base = sb("neg_base", [P, GROUPS], fp32)
        T.passes_f = sb("passes_f", [1, 1], fp32)
        T.passes_i = sb("passes_i", [1, 1], i32)
        T.edges_of = sb("edges_of", [P, NWIN], fp32)
        T.ident = sb("ident", [P, P], fp32)
        T.x1 = sb("x1", [BLK, NBLK, D], fp32)
        T.den = sb("den", [BLK, NBLK], fp32)
        T.std = sb("std", [BLK, NBLK], fp32)
        T.stats = sb("stats", [BLK, NBLK, 6], fp32)
        T.mv = sb("mv", [BLK, NBLK, 2], fp32)
        with ExitStack() as early:
            def sb_early(name, shape, dt):
                return early.enter_context(nc.sbuf_tensor(name, shape, dt))
            T.iota_m = sb_early("iota_m", [P, NWIN * WM + 1], i16)
            T.row_keys = sb_early("row_keys", [P, TILES + TPT - 1], i16)
            T.hx = sb_early("hx", [BLK, NBLK + 1, D + 2], fp32)
            T.s1r = sb_early("s1r", [P, N], fp32)
            T.s2s = sb_early("s2s", [BLK, NBLK], fp32)
            index_tables(nc, src, dst, x, w0, att, T, scr_tile, scr_dst, scr_win, scr_pass)
            attention(nc, T)
        T.x1T = sb("x1T", [D, N], fp32)
        T.agg = sb("agg", [P, 2, NPAD], fp32)
        T.w3 = sb("w3_u", [P, 2, D], fp32)
        T.b3 = sb("b3_u", [D, 1], fp32)
        T.wa = sb("wa_u", [P, 2, H], fp32)
        T.ba = sb("ba_u", [P, 2], fp32)
        T.wb = sb("wb_u", [P, 2, D], fp32)
        T.bb = sb("bb_u", [P, D], fp32)
        T.inv = sb("inv", [P, N], fp32)
        node_tables(nc, T, wm1, bm1, table_a, table_b)
        messages(nc, T, wm2, bm2, table_a, table_b, scr_dst, bm3, wm3, bn1, wn1, wn2, bn2)
        update_nodes(nc, T, out)


_INS = ["x", "src", "dst", "L0_gnn_kernel", "L0_gnn_kernel_attention", "L1_gnn_Wm1", "L1_gnn_bm1", "L1_gnn_Wm2",
        "L1_gnn_bm2", "L1_gnn_Wm3", "L1_gnn_bm3", "L1_gnn_Wn1", "L1_gnn_bn1", "L1_gnn_Wn2", "L1_gnn_bn2"]


def kernel(**inputs):
    import numpy as np
    import concourse.bacc as bacc
    from concourse import mybir as mb
    from concourse.bass_utils import run_bass_kernel_spmd as run

    nc = bacc.Bacc("TRN2", target_bir_lowering=False, num_devices=1)
    arrays, args = {}, []
    for name in _INS:
        a = np.ascontiguousarray(inputs[name])
        arrays[f"in_{name}"] = a
        args.append(nc.dram_tensor(f"in_{name}", a.shape, mb.dt.from_np(a.dtype), kind="ExternalInput").ap())
    out = nc.dram_tensor("out_0", (N, D), mb.dt.float32, kind="ExternalOutput").ap()
    gnn_kernel(nc, *args, out)
    return run(nc, [arrays], core_ids=[0]).results[0]["out_0"]
```
